# Optimizing a Trainium2 kernel written in Bass

```python
import numpy as np
import jax
import jax.numpy as jnp

def _softmax(x, axis=-1):
    return jax.nn.softmax(x, axis=axis)

def _gelu(x):
    return jax.nn.gelu(x, approximate=True)

def _silu(x):
    return jax.nn.silu(x)

def _sigmoid(x):
    return jax.nn.sigmoid(x)

def _layernorm(x, axis=-1, eps=1e-05):
    m = jnp.mean(x, axis=axis, keepdims=True)
    v = jnp.var(x, axis=axis, keepdims=True)
    return (x - m) / jnp.sqrt(v + eps)

def _scatter_add(tgt, idx, src, axis=0):
    return tgt.at[idx].add(src)

def _segment_sum(src, seg, n):
    return jax.ops.segment_sum(src, seg, n)
kernel_name = 'mk_metaformer_d2_conv_nhwc256_r4_c0e1d2'

def setup_inputs(seed: int=0):
    np.random.seed(seed)
    _w = jnp.asarray

    def _rec_inputs():
        import jax
        import jax.numpy as jnp
        _gk = jax.random.key(seed)
        x = -0.000125 + 0.9999 * jax.random.normal(jax.random.fold_in(_gk, 1), (32, 16, 16, 64), jnp.float32)
        return x
    x = _rec_inputs()

    def _L0_conv_setup():
        import jax, jax.numpy as jnp
        import numpy as np
        B, H, W, C = (32, 16, 16, 64)
        CROP = 48
        ITER_N = 5

        def _conv2d_same(y, w, b):
            out = jax.lax.conv_general_dilated(y, w, window_strides=(1, 1), padding='SAME', dimension_numbers=('NHWC', 'HWIO', 'NHWC'))
            return out + b
        key = jax.random.key(seed)
        k0, k1, k2 = jax.random.split(key, 3)
        x = jax.random.normal(k0, (B, H, W, C), dtype=jnp.float32)
        w1 = jax.random.normal(k1, (3, 3, C, C), dtype=jnp.float32) * 0.02
        b1 = jnp.zeros((C,), dtype=jnp.float32)
        w2 = jax.random.normal(k2, (3, 3, C, C), dtype=jnp.float32) * 0.02
        b2 = jnp.zeros((C,), dtype=jnp.float32)
        return {'x': x, 'w1': w1, 'b1': b1, 'w2': w2, 'b2': b2}
    _L0_conv_all = _L0_conv_setup()
    _L0_conv_in = {k: v for k, v in _L0_conv_all.items() if k in ('w1', 'b1', 'w2', 'b2')}
    del _L0_conv_all

    def _L0_ffn_setup():
        import jax, jax.numpy as jnp
        import numpy as np
        NUM_EXPERTS = 8
        TOP_K = 2
        B, S, D = (8, 2048, 64)

        def _moe(tokens, router_w, w1, b1, w2, b2):
            N = tokens.shape[0]
            E = router_w.shape[0]
            logits = tokens.astype(jnp.float32) @ router_w.astype(jnp.float32).T
            probs = jax.nn.softmax(logits, axis=-1)
            rw, re = jax.lax.top_k(probs, TOP_K)
            if TOP_K > 1:
                rw = rw / jnp.maximum(rw.sum(-1, keepdims=True), 1e-12)
            rw = rw.astype(tokens.dtype)
            combine = jnp.zeros((N, E), tokens.dtype).at[jnp.arange(N)[:, None], re].set(rw)
            out = tokens
            for e in range(E):
                h = jax.nn.gelu(tokens @ w1[e] + b1[e], approximate=False)
                y = h @ w2[e] + b2[e]
                out = out + combine[:, e:e + 1] * y
            return out
        key = jax.random.key(seed)
        ks = jax.random.split(key, 4)
        scale = 1.0 / np.sqrt(D).astype(np.float32)
        return {'input_embeddings': jax.random.normal(ks[0], (B, S, D), jnp.float32), 'router_w': jax.random.normal(ks[1], (NUM_EXPERTS, D), jnp.float32) * scale, 'w1': jax.random.normal(ks[2], (NUM_EXPERTS, D, D), jnp.float32) * scale, 'b1': jnp.zeros((NUM_EXPERTS, D), jnp.float32), 'w2': jax.random.normal(ks[3], (NUM_EXPERTS, D, D), jnp.float32) * scale, 'b2': jnp.zeros((NUM_EXPERTS, D), jnp.float32)}
    _L0_ffn_all = _L0_ffn_setup()
    _L0_ffn_in = {k: v for k, v in _L0_ffn_all.items() if k in ('router_w', 'w1', 'b1', 'w2', 'b2')}
    del _L0_ffn_all

    def _L1_conv_setup():
        import jax, jax.numpy as jnp
        import numpy as np
        B, H, W, C = (16, 16, 16, 64)
        DIRECTIONS = [(0, -1), (1, -1), (1, 0), (1, 1), (0, 1), (-1, 1), (-1, 0), (-1, -1)]

        def _shift(g, dx, dy):
            _, h, w, _ = g.shape
            padded = jnp.pad(g, ((0, 0), (max(0, dy), max(0, -dy)), (max(0, dx), max(0, -dx)), (0, 0)))
            return padded[:, max(0, -dy):max(0, -dy) + h, max(0, -dx):max(0, -dx) + w, :]
        key = jax.random.key(seed)
        k1, k2, k3, k4 = jax.random.split(key, 4)
        grid_embedding = jax.random.normal(k1, (B, H, W, C), dtype=jnp.float32)
        Wd = jax.random.normal(k2, (8, C, C), dtype=jnp.float32) * 0.01
        Wc = jax.random.normal(k3, (C, 8 * C), dtype=jnp.float32) * 0.02
        bc = jax.random.normal(k4, (C,), dtype=jnp.float32) * 0.02
        return {'grid_embedding': grid_embedding, 'Wd': Wd, 'Wc': Wc, 'bc': bc}
    _L1_conv_all = _L1_conv_setup()
    _L1_conv_in = {k: v for k, v in _L1_conv_all.items() if k in ('Wd', 'Wc', 'bc')}
    del _L1_conv_all

    def _L1_ffn_setup():
        import jax, jax.numpy as jnp
        import numpy as np
        BN_EPS = 0.001

        def _bn(h, g, b, m, v):
            return g * (h - m) * jax.lax.rsqrt(v + BN_EPS) + b
        key = jax.random.key(seed)
        ks = jax.random.split(key, 8)
        B, F, Df = (64, 16, 64)
        E, H, D = (8, 64, 64)
        s1 = 1.0 / np.sqrt(Df)
        s2 = 1.0 / np.sqrt(H)
        return {'x': jax.random.normal(ks[0], (B, F, Df), jnp.float32), 'Wr': jax.random.normal(ks[1], (Df, E), jnp.float32) * s1, 'br': jnp.zeros((E,), jnp.float32), 'W1': jax.random.normal(ks[2], (E, Df, H), jnp.float32) * s1, 'b1': jnp.zeros((E, H), jnp.float32), 'g1': jnp.ones((E, H), jnp.float32), 'be1': jnp.zeros((E, H), jnp.float32), 'm1': jnp.zeros((E, H), jnp.float32), 'v1': jnp.ones((E, H), jnp.float32), 'W2': jax.random.normal(ks[3], (E, H, H), jnp.float32) * s2, 'b2': jnp.zeros((E, H), jnp.float32), 'g2': jnp.ones((E, H), jnp.float32), 'be2': jnp.zeros((E, H), jnp.float32), 'm2': jnp.zeros((E, H), jnp.float32), 'v2': jnp.ones((E, H), jnp.float32), 'Wo': jax.random.normal(ks[4], (E, H, D), jnp.float32) * s2, 'bo': jnp.zeros((E, D), jnp.float32)}
    _L1_ffn_all = _L1_ffn_setup()
    _L1_ffn_in = {k: v for k, v in _L1_ffn_all.items() if k in ('Wr', 'br', 'W1', 'b1', 'g1', 'be1', 'm1', 'v1', 'W2', 'b2', 'g2', 'be2', 'm2', 'v2', 'Wo', 'bo')}
    del _L1_ffn_all
    return {'x': x, 'L0_conv_w1': _L0_conv_in['w1'], 'L0_conv_b1': _L0_conv_in['b1'], 'L0_conv_w2': _L0_conv_in['w2'], 'L0_conv_b2': _L0_conv_in['b2'], 'L0_ffn_router_w': _L0_ffn_in['router_w'], 'L0_ffn_w1': _L0_ffn_in['w1'], 'L0_ffn_b1': _L0_ffn_in['b1'], 'L0_ffn_w2': _L0_ffn_in['w2'], 'L0_ffn_b2': _L0_ffn_in['b2'], 'L1_conv_Wd': _L1_conv_in['Wd'], 'L1_conv_Wc': _L1_conv_in['Wc'], 'L1_conv_bc': _L1_conv_in['bc'], 'L1_ffn_Wr': _L1_ffn_in['Wr'], 'L1_ffn_br': _L1_ffn_in['br'], 'L1_ffn_W1': _L1_ffn_in['W1'], 'L1_ffn_b1': _L1_ffn_in['b1'], 'L1_ffn_g1': _L1_ffn_in['g1'], 'L1_ffn_be1': _L1_ffn_in['be1'], 'L1_ffn_m1': _L1_ffn_in['m1'], 'L1_ffn_v1': _L1_ffn_in['v1'], 'L1_ffn_W2': _L1_ffn_in['W2'], 'L1_ffn_b2': _L1_ffn_in['b2'], 'L1_ffn_g2': _L1_ffn_in['g2'], 'L1_ffn_be2': _L1_ffn_in['be2'], 'L1_ffn_m2': _L1_ffn_in['m2'], 'L1_ffn_v2': _L1_ffn_in['v2'], 'L1_ffn_Wo': _L1_ffn_in['Wo'], 'L1_ffn_bo': _L1_ffn_in['bo']}

def reference(x, L0_conv_w1, L0_conv_b1, L0_conv_w2, L0_conv_b2, L0_ffn_router_w, L0_ffn_w1, L0_ffn_b1, L0_ffn_w2, L0_ffn_b2, L1_conv_Wd, L1_conv_Wc, L1_conv_bc, L1_ffn_Wr, L1_ffn_br, L1_ffn_W1, L1_ffn_b1, L1_ffn_g1, L1_ffn_be1, L1_ffn_m1, L1_ffn_v1, L1_ffn_W2, L1_ffn_b2, L1_ffn_g2, L1_ffn_be2, L1_ffn_m2, L1_ffn_v2, L1_ffn_Wo, L1_ffn_bo):
    import jax
    import jax.numpy as jnp

    def _L0_conv_ref(x, w1, b1, w2, b2):
        import jax, jax.numpy as jnp
        import numpy as np
        B, H, W, C = (32, 16, 16, 64)
        CROP = 48
        ITER_N = 5

        def _conv2d_same(y, w, b):
            out = jax.lax.conv_general_dilated(y, w, window_strides=(1, 1), padding='SAME', dimension_numbers=('NHWC', 'HWIO', 'NHWC'))
            return out + b
        b, h, w_, c = x.shape
        ch, cw = (min(CROP, h), min(CROP, w_))
        oh, ow = ((h - ch) // 2, (w_ - cw) // 2)
        x_sub = x[:, oh:oh + ch, ow:ow + cw, :]
        M = ch * cw
        xs = x_sub.reshape(b, c, M)
        Minv = jnp.float32(1.0 / M)
        I_hat = Minv * (jnp.eye(M, dtype=x.dtype) - Minv * jnp.ones((M, M), dtype=x.dtype))
        cov = jnp.einsum('bcm,mn,bdn->bcd', xs, I_hat, xs)
        I3 = 3.0 * jnp.eye(c, dtype=x.dtype)
        normA = jnp.einsum('bii->b', cov)
        A = cov / normA[:, None, None]
        ZY = 0.5 * (I3 - A)
        Y = jnp.matmul(A, ZY)
        Z = ZY
        for _ in range(1, ITER_N - 1):
            ZY = 0.5 * (I3 - jnp.matmul(Z, Y))
            Y = jnp.matmul(Y, ZY)
            Z = jnp.matmul(ZY, Z)
        ZY = 0.5 * jnp.matmul(Y, I3 - jnp.matmul(Z, Y))
        y = ZY * jnp.sqrt(normA)[:, None, None]
        y = jnp.mean(y, axis=-1).reshape(b, 1, 1, c)
        y = jax.nn.relu(_conv2d_same(y, w1, b1))
        y = jax.nn.sigmoid(_conv2d_same(y, w2, b2))
        return y * x

    def _L0_ffn_ref(input_embeddings, router_w, w1, b1, w2, b2):
        import jax, jax.numpy as jnp
        import numpy as np
        NUM_EXPERTS = 8
        TOP_K = 2
        B, S, D = (8, 2048, 64)

        def _moe(tokens, router_w, w1, b1, w2, b2):
            N = tokens.shape[0]
            E = router_w.shape[0]
            logits = tokens.astype(jnp.float32) @ router_w.astype(jnp.float32).T
            probs = jax.nn.softmax(logits, axis=-1)
            rw, re = jax.lax.top_k(probs, TOP_K)
            if TOP_K > 1:
                rw = rw / jnp.maximum(rw.sum(-1, keepdims=True), 1e-12)
            rw = rw.astype(tokens.dtype)
            combine = jnp.zeros((N, E), tokens.dtype).at[jnp.arange(N)[:, None], re].set(rw)
            out = tokens
            for e in range(E):
                h = jax.nn.gelu(tokens @ w1[e] + b1[e], approximate=False)
                y = h @ w2[e] + b2[e]
                out = out + combine[:, e:e + 1] * y
            return out
        b, s, d = input_embeddings.shape
        tokens = input_embeddings.reshape(b * s, d)
        return _moe(tokens, router_w, w1, b1, w2, b2).reshape(b, s, d)

    def _L1_conv_ref(grid_embedding, Wd, Wc, bc):
        import jax, jax.numpy as jnp
        import numpy as np
        B, H, W, C = (16, 16, 16, 64)
        DIRECTIONS = [(0, -1), (1, -1), (1, 0), (1, 1), (0, 1), (-1, 1), (-1, 0), (-1, -1)]

        def _shift(g, dx, dy):
            _, h, w, _ = g.shape
            padded = jnp.pad(g, ((0, 0), (max(0, dy), max(0, -dy)), (max(0, dx), max(0, -dx)), (0, 0)))
            return padded[:, max(0, -dy):max(0, -dy) + h, max(0, -dx):max(0, -dx) + w, :]
        shifted = jnp.stack([_shift(grid_embedding, dx, dy) for dx, dy in DIRECTIONS], axis=0)
        proc = jnp.einsum('dbhwc,dce->bhwde', shifted, Wd)
        combined = proc.reshape(grid_embedding.shape[0], grid_embedding.shape[1], grid_embedding.shape[2], -1)
        return combined @ Wc.T + bc

    def _L1_ffn_ref(x, Wr, br, W1, b1, g1, be1, m1, v1, W2, b2, g2, be2, m2, v2, Wo, bo):
        import jax, jax.numpy as jnp
        import numpy as np
        BN_EPS = 0.001

        def _bn(h, g, b, m, v):
            return g * (h - m) * jax.lax.rsqrt(v + BN_EPS) + b
        feat = jnp.mean(x, axis=0)
        w = jax.nn.softmax(feat @ Wr + br, axis=-1)
        h = jnp.einsum('bfd,edh->bfeh', x, W1) + b1
        h = jax.nn.relu(_bn(h, g1, be1, m1, v1))
        h = jnp.einsum('bfeh,ehk->bfek', h, W2) + b2
        h = jax.nn.relu(_bn(h, g2, be2, m2, v2))
        y = jnp.einsum('bfeh,ehd->bfed', h, Wo) + bo
        return jnp.einsum('bfed,fe->bfd', y, w)

    def _gn(v, G=32, eps=1e-05):
        B_, H_, W_, C_ = v.shape
        g = v.reshape(B_, H_, W_, G, C_ // G)
        m = jnp.mean(g, axis=(1, 2, 4), keepdims=True)
        s = jnp.var(g, axis=(1, 2, 4), keepdims=True)
        return ((g - m) / jnp.sqrt(s + eps)).reshape(v.shape)

    def _ln_c(v, eps=1e-06):
        m = jnp.mean(v, axis=-1, keepdims=True)
        s = jnp.var(v, axis=-1, keepdims=True)
        return (v - m) / jnp.sqrt(s + eps)

    def _ln_t(v, eps=1e-05):
        m = jnp.mean(v, axis=-1, keepdims=True)
        s = jnp.var(v, axis=-1, keepdims=True)
        return (v - m) / jnp.sqrt(s + eps)

    def _to_tokens(v):
        B_, H_, W_, C_ = v.shape
        return v.reshape(B_, H_ * W_, C_)

    def _from_tokens(t, like):
        return t.reshape(like.shape)
    x = x + _L0_conv_ref(_ln_c(x), L0_conv_w1, L0_conv_b1, L0_conv_w2, L0_conv_b2)
    t = _to_tokens(x)
    t = t + _L0_ffn_ref(_ln_t(t), L0_ffn_router_w, L0_ffn_w1, L0_ffn_b1, L0_ffn_w2, L0_ffn_b2)
    x = _from_tokens(t, x)
    x = x + _L1_conv_ref(_ln_c(x), L1_conv_Wd, L1_conv_Wc, L1_conv_bc)
    t = _to_tokens(x)
    t = t + _L1_ffn_ref(_ln_t(t), L1_ffn_Wr, L1_ffn_br, L1_ffn_W1, L1_ffn_b1, L1_ffn_g1, L1_ffn_be1, L1_ffn_m1, L1_ffn_v1, L1_ffn_W2, L1_ffn_b2, L1_ffn_g2, L1_ffn_be2, L1_ffn_m2, L1_ffn_v2, L1_ffn_Wo, L1_ffn_bo)
    x = _from_tokens(t, x)
    return x

_drawn_inputs = setup_inputs


def setup_inputs(seed=0):
    import zlib

    import numpy as np

    out = dict(_drawn_inputs(seed))
    spreads = {'L0_conv_b1': (0.0, 0.8),
     'L0_conv_b2': (0.0, 0.283),
     'L0_ffn_b1': (0.0, 0.402),
     'L0_ffn_b2': (0.0, 0.284),
     'L1_ffn_br': (0.0, 0.8),
     'L1_ffn_b1': (0.0, 0.8),
     'L1_ffn_g1': (1.0, 0.6),
     'L1_ffn_be1': (0.0, 0.8),
     'L1_ffn_m1': (0.0, 0.8),
     'L1_ffn_v1': (1.0, 0.6),
     'L1_ffn_b2': (0.0, 0.703),
     'L1_ffn_g2': (1.0, 0.6),
     'L1_ffn_be2': (0.0, 0.8),
     'L1_ffn_m2': (0.0, 0.741),
     'L1_ffn_v2': (1.0, 0.6),
     'L1_ffn_bo': (0.0, 0.511)}
    factors = {'L0_conv_w1': 189.965,
     'L0_conv_w2': 8.0,
     'L1_conv_Wd': 4.182,
     'L1_conv_Wc': 4.186,
     'L1_conv_bc': 5.817,
     'L1_ffn_Wr': 4.244}
    for name, (base, spread) in spreads.items():
        noise = np.random.default_rng([zlib.crc32(name.encode()), seed]).standard_normal(out[name].shape)
        drawn = base * np.exp(spread * noise) if base else spread * noise
        out[name] = jnp.asarray(drawn.astype(out[name].dtype))
    for name, factor in factors.items():
        out[name] = (out[name] * factor).astype(out[name].dtype)
    return out
```

```python
from contextlib import ExitStack

import concourse.bass as bass
from concourse import mybir

ALU = mybir.AluOpType
ACT = mybir.ActivationFunctionType
AX = mybir.AxisListType
F32 = mybir.dt.float32
F32R = mybir.dt.float32r

P = 128
B, H, W, C = 32, 16, 16, 64
E = 8
T = 4
NP = B // 2
KP = E // 2
CH = P * T
NB = NP // 2
T2 = 2 * T
NG = 4
GP = NP // NG
M = H * W
PADH, PADW = H + 2, W + 2
EPS_C, EPS_T, EPS_BN = 1e-6, 1e-5, 1e-3
ROUNDS = 3
DIRECTIONS = [(0, -1), (1, -1), (1, 0), (1, 1), (0, 1), (-1, 1), (-1, 0), (-1, -1)]

VECS = ["L0_ffn_b1", "L1_ffn_b1", "L1_ffn_g1", "L1_ffn_be1", "L1_ffn_m1", "L1_ffn_v1",
        "L1_ffn_b2", "L1_ffn_g2", "L1_ffn_be2", "L1_ffn_m2", "L1_ffn_v2"]
ROW = {name: KP * n for n, name in enumerate(VECS)}
ROW_GB1 = KP * len(VECS)
ROW_GB2 = ROW_GB1 + 1
ROW_BC = ROW_GB1 + 2
ROW_ROUTER = ROW_GB1 + 4
NROWS = ROW_ROUTER + E


def wait(eng, sem, value):
    if isinstance(value, int) and value <= 0:
        return
    eng.wait_ge(sem, value)


def rep(ap, axis, n):
    shape = list(ap.shape)
    shape[axis] = n
    return ap.broadcast_to(shape)


def metaformer_kernel(nc, a, out):
    ctx = ExitStack()
    with ctx:
        def sb(name, shape, dt=F32):
            return ctx.enter_context(nc.sbuf_tensor(name, shape, dt))

        sems = {}

        def sem(name):
            sems[name] = ctx.enter_context(nc.semaphore(name))
            return sems[name]

        bank = [ctx.enter_context(nc.psum_tensor(f"bank{i}", [P, 512], F32)) for i in range(8)]

        x = sb("x", [P, NP, T * C])
        xn = sb("xn", [P, NP, T * C])
        gate = sb("gate", [P, NP, C])
        xs_ffn = sb("xs_ffn", [P, NB, T2 * P], F32R)

        ident = sb("ident", [P, P])
        ident15 = sb("ident15", [P, P])
        same_img = sb("same_img", [P, P])
        two_ident = sb("two_ident", [P, C])
        half_mean = sb("half_mean", [P, P])
        sel_f = sb("sel_f", [P, KP, P])
        sel = sb("sel", [P, KP, P], F32R)
        rank = sb("rank", [P, E])
        neg_half = sb("neg_half", [P, 16])
        pos_half = sb("pos_half", [P, 16])

        vec_rows = sb("vec_rows", [NROWS, P])
        cols = sb("cols", [P, NROWS])
        gw1 = sb("gw1", [P, P])
        gw2 = sb("gw2", [P, P])
        half_gb2 = sb("half_gb2", [P, 1])
        w1f = sb("w1f", [P, E * C])
        w1s = sb("w1s", [P, 2, E * C], F32R)
        w2 = sb("w2", [P, KP, C])
        b2rows = sb("b2rows", [P, C])
        router = sb("router", [P, 2, E], F32R)
        wd = sb("wd", [P, 4, C])
        wc = sb("wc", [C, 8, C])
        wdT = sb("wdT", [C, 8, 2, C])
        wcT = sb("wcT", [C, 8, C])
        vconv = sb("vconv", [P, 8, 2, C], F32R)
        f1f = sb("f1f", [P, E * C])
        f1s = sb("f1s", [P, 2, E * C], F32R)
        f2 = sb("f2", [P, KP, P])
        fo = sb("fo", [P, KP, C])
        bo = sb("bo", [E, C])
        wr = sb("wr", [C, E])
        br = sb("br", [P, E])
        bn1 = sb("bn1", [P, 2, KP])
        bn2 = sb("bn2", [P, 3, KP])
        bn_t = sb("bn_t", [P, 4, KP])

        stats = sb("stats", [P, 16, 6])
        mv = sb("mv", [P, 16, 2])
        veps = sb("veps", [P, 16])
        rstd = sb("rstd", [P, 16])
        rsum = sb("rsum", [P, GP])
        rmean = sb("rmean", [P, GP])
        xcc = sb("xcc", [P, GP, M])
        sqj = sb("sqj", [P, M])
        sumsq = sb("sumsq", [P, NP])
        xT = sb("xT", [P, 2, GP * P])
        rtrace = sb("rtrace", [P, NP])
        trm = sb("trm", [P, NP])
        root = sb("root", [P, NP])
        Am = sb("Am", [P, NP, P])
        Ym = sb("Ym", [P, NP, P])
        Zm = sb("Zm", [P, NP, P])
        Tm = sb("Tm", [P, NP, P])
        A15 = Tm
        u_sum = sb("u_sum", [P, NP])
        zu = sb("zu", [P, NP])
        ycol = sb("ycol", [P, 3, NP])
        g1 = sb("g1", [P, NP])
        g2 = sb("g2", [P, 2, NP])
        gspread = sb("gspread", [P, NP, C])

        xc = sb("xc", [P, T2, C])
        xnb = sb("xnb", [P, 2, T2, C])
        hl = sb("hl", [P, T2, 2, C], F32R)
        xs = sb("xs", [P, 2, T2 * P], F32R)
        cs = sb("cs", [P, T2 * P], F32R)
        act = sb("act", [P, 2, CH])
        scaled = sb("scaled", [P, 2, CH])
        yTs = sb("yTs", [P, 2, 2 * P])
        lg = sb("lg", [P, T2, E])
        tmp = sb("tmp", [P, T2, E])
        one1 = sb("one1", [P, T2, E])
        one2 = sb("one2", [P, T2, E])
        m12 = sb("m12", [P, 8, T2])
        cw = sb("cw", [P, T2, E])
        chl = sb("chl", [P, T2, P // E, E], F32R)
        xp = sb("xp", [P, 4, PADH, PADW], F32R)
        cvs = sb("cvs", [P, 2, CH])
        fsum = sb("fsum", [P, T2, C])
        feat = Tm[:, 8:10, :].rearrange("p i (u c) -> p (i u) c", u=2)
        featT = Tm[0:C, 0:4, :].rearrange("p i n -> p (i n)")
        fl = sb("fl", [P, 4, T, E])
        fm = sb("fm", [P, 4, T])
        wtT = Tm[0:E, 4:8, :].rearrange("p i n -> p (i n)")
        wrep = Zm[:, :, :].rearrange("p (t e) (u c) -> p t (e u) c", t=T, u=2)
        wspread = Am[:, :, :].rearrange("p (k i) n -> p k (i n)", k=KP)
        b2sel = sb("b2sel", [P, KP, E])
        u8 = sb("u8", [E, C])
        ctab = sb("ctab", [P, T * C])

        S = sem
        x_in = [S(f"x_in{g}") for g in range(NG)]
        w_gate, w_moe, w_conv, w_ffn, w_vec = S("w_gate"), S("w_moe"), S("w_conv"), S("w_ffn"), S("w_vec")
        consts, consts_v, zeroed = S("consts"), S("consts_v"), S("zeroed")
        vecs_ready, cols_ready = S("vecs_ready"), S("cols_ready")
        w_split = S("w_split")
        bn_step, bn_pow, s2_spread = S("bn_step"), S("bn_pow"), S("s2_spread")
        conv_wT, conv_wTs, conv_v, conv_vs = S("conv_wT"), S("conv_wTs"), S("conv_v"), S("conv_vs")
        a_stats, a_mv, a_veps, a_rstd, a_xc, a_xn = (S(n) for n in ("a_stats", "a_mv", "a_veps", "a_rstd", "a_xc", "a_xn"))
        a_rsum, a_rmean, a_xcc, a_sq, a_xT, a_xTs, a_gram = (S(n) for n in ("a_rsum", "a_rmean", "a_xcc", "a_sq", "a_xT", "a_xTs", "a_gram"))
        a_trace, a_rtr, a_trm, a_root, a_A, a_A15, a_Z0, a_P0, a_Y0 = (S(n) for n in ("a_trace", "a_rtr", "a_trm", "a_root", "a_A", "a_A15", "a_Z0", "a_P0", "a_Y0"))
        n_P, n_T, n_YZ, n_Y, n_Z = (S(n) for n in ("n_P", "n_T", "n_YZ", "n_Y", "n_Z"))
        a_u, a_zu, a_zus, a_w, a_y = (S(n) for n in ("a_u", "a_zu", "a_zus", "a_w", "a_y"))
        g_c1, g_r1, g_c2, g_s, g_sp, g_G, g_done = (S(n) for n in ("g_c1", "g_r1", "g_c2", "g_s", "g_sp", "g_G", "g_done"))
        m_gx, m_x1, m_st, m_mv, m_ve, m_rs, m_xc, m_xn, m_hi, m_lo, m_xr = (S("m_" + n) for n in ("gx", "x1", "st", "mv", "ve", "rs", "xc", "xn", "hi", "lo", "xr"))
        m_X, m_xs, m_L, m_route, m_C, m_cs, m_cb, m_z, m_act, m_sc, m_l2, m_y, m_yT, m_yo, m_res = (
            S("m_" + n) for n in ("X", "xs", "L", "route", "C", "cs", "cb", "z", "act", "sc", "l2", "y", "yT", "yo", "res"))
        c_st, c_mv, c_ve, c_rs, c_xc, c_xn, c_hi, c_lo, c_X, c_xp, c_cv, c_cvs, c_bk, c_r1, c_r2 = (
            S("c_" + n) for n in ("st", "mv", "ve", "rs", "xc", "xn", "hi", "lo", "X", "xp", "cv", "cvs", "bk", "r1", "r2"))
        d_st, d_mv, d_ve, d_rs, d_xc, d_xn, d_hi, d_lo, d_X, d_xs, d_acc = (
            S("d_" + n) for n in ("st", "mv", "ve", "rs", "xc", "xn", "hi", "lo", "X", "xs", "acc"))
        r_pe, r_dve, r_act, r_add = S("r_pe"), S("r_dve"), S("r_act"), S("r_add")
        f_z1, f_h1, f_z2, f_h2, f_l3, f_y, f_yT, f_yo, f_res = (S("f_" + n) for n in ("z1", "h1", "z2", "h2", "l3", "y", "yT", "yo", "res"))
        stored = S("stored")
        a_sqj, m_tanh, m_chl = S("a_sqj"), S("m_tanh"), S("m_chl")

        x_dram = a["x"].rearrange("b h w c -> (b h w c)").rearrange("(i p n) -> p i n", p=P, n=T * C)
        o_dram = out.rearrange("b h w c -> (b h w c)").rearrange("(i p n) -> p i n", p=P, n=T * C)

        def blk(t, b):
            return t[:, bass.ds(2 * b, 2), :].rearrange("p i (t c) -> p (i t) c", c=C)

        block = ctx.enter_context(nc.Block())

        @block.sync
        def _(sp):
            for g in range(NG):
                sp.dma_start(x[:, GP * g:GP * (g + 1), :], x_dram[:, GP * g:GP * (g + 1), :]).then_inc(x_in[g], 16)
            sp.wait_ge(zeroed, 7)
            for half in range(2):
                s = slice(C * half, C * (half + 1))
                sp.dma_start(gw1[s, s], a["L0_conv_w1"][1, 1]).then_inc(w_gate, 16)
                sp.dma_start(gw2[s, s], a["L0_conv_w2"][1, 1]).then_inc(w_gate, 16)
            for name in VECS:
                sp.dma_start(vec_rows[ROW[name]:ROW[name] + KP, :],
                             a[name].rearrange("(k two) h -> k (two h)", two=2)).then_inc(w_vec, 16)
            for half in range(2):
                s = slice(C * half, C * (half + 1))
                sp.dma_start(vec_rows[ROW_GB1:ROW_GB1 + 1, s], a["L0_conv_b1"].rearrange("(a c) -> a c", a=1)).then_inc(w_vec, 16)
                sp.dma_start(vec_rows[ROW_GB2:ROW_GB2 + 1, s], a["L0_conv_b2"].rearrange("(a c) -> a c", a=1)).then_inc(w_vec, 16)
                sp.dma_start(vec_rows[ROW_ROUTER:NROWS, s], a["L0_ffn_router_w"]).then_inc(w_vec, 16)
            sp.dma_start(vec_rows[ROW_BC:ROW_BC + 1, 0:C], a["L1_conv_bc"].rearrange("(a c) -> a c", a=1)).then_inc(w_vec, 16)
            for half in range(2):
                s = slice(C * half, C * (half + 1))
                sp.dma_start(w1f[s, :].rearrange("p (e h) -> p e h", e=E), a["L0_ffn_w1"].rearrange("e c h -> c e h")).then_inc(w_moe, 16)
                sp.dma_start(b2rows[E * half:E * (half + 1), :], a["L0_ffn_b2"]).then_inc(w_moe, 16)
                sp.dma_start(w2[s, :, :], a["L0_ffn_w2"].rearrange("(k two) h c -> two h k c", two=2)[half]).then_inc(w_moe, 16)
                sp.dma_start(wd[s, :, :], a["L1_conv_Wd"].rearrange("(k two) c e -> two c k e", two=2)[half]).then_inc(w_conv, 16)
            sp.dma_start(wc[:, :, :], a["L1_conv_Wc"].rearrange("o (d e) -> o d e", d=8)).then_inc(w_conv, 16)
            for half in range(2):
                s = slice(C * half, C * (half + 1))
                sp.dma_start(f1f[s, :].rearrange("p (e h) -> p e h", e=E), a["L1_ffn_W1"].rearrange("e c h -> c e h")).then_inc(w_ffn, 16)
                sp.dma_start(f2[s, :, s], a["L1_ffn_W2"].rearrange("(k two) h o -> two h k o", two=2)[half]).then_inc(w_ffn, 16)
                sp.dma_start(fo[s, :, :], a["L1_ffn_Wo"].rearrange("(k two) h c -> two h k c", two=2)[half]).then_inc(w_ffn, 16)
            sp.dma_start(bo[:, :], a["L1_ffn_bo"]).then_inc(w_ffn, 16)
            sp.dma_start(wr[:, :], a["L1_ffn_Wr"]).then_inc(w_ffn, 16)
            sp.dma_start(br[:, :], rep(a["L1_ffn_br"].rearrange("(a e) -> a e", a=1), 0, P)).then_inc(w_ffn, 16)
            for b in range(NB):
                for q in range(2):
                    sp.wait_ge(f_res, 2 * b + q + 1)
                    sp.dma_start(o_dram[:, 2 * b + q:2 * b + q + 1, :], x[:, 2 * b + q:2 * b + q + 1, :]).then_inc(stored, 16)
            sp.wait_ge(stored, 16 * NP)
        R_FEAT, R_FEATT, R_LOG, R_MAX, R_SUB, R_SUM, R_REC, R_W, R_WREP, R_WT, R_U8, R_CTAB, R_WS = range(1, 14)

        W_GATE, W_VEC, W_MOE, W_CONV, W_FFN = 64, 16 * (len(VECS) + 7), 96, 48, 16 * 9

        @block.gpsimd
        def _(pool):
            g = nc.gpsimd
            g.memset(neg_half[:, :], -0.5).then_inc(consts, 1)
            g.memset(pos_half[:, :], 0.5).then_inc(consts, 1)
            g.memset(vec_rows[:, :], 0.0).then_inc(zeroed, 1)
            g.memset(gw1[:, :], 0.0).then_inc(zeroed, 1)
            g.memset(gw2[:, :], 0.0).then_inc(zeroed, 1)
            g.memset(b2rows[:, :], 0.0).then_inc(zeroed, 1)
            g.memset(f2[:, :, :], 0.0).then_inc(zeroed, 1)
            g.memset(fsum[:, :, :], 0.0).then_inc(zeroed, 1)
            g.memset(b2sel[:, :, :], 0.0).then_inc(zeroed, 1)
            g.memset(ident[:, :], 0.0).then_inc(consts, 1)
            g.memset(ident15[:, :], 0.0).then_inc(consts, 1)
            g.memset(two_ident[:, :], 0.0).then_inc(consts, 1)
            g.memset(half_mean[:, :], 0.0).then_inc(consts, 1)
            g.memset(sel_f[:, :, :], 0.0).then_inc(consts, 1)
            g.memset(same_img[:, :], 0.0).then_inc(consts, 1)
            for e in range(E):
                g.memset(rank[:, e:e + 1], float(E - e)).then_inc(consts, 1)
            pool.wait_ge(consts, 16)
            g.memset(same_img[0:C, 0:C], 1.0).then_inc(consts, 1)
            pool.wait_ge(consts, 17)
            g.memset(same_img[C:P, C:P], 1.0).then_inc(consts, 1)
            pool.wait_ge(consts, 18)

            def fill(tile, value, base, pattern):
                return g.affine_select(out=tile, in_=tile, compare_op=ALU.not_equal, fill=value, base=base,
                                       pattern=pattern, channel_multiplier=1)
            fill(ident[:, :], 1.0, 0, [[-1, P]]).then_inc(consts, 1)
            fill(ident15[:, :], 1.5, 0, [[-1, P]]).then_inc(consts, 1)
            n = 20
            for tile, value, step in ((two_ident, 1.0, (0, -C)), (half_mean, 1.0 / B, (0, -C, C))):
                for base in step:
                    pool.wait_ge(consts, n)
                    fill(tile[:, :], value, base, [[-1, tile.shape[1]]]).then_inc(consts, 1)
                    n += 1
            for base in (0, -E):
                pool.wait_ge(consts, n)
                fill(sel_f[:, :, :].rearrange("p k (u h) -> p k u h", u=2), 1.0, base, [[-2, KP], [-1, 2], [0, C]]).then_inc(consts, 1)
                n += 1

            pool.wait_ge(zeroed, 7)
            for gr in range(NG):
                pool.wait_ge(a_mv, gr + 1)
                g.tensor_scalar(veps[:, :], mv[:, :, 1], EPS_C, None, ALU.add).then_inc(a_veps, 1)
                pool.wait_ge(a_veps, gr + 1)
                wait(pool, a_xn, gr)
                g.tensor_tensor(rstd[:, :], veps[:, :], neg_half[:, :], ALU.pow).then_inc(a_rstd, 1)
            pool.wait_ge(a_trm, 1)
            g.tensor_tensor(root[:, :], trm[:, :], pos_half[:, :], ALU.pow).then_inc(a_root, 1)

            for i in range(2):
                pool.wait_ge(bn_step, i + 1)
                g.tensor_tensor(bn_t[:, 2 * i + 1, :], bn_t[:, 2 * i, :], neg_half[:, 0:KP], ALU.pow).then_inc(bn_pow, 1)

            pool.wait_ge(g_done, 2)

            def norm_rstd(b, eps, s_mv, s_ve, s_rs, s_used):
                pool.wait_ge(s_mv, b + 1)
                g.tensor_scalar(veps[:, 0:T2], mv[:, 0:T2, 1], eps, None, ALU.add).then_inc(s_ve, 1)
                pool.wait_ge(s_ve, b + 1)
                wait(pool, s_used, b)
                g.tensor_tensor(rstd[:, 0:T2], veps[:, 0:T2], neg_half[:, 0:T2], ALU.pow).then_inc(s_rs, 1)

            for b in range(NB):
                u = b % 2
                gx = blk(xn, b)
                gb = rep(gate[:, 2 * b:2 * b + 2, :].rearrange("p i (o c) -> p i o c", o=1), 2, T)
                g.tensor_tensor(gx.rearrange("p (i t) c -> p i t c", t=T), gx.rearrange("p (i t) c -> p i t c", t=T), gb,
                                ALU.mult).then_inc(m_gx, 1)
                pool.wait_ge(m_gx, b + 1)
                g.tensor_tensor(blk(x, b), blk(x, b), gx, ALU.add).then_inc(m_x1, 1)
                norm_rstd(b, EPS_T, m_mv, m_ve, m_rs, m_xn)
                pool.wait_ge(m_hi, b + 1)
                g.tensor_tensor(hl[:, :, 1, :], xnb[:, u], hl[:, :, 0, :].bitcast(F32), ALU.subtract).then_inc(m_lo, 1)
                g.tensor_tensor(blk(x, b), blk(x, b), xnb[:, u], ALU.add).then_inc(m_xr, 1)

            for b in range(NB):
                norm_rstd(b, EPS_C, c_mv, c_ve, c_rs, c_xn)
                pool.wait_ge(c_hi, b + 1)
                g.tensor_tensor(hl[:, :, 1, :], xnb[:, 0], hl[:, :, 0, :].bitcast(F32), ALU.subtract).then_inc(c_lo, 1)
                norm_rstd(b, EPS_T, d_mv, d_ve, d_rs, d_xn)
                pool.wait_ge(d_hi, b + 1)
                g.tensor_tensor(hl[:, :, 1, :], xnb[:, 1], hl[:, :, 0, :].bitcast(F32), ALU.subtract).then_inc(d_lo, 1)
                wait(pool, d_acc, b)
                g.tensor_tensor(fsum[:, :, :], fsum[:, :, :], xnb[:, 1], ALU.add).then_inc(d_acc, 1)

            pool.wait_ge(r_dve, R_CTAB)
            for b in range(NB):
                ct = rep(ctab[:, :].rearrange("p (o n) -> p o n", o=1), 1, 2)
                g.tensor_tensor(x[:, 2 * b:2 * b + 2, :], x[:, 2 * b:2 * b + 2, :], ct, ALU.add).then_inc(r_add, 1)

        @block.vector
        def _(dve):
            v = nc.vector

            def split(hi, lo, src):
                v.tensor_copy(hi, src).then_inc(w_split, 1)
                split.n += 1
                dve.wait_ge(w_split, split.n)
                v.tensor_tensor(lo, src, hi.bitcast(F32), ALU.subtract).then_inc(w_split, 1)
                split.n += 1
            split.n = 0

            def token_stats(b, src, n, s_st, s_mv, free=None):
                for t in range(n):
                    last = v.bn_stats(stats[:, t, :], src(t))
                last.then_inc(s_st, 1)
                dve.wait_ge(s_st, b + 1)
                for t in range(n):
                    last = v.bn_aggr(mv[:, t, :], stats[:, t, :])
                last.then_inc(s_mv, 1)

            def over(col, n, c=C):
                return rep(col.rearrange("p (n o) -> p n o", o=1), 2, c)

            for gr in range(NG):
                dve.wait_ge(x_in[gr], 16)
                xg = x[:, GP * gr:GP * (gr + 1), :].rearrange("p i (t c) -> p (i t) c", c=C)
                ng = xn[:, GP * gr:GP * (gr + 1), :].rearrange("p i (t c) -> p (i t) c", c=C)
                wait(dve, a_veps, gr)
                token_stats(gr, lambda t: xg[:, t, :], 16, a_stats, a_mv)
                dve.wait_ge(a_mv, gr + 1)
                v.tensor_tensor(ng, xg, over(mv[:, :, 0], 16), ALU.subtract).then_inc(a_xc, 1)
                dve.wait_ge(a_xc, gr + 1)
                dve.wait_ge(a_rstd, gr + 1)
                v.tensor_tensor(ng, ng, over(rstd[:, :], 16), ALU.mult).then_inc(a_xn, 1)
                dve.wait_ge(a_xn, gr + 1)
                v.tensor_reduce(rsum[:, :], xn[:, GP * gr:GP * (gr + 1), :], AX.X, ALU.add).then_inc(a_rsum, 1)
                dve.wait_ge(a_rsum, gr + 1)
                v.tensor_scalar(rmean[:, :], rsum[:, :], 1.0 / M, None, ALU.mult).then_inc(a_rmean, 1)
                dve.wait_ge(a_rmean, gr + 1)
                wait(dve, a_xT, 2 * gr)
                wait(dve, a_sqj, GP * gr)
                v.tensor_tensor(xcc[:, :, :], xn[:, GP * gr:GP * (gr + 1), :], over(rmean[:, :], GP, M),
                                ALU.subtract).then_inc(a_xcc, 1)
                dve.wait_ge(a_trace, gr + 1)
                gs = slice(GP * gr, GP * (gr + 1))
                v.reciprocal(rtrace[:, gs], bank[6][:, gs]).then_inc(a_rtr, 1)
                v.tensor_scalar(trm[:, gs], bank[6][:, gs], 1.0 / M, None, ALU.mult).then_inc(a_trm if gr == NG - 1 else a_rtr, 1)
                dve.wait_ge(a_rtr, 2 * gr + 1)
                dve.wait_ge(a_gram, gr + 1)
                for i in range(GP):
                    last = v.scalar_tensor_tensor(out=Am[:, GP * gr + i, :], in0=bank[gr % 2][:, P * i:P * (i + 1)],
                                                  scalar=rtrace[:, GP * gr + i:GP * gr + i + 1], in1=same_img[:, :],
                                                  op0=ALU.mult, op1=ALU.mult)
                last.then_inc(a_A, 1)
                dve.wait_ge(a_A, gr + 1)
                i15 = rep(ident15[:, :].rearrange("p (o n) -> p o n", o=1), 1, GP)
                v.tensor_scalar(A15[:, gs, :], Am[:, gs, :], 1.5, None, ALU.mult).then_inc(a_A15, 1)
                v.scalar_tensor_tensor(out=Zm[:, gs, :], in0=Am[:, gs, :], scalar=-0.5, in1=i15,
                                       op0=ALU.mult, op1=ALU.add).then_inc(a_Z0, 1)
            flat = lambda t, gr: t[:, GP * gr:GP * (gr + 1), :].rearrange("p i n -> p (i n)")
            for gr in range(NG):
                dve.wait_ge(a_P0, gr + 1)
                dve.wait_ge(a_A15, gr + 1)
                v.scalar_tensor_tensor(out=flat(Ym, gr), in0=bank[2 + gr % 2][:, :], scalar=-0.5, in1=flat(A15, gr),
                                       op0=ALU.mult, op1=ALU.add).then_inc(a_Y0, 1)
            for r in range(ROUNDS):
                for gr in range(NG):
                    n = NG * r + gr
                    dve.wait_ge(n_P, n + 1)
                    i15 = rep(ident15[:, :].rearrange("p (o n) -> p o n", o=1), 1, GP)
                    v.scalar_tensor_tensor(out=Tm[:, GP * gr:GP * (gr + 1), :],
                                           in0=bank[gr % 2][:, :].rearrange("p (i n) -> p i n", n=P), scalar=-0.5, in1=i15,
                                           op0=ALU.mult, op1=ALU.add).then_inc(n_T, 1)
                    if gr >= 1:
                        dve.wait_ge(n_YZ, n)
                        v.tensor_copy(flat(Zm, gr - 1), bank[4 + (gr - 1) % 2][:, :]).then_inc(n_Z, 1)
                dve.wait_ge(n_YZ, NG * (r + 1))
                v.tensor_copy(flat(Zm, NG - 1), bank[4 + (NG - 1) % 2][:, :]).then_inc(n_Z, 1)
            dve.wait_ge(vecs_ready, 1)
            v.tensor_copy(cols[:, :], bank[0][:, 0:NROWS]).then_inc(cols_ready, 1)
            dve.wait_ge(cols_ready, 1)
            v.tensor_scalar(half_gb2[:, :], cols[:, ROW_GB2:ROW_GB2 + 1], 0.5, None, ALU.mult).then_inc(cols_ready, 1)
            dve.wait_ge(n_Y, NG * ROUNDS)
            v.tensor_reduce(u_sum[:, :], Ym[:, :, :], AX.X, ALU.add).then_inc(a_u, 1)
            dve.wait_ge(a_zu, 1)
            v.tensor_copy(zu[:, :], bank[7][:, 0:NP]).then_inc(a_zus, 1)
            dve.wait_ge(a_u, 1)
            v.tensor_scalar(ycol[:, 0, :], u_sum[:, :], 1.5 / C, None, ALU.mult).then_inc(a_y, 1)
            dve.wait_ge(a_w, 1)
            dve.wait_ge(a_y, 1)
            v.scalar_tensor_tensor(out=ycol[:, 1, :], in0=bank[6][:, 32:32 + NP], scalar=-0.5 / C, in1=ycol[:, 0, :],
                                   op0=ALU.mult, op1=ALU.add).then_inc(a_y, 1)
            dve.wait_ge(a_y, 2)
            dve.wait_ge(a_root, 1)
            v.tensor_tensor(ycol[:, 2, :], ycol[:, 1, :], root[:, :], ALU.mult).then_inc(a_y, 1)
            dve.wait_ge(g_s, 1)
            v.tensor_scalar(g2[:, 1, :], g2[:, 0, :], 0.5, 0.5, ALU.mult, ALU.add).then_inc(g_sp, 1)
            dve.wait_ge(g_sp, 1)
            v.tensor_tensor(gspread[:, :, :], over(g2[:, 1, :], NP), rep(two_ident[:, :].rearrange("p (o c) -> p o c", o=1), 1, NP),
                            ALU.mult).then_inc(g_sp, 1)

            split(router[:, 0, :], router[:, 1, :], cols[:, ROW_ROUTER:NROWS])
            dve.wait_ge(w_moe, W_MOE)
            split(w1s[:, 0, :], w1s[:, 1, :], w1f[:, :])
            dve.wait_ge(w_ffn, W_FFN)
            split(f1s[:, 0, :], f1s[:, 1, :], f1f[:, :])
            v.tensor_copy(sel[:, :, :], sel_f[:, :, :]).then_inc(w_split, 1)
            assert split.n == 6
            col = lambda name: cols[:, ROW[name]:ROW[name] + KP]
            for i, n in enumerate("12"):
                v.tensor_scalar(bn_t[:, 2 * i, :], col("L1_ffn_v" + n), EPS_BN, None, ALU.add).then_inc(bn_step, 1)
            for i, (n, bn) in enumerate((("1", bn1), ("2", bn2))):
                dve.wait_ge(bn_pow, i + 1)
                k = 2 + 4 * i
                v.tensor_tensor(bn[:, 0, :], bn_t[:, 2 * i + 1, :], col("L1_ffn_g" + n), ALU.mult).then_inc(bn_step, 1)
                v.tensor_tensor(bn_t[:, 2 * i, :], col("L1_ffn_b" + n), col("L1_ffn_m" + n), ALU.subtract).then_inc(bn_step, 1)
                dve.wait_ge(bn_step, k + 2)
                v.tensor_tensor(bn_t[:, 2 * i + 1, :], bn_t[:, 2 * i, :], bn[:, 0, :], ALU.mult).then_inc(bn_step, 1)
                dve.wait_ge(bn_step, k + 3)
                v.tensor_tensor(bn[:, 1, :], bn_t[:, 2 * i + 1, :], col("L1_ffn_be" + n), ALU.add).then_inc(bn_step, 1)
            dve.wait_ge(bn_step, 10)
            v.tensor_scalar(bn2[:, 2, :], bn2[:, 1, :], -1.0, None, ALU.mult).then_inc(bn_step, 1)
            for k in range(KP):
                for half in range(2):
                    s = slice(C * half, C * (half + 1))
                    v.tensor_copy(b2sel[s, k, 2 * k + half:2 * k + half + 1], bn2[s, 1, k:k + 1]).then_inc(bn_step, 1)
            dve.wait_ge(s2_spread, 1)
            v.tensor_tensor(f2[:, :, :], f2[:, :, :], bank[5][:, :].rearrange("p (k n) -> p k n", n=P), ALU.mult).then_inc(bn_step, 1)
            dve.wait_ge(conv_wT, 1)
            for half in range(2):
                last = v.tensor_copy(wdT[:, :, half, :], bank[2][0:C, :].rearrange("p (d c) -> p d c", d=8))
            last.then_inc(conv_wTs, 1)
            v.tensor_copy(wcT[:, :, :].rearrange("p d c -> p (d c)"), bank[3][0:C, :]).then_inc(conv_wTs, 1)
            dve.wait_ge(conv_v, 1)
            v8 = bank[4][:, :].rearrange("p (d o) -> p d o", d=8)
            v.tensor_copy(vconv[:, :, 0, :], v8).then_inc(conv_vs, 1)
            dve.wait_ge(conv_vs, 1)
            v.tensor_tensor(vconv[:, :, 1, :], v8, vconv[:, :, 0, :].bitcast(F32), ALU.subtract).then_inc(conv_vs, 1)
            v.memset(xp[:, :, :, :].bitcast(F32), 0.0).then_inc(consts_v, 1)
            v.memset(chl[:, :, :, :].bitcast(F32), 0.0).then_inc(consts_v, 1)
            dve.wait_ge(consts_v, 2)

            def moe_norm(b):
                dve.wait_ge(m_x1, b + 1)
                wait(dve, m_ve, b)
                src = blk(x, b)
                token_stats(b, lambda t: src[:, t, :], T2, m_st, m_mv)
                dve.wait_ge(m_mv, b + 1)
                v.tensor_tensor(xc[:, :, :], src, over(mv[:, 0:T2, 0], T2), ALU.subtract).then_inc(m_xc, 1)

            def moe_norm2(b):
                u = b % 2
                dve.wait_ge(m_rs, b + 1)
                dve.wait_ge(m_xc, b + 1)
                wait(dve, m_xr, b - 1)
                wait(dve, m_lo, b - 1)
                wait(dve, m_hi, b - 1)
                v.tensor_tensor(xnb[:, u], xc[:, :, :], over(rstd[:, 0:T2], T2), ALU.mult).then_inc(m_xn, 1)

            ROUTE = 19

            def route(b, part=None):
                st = route.st
                if part in (None, 0):
                    st["n"] = ROUTE * b

                def step(ins):
                    ins.then_inc(m_route, 1)
                    st["n"] += 1

                def sync():
                    dve.wait_ge(m_route, st["n"])

                mx = lambda i: m12[:, i, :]
                rk = rep(rank[:, :].rearrange("p (o e) -> p o e", o=1), 1, T2)
                TT = v.tensor_tensor

                def best(values, m, onehot):
                    step(v.tensor_reduce(mx(m), values, AX.X, ALU.max))
                    sync()
                    step(TT(onehot, values, over(mx(m), T2, E), ALU.is_equal))
                    sync()
                    step(TT(onehot, onehot, rk, ALU.mult))
                    sync()
                    step(v.tensor_reduce(mx(7), onehot, AX.X, ALU.max))
                    sync()
                    step(TT(onehot, onehot, over(mx(7), T2, E), ALU.is_equal))
                    sync()
                if part in (None, 0):
                    dve.wait_ge(m_L, 2 * b + 2)
                    for q in range(2):
                        lq = bank[6 + q][:, 0:T * 2 * E].rearrange("p (t s e) -> p t e s", t=T, s=2)
                        step(v.tensor_reduce(lg[:, T * q:T * (q + 1), :], lq, AX.X, ALU.add))
                    sync()
                    best(lg[:, :, :], 0, one1[:, :, :])
                if part in (None, 1):
                    step(v.scalar_tensor_tensor(out=tmp[:, :, :], in0=one1[:, :, :], scalar=-3.0e38, in1=lg[:, :, :],
                                                op0=ALU.mult, op1=ALU.add))
                    sync()
                    best(tmp[:, :, :], 1, one2[:, :, :])
                if part in (None, 2):
                    step(TT(mx(2), mx(1), mx(0), ALU.subtract))
                    dve.wait_ge(m_tanh, b + 1)
                    step(v.tensor_scalar(mx(4), mx(3), 0.5, 0.5, ALU.mult, ALU.add))
                    step(v.tensor_scalar(mx(5), mx(3), -0.5, 0.5, ALU.mult, ALU.add))
                    sync()
                    step(TT(one1[:, :, :], one1[:, :, :], over(mx(5), T2, E), ALU.mult))
                    step(TT(one2[:, :, :], one2[:, :, :], over(mx(4), T2, E), ALU.mult))
                    sync()
                    step(TT(cw[:, :, :], one1[:, :, :], one2[:, :, :], ALU.add))
                    assert st["n"] == ROUTE * (b + 1)
                    sync()
                    wait(dve, m_C, 2 * b)
                    v.tensor_copy(chl[:, :, 0, :], cw[:, :, :]).then_inc(m_chl, 1)
                    dve.wait_ge(m_chl, 2 * b + 1)
                    v.tensor_tensor(chl[:, :, 1, :], cw[:, :, :], chl[:, :, 0, :].bitcast(F32), ALU.subtract).then_inc(m_chl, 1)
            route.st = {}

            def moe_add(b, q):
                dve.wait_ge(m_yo, 2 * b + q + 1)
                dve.wait_ge(m_xr, b + 1)
                i = 2 * b + q
                v.tensor_tensor(x[:, i, :], x[:, i, :], bank[4 + q][:, 2 * P:4 * P], ALU.add).then_inc(m_res, 1)

            def moe_scale(b, n):
                N = 8 * b + n
                dve.wait_ge(m_cb, N + 1)
                dve.wait_ge(m_act, N + 1)
                wait(dve, m_l2, N - 1)
                v.tensor_tensor(scaled[:, n % 2, :], act[:, n % 2, :], bank[2 + n % 2][:, :], ALU.mult).then_inc(m_sc, 1)

            moe_norm(0)
            moe_norm2(0)
            route(0)
            moe_norm(1)
            moe_norm2(1)
            for b in range(NB):
                more, more2 = b + 1 < NB, b + 2 < NB
                moe_scale(b, 0)
                if more2:
                    moe_norm(b + 2)
                moe_scale(b, 1)
                moe_scale(b, 2)
                moe_scale(b, 3)
                if b:
                    moe_add(b - 1, 1)
                if more2:
                    moe_norm2(b + 2)
                moe_scale(b, 4)
                if more:
                    route(b + 1, 0)
                moe_scale(b, 5)
                if more:
                    route(b + 1, 1)
                moe_scale(b, 6)
                if more:
                    route(b + 1, 2)
                moe_scale(b, 7)
                moe_add(b, 0)
            moe_add(NB - 1, 1)

            def norm(b, u, s_st, s_mv, s_ve, s_rs, s_xc, s_xn, used):
                src = blk(x, b)
                wait(dve, s_ve, b)
                token_stats(b, lambda t: src[:, t, :], T2, s_st, s_mv)
                dve.wait_ge(s_mv, b + 1)
                v.tensor_tensor(xc[:, :, :], src, over(mv[:, 0:T2, 0], T2), ALU.subtract).then_inc(s_xc, 1)
                dve.wait_ge(s_xc, b + 1)
                dve.wait_ge(s_rs, b + 1)
                for s_used, k in used:
                    wait(dve, s_used, k)
                v.tensor_tensor(xnb[:, u], xc[:, :, :], over(rstd[:, 0:T2], T2), ALU.mult).then_inc(s_xn, 1)

            for b in range(NB):
                dve.wait_ge(m_res, 2 * b + 2)
                norm(b, 0, c_st, c_mv, c_ve, c_rs, c_xc, c_xn, [(c_lo, b), (c_hi, b), (m_xr, NB), (m_lo, NB), (m_hi, NB), (d_ve, b)])
                for q in range(2):
                    i = 2 * b + q
                    dve.wait_ge(c_bk, i + 1)
                    bt = bank[4 + q][:, :].rearrange("p (t s c) -> p t s c", t=T, s=2)
                    xi = x[:, i, :].rearrange("p (t c) -> p t c", t=T)
                    v.tensor_tensor(xi, xi, bt[:, :, 0, :], ALU.add).then_inc(c_r1, 1)
                    dve.wait_ge(c_r1, i + 1)
                    v.tensor_tensor(xi, xi, bt[:, :, 1, :], ALU.add).then_inc(c_r2, 1)
                dve.wait_ge(c_r2, 2 * b + 2)
                norm(b, 1, d_st, d_mv, d_ve, d_rs, d_xc, d_xn, [(d_lo, b), (d_hi, b), (d_acc, b)])

            def rstep(n, ins):
                ins.then_inc(r_dve, 1)
            dve.wait_ge(r_pe, 1)
            rstep(R_FEAT, v.tensor_copy(feat[:, :, :].rearrange("p t c -> p (t c)"), bank[0][:, 0:T * C]))
            dve.wait_ge(r_pe, 2)
            rstep(R_FEATT, v.tensor_copy(featT[:, :], bank[1][0:C, :]))
            dve.wait_ge(r_pe, 3)
            brb = rep(br[:, :].rearrange("p (o e) -> p o e", o=1), 1, T)
            rstep(R_LOG, v.tensor_tensor(fl[:, 0], bank[2][:, 0:T * E].rearrange("p (t e) -> p t e", t=T), brb, ALU.add))
            dve.wait_ge(r_dve, R_LOG)
            rstep(R_MAX, v.tensor_reduce(fm[:, 0, :], fl[:, 0], AX.X, ALU.max))
            dve.wait_ge(r_dve, R_MAX)
            rstep(R_SUB, v.tensor_tensor(fl[:, 1], fl[:, 0], over(fm[:, 0, :], T, E), ALU.subtract))
            dve.wait_ge(r_act, 1)
            rstep(R_SUM, v.tensor_reduce(fm[:, 1, :], fl[:, 2], AX.X, ALU.add))
            dve.wait_ge(r_dve, R_SUM)
            rstep(R_REC, v.reciprocal(fm[:, 2, :], fm[:, 1, :]))
            dve.wait_ge(r_dve, R_REC)
            rstep(R_W, v.tensor_tensor(fl[:, 3], fl[:, 2], over(fm[:, 2, :], T, E), ALU.mult))
            dve.wait_ge(r_dve, R_W)
            rstep(R_WREP, v.tensor_copy(wrep, rep(fl[:, 3].rearrange("p t (e o) -> p t e o", o=1), 3, C)))
            dve.wait_ge(r_pe, 4)
            rstep(R_WT, v.tensor_copy(wtT[:, :], bank[3][0:E, :]))
            dve.wait_ge(r_pe, 5)
            rstep(R_U8, v.tensor_tensor(u8[:, :], bank[4][0:E, 0:C], bo[:, :], ALU.add))
            dve.wait_ge(r_pe, 6)
            rstep(R_CTAB, v.tensor_copy(ctab[:, :], bank[5][:, 0:T * C]))
            for k in range(KP):
                dve.wait_ge(r_pe, 7 + k)
                rstep(R_WS + k, v.tensor_copy(wspread[:, k, :], bank[k][:, :]))

            def ffn_add(b, q):
                i = 2 * b + q
                dve.wait_ge(f_yo, i + 1)
                dve.wait_ge(r_add, b + 1)
                v.tensor_tensor(x[:, i, :], x[:, i, :], bank[4 + q][:, 2 * P:4 * P], ALU.add).then_inc(f_res, 1)

            for b in range(NB):
                for n in range(8):
                    N, k = 8 * b + n, n % KP
                    dve.wait_ge(f_z2, N + 1)
                    wait(dve, f_l3, N - 1)
                    if b == 0:
                        dve.wait_ge(r_dve, R_WS + k)
                    v.scalar_tensor_tensor(out=scaled[:, n % 2, :], in0=bank[2 + n % 2][:, :], scalar=bn2[:, 2, k:k + 1],
                                           in1=wspread[:, k, :], op0=ALU.max, op1=ALU.mult).then_inc(f_h2, 1)
                    if n == 3 and b:
                        ffn_add(b - 1, 1)
                ffn_add(b, 0)
            ffn_add(NB - 1, 1)

        @block.scalar
        def _(act_e):
            s = nc.scalar
            for gr in range(NG):
                act_e.wait_ge(a_xcc, gr + 1)
                for i in range(GP):
                    if gr or i:
                        act_e.wait_ge(a_sqj, GP * gr + i)
                    last = s.activation(sqj[:, :], xcc[:, i, :], ACT.Square, accum_out=sumsq[:, GP * gr + i:GP * gr + i + 1])
                    last.then_inc(a_sqj, 1)
                for c in range(2):
                    act_e.wait_ge(a_xT, 2 * gr + c + 1)
                    wait(act_e, a_gram, gr)
                    s.activation(xT[:, c, :], bank[4 + c][:, :], ACT.Copy).then_inc(a_xTs, 1)
            for r in range(ROUNDS):
                for gr in range(NG):
                    act_e.wait_ge(n_YZ, NG * r + gr + 1)
                    s.activation(Ym[:, GP * gr:GP * (gr + 1), :].rearrange("p i n -> p (i n)"), bank[2 + gr % 2][:, :],
                                 ACT.Copy).then_inc(n_Y, 1)
            act_e.wait_ge(g_c1, 1)
            act_e.wait_ge(cols_ready, 2)
            s.activation(g1[:, :], bank[7][:, 32:32 + NP], ACT.Relu, bias=cols[:, ROW_GB1:ROW_GB1 + 1]).then_inc(g_r1, 1)
            act_e.wait_ge(g_c2, 1)
            s.activation(g2[:, 0, :], bank[6][:, 64:64 + NP], ACT.Tanh, scale=0.5, bias=half_gb2[:, 0:1]).then_inc(g_s, 1)
            for i in range(2):
                act_e.wait_ge(g_G, i + 1)
                s.activation(gate[:, 8 * i:8 * (i + 1), :].rearrange("p i c -> p (i c)"), bank[i][:, :], ACT.Copy).then_inc(g_done, 1)

            def evac_x(b, q):
                act_e.wait_ge(m_X, 2 * b + q + 1)
                s.activation(xs[:, b % 2, CH * q:CH * (q + 1)], bank[6 + q][:, :], ACT.Copy).then_inc(m_xs, 1)

            def hi(b, u, s_xn, s_hi, free):
                act_e.wait_ge(s_xn, b + 1)
                for s_used, k in free:
                    wait(act_e, s_used, k)
                s.activation(hl[:, :, 0, :], xnb[:, u], ACT.Copy).then_inc(s_hi, 1)

            def tanh(b):
                act_e.wait_ge(m_route, 19 * b + 14)
                s.activation(m12[:, 3, :], m12[:, 2, :], ACT.Tanh, scale=0.5).then_inc(m_tanh, 1)

            def evac_c(b, q):
                act_e.wait_ge(m_C, 2 * b + q + 1)
                s.activation(cs[:, CH * q:CH * (q + 1)], bank[6 + q][:, :], ACT.Copy).then_inc(m_cs, 1)

            def evac_y(b, q):
                act_e.wait_ge(m_l2, KP * (2 * b + q + 1))
                wait(act_e, m_yo, 2 * b + q - 1)
                s.activation(yTs[:, q, :], bank[4 + q][:, 0:2 * P], ACT.Copy).then_inc(m_yT, 1)

            def gelu(b, n):
                N = 8 * b + n
                act_e.wait_ge(m_z, N + 1)
                wait(act_e, m_sc, N - 1)
                s.activation(act[:, n % 2, :], bank[n % 2][:, :], ACT.Gelu, bias=cols[:, n % KP:n % KP + 1]).then_inc(m_act, 1)

            hi(0, 0, m_xn, m_hi, [])
            evac_x(0, 0)
            evac_x(0, 1)
            tanh(0)
            hi(1, 1, m_xn, m_hi, [(m_X, 2)])
            for b in range(NB):
                more, more2 = b + 1 < NB, b + 2 < NB
                evac_c(b, 0)
                evac_c(b, 1)
                gelu(b, 0)
                if more:
                    evac_x(b + 1, 0)
                gelu(b, 1)
                if more:
                    evac_x(b + 1, 1)
                gelu(b, 2)
                if b:
                    evac_y(b - 1, 1)
                gelu(b, 3)
                gelu(b, 4)
                gelu(b, 5)
                if more2:
                    hi(b + 2, b % 2, m_xn, m_hi, [(m_X, 2 * b + 4)])
                gelu(b, 6)
                evac_y(b, 0)
                if more:
                    tanh(b + 1)
                gelu(b, 7)
            evac_y(NB - 1, 1)

            for b in range(NB):
                hi(b, 0, c_xn, c_hi, [(m_X, 2 * NB), (d_X, 2 * b)])
                for q in range(2):
                    i = 2 * b + q
                    act_e.wait_ge(c_X, i + 1)
                    wait(act_e, c_cv, i - 1)
                    if i == 0:
                        act_e.wait_ge(consts_v, 1)
                    src = bank[6 + q][:, :].rearrange("p (t i r w) -> p i r w t", t=T, i=2, r=H)
                    for j in range(2):
                        dst = xp[:, 2 * q + j, 1:H + 1, 1:W + 1].rearrange("p r (w t) -> p r w t", t=T)
                        last = s.activation(dst, src[:, j], ACT.Copy)
                    last.then_inc(c_xp, 1)
                for q in range(2):
                    i = 2 * b + q
                    act_e.wait_ge(c_cv, i + 1)
                    wait(act_e, c_bk, i - 1)
                    s.activation(cvs[:, q, :], bank[q][:, :], ACT.Identity, bias=cols[:, ROW_BC:ROW_BC + 1]).then_inc(c_cvs, 1)
                hi(b, 1, d_xn, d_hi, [(c_X, 2 * b + 2)])
                for q in range(2):
                    i = 2 * b + q
                    act_e.wait_ge(d_X, i + 1)
                    s.activation(xs_ffn[:, b, CH * q:CH * (q + 1)], bank[6 + q][:, :], ACT.Copy).then_inc(d_xs, 1)

            act_e.wait_ge(r_dve, R_SUB)
            s.activation(fl[:, 2], fl[:, 1], ACT.Exp).then_inc(r_act, 1)

            def evac_f(b, q):
                act_e.wait_ge(f_l3, KP * (2 * b + q + 1))
                wait(act_e, f_yo, 2 * b + q - 1)
                s.activation(yTs[:, q, :], bank[4 + q][:, 0:2 * P], ACT.Copy).then_inc(f_yT, 1)

            for b in range(NB):
                for n in range(8):
                    N, k = 8 * b + n, n % KP
                    act_e.wait_ge(f_z1, N + 1)
                    wait(act_e, f_z2, N - 1)
                    if N == 0:
                        act_e.wait_ge(bn_step, 19)
                    s.activation(act[:, n % 2, :], bank[6 + n % 2][:, :], ACT.Relu, scale=bn1[:, 0, k:k + 1],
                                 bias=bn1[:, 1, k:k + 1]).then_inc(f_h1, 1)
                    if n == 2 and b:
                        evac_f(b - 1, 1)
                    if n == 6:
                        evac_f(b, 0)
            evac_f(NB - 1, 1)

        @block.tensor
        def _(pe):
            t = nc.tensor
            pe.wait_ge(consts, 27)
            for gr in range(NG):
                pe.wait_ge(a_xcc, gr + 1)
                wait(pe, a_xTs, 2 * gr)
                for c in range(2):
                    for i in range(GP):
                        last = t.transpose(bank[4 + c][:, P * i:P * (i + 1)], xcc[:, i, P * c:P * (c + 1)], ident[:, :])
                    last.then_inc(a_xT, 1)
                pe.wait_ge(a_sqj, GP * (gr + 1))
                wait(pe, a_rtr, 2 * gr)
                t.matmul(bank[6][:, GP * gr:GP * (gr + 1)], same_img[:, :], sumsq[:, GP * gr:GP * (gr + 1)],
                         start=True, stop=True).then_inc(a_trace, 1)
                pe.wait_ge(a_xTs, 2 * gr + 2)
                wait(pe, a_A, gr - 1)
                for i in range(GP):
                    cs_ = slice(P * i, P * (i + 1))
                    for c in range(2):
                        last = t.matmul(bank[gr % 2][:, cs_], xT[:, c, cs_], xT[:, c, cs_], start=(c == 0), stop=(c == 1))
                last.then_inc(a_gram, 1)
            for gr in range(NG):
                pe.wait_ge(a_A, gr + 1)
                wait(pe, a_Y0, gr - 1)
                for i in range(GP):
                    k = GP * gr + i
                    last = t.matmul(bank[2 + gr % 2][:, P * i:P * (i + 1)], Am[:, k, :], Am[:, k, :], start=True, stop=True)
                last.then_inc(a_P0, 1)

            def prod_p(r, gr):
                n = NG * r + gr
                pe.wait_ge(a_Y0, gr + 1)
                if r == 0:
                    pe.wait_ge(a_Z0, gr + 1)
                    pe.wait_ge(a_A, NG)
                wait(pe, n_Y, n - NG + 1)
                wait(pe, n_Z, n - NG + 1)
                wait(pe, n_T, n - 1)
                for i in range(GP):
                    k = GP * gr + i
                    last = t.matmul(bank[gr % 2][:, P * i:P * (i + 1)], Zm[:, k, :], Ym[:, k, :], start=True, stop=True)
                last.then_inc(n_P, 1)

            def prod_yz(r, gr):
                n = NG * r + gr
                pe.wait_ge(n_T, n + 1)
                wait(pe, n_Y, n - 1)
                wait(pe, n_Z, n - 1)
                if r == 0:
                    pe.wait_ge(a_Y0, NG)
                for b0, src in ((2, Ym), (4, Zm)):
                    for i in range(GP):
                        k = GP * gr + i
                        last = t.matmul(bank[b0 + gr % 2][:, P * i:P * (i + 1)], Tm[:, k, :], src[:, k, :], start=True, stop=True)
                last.then_inc(n_YZ, 1)

            for r in range(ROUNDS):
                prod_p(r, 0)
                prod_p(r, 1)
                prod_yz(r, 0)
                prod_p(r, 2)
                prod_yz(r, 1)
                prod_p(r, 3)
                prod_yz(r, 2)
                prod_yz(r, 3)
            pe.wait_ge(w_vec, W_VEC)
            pe.wait_ge(n_T, NG * ROUNDS)
            t.transpose(bank[0][:, 0:NROWS], vec_rows[:, :], ident[0:NROWS, 0:NROWS]).then_inc(vecs_ready, 1)
            pe.wait_ge(a_u, 1)
            pe.wait_ge(n_Z, NG * ROUNDS)
            for i in range(NP):
                last = t.matmul(bank[7][:, i:i + 1], Zm[:, i, :], u_sum[:, i:i + 1], start=True, stop=True)
            last.then_inc(a_zu, 1)
            pe.wait_ge(a_zus, 1)
            pe.wait_ge(a_trm, 1)
            pe.wait_ge(a_rtr, 7)
            for i in range(NP):
                last = t.matmul(bank[6][:, 32 + i:33 + i], Ym[:, i, :], zu[:, i:i + 1], start=True, stop=True)
            last.then_inc(a_w, 1)
            pe.wait_ge(a_y, 3)
            pe.wait_ge(w_gate, W_GATE)
            t.matmul(bank[7][:, 32:32 + NP], gw1[:, :], ycol[:, 2, :], start=True, stop=True).then_inc(g_c1, 1)
            pe.wait_ge(g_r1, 1)
            t.matmul(bank[6][:, 64:64 + NP], gw2[:, :], g1[:, :], start=True, stop=True).then_inc(g_c2, 1)
            pe.wait_ge(g_sp, 2)
            pe.wait_ge(cols_ready, 1)
            for i in range(2):
                t.matmul(bank[i][:, :], same_img[:, :], gspread[:, 8 * i:8 * (i + 1), :].rearrange("p i c -> p (i c)"),
                         start=True, stop=True).then_inc(g_G, 1)
            pe.wait_ge(bn_step, 10)
            pe.wait_ge(n_Z, NG * ROUNDS)
            for k in range(KP):
                last = t.transpose(bank[5][:, P * k:P * (k + 1)], rep(bn2[:, 0, k:k + 1], 1, P), ident[:, :])
            last.then_inc(s2_spread, 1)
            pe.wait_ge(w_conv, W_CONV)
            pe.wait_ge(n_Y, NG * ROUNDS)
            for k in range(4):
                t.transpose(bank[2][0:C, P * k:P * (k + 1)], wd[:, k, :], ident[:, :])
            for d in range(8):
                last = t.transpose(bank[3][0:C, C * d:C * (d + 1)], wc[:, d, :], ident[0:C, 0:C])
            last.then_inc(conv_wT, 1)
            pe.wait_ge(conv_wTs, 2)
            for d in range(8):
                last = t.matmul(bank[4][:, C * d:C * (d + 1)],
                                wdT[:, d, :, :].rearrange("p o c -> p (o c)"),
                                wcT[:, d, :], start=True, stop=True)
            last.then_inc(conv_v, 1)

            def moe_x(b, q):
                pe.wait_ge(m_lo, b + 1)
                for j in range(T):
                    last = t.transpose(bank[6 + q][:, P * j:P * (j + 1)],
                                       hl[:, T * q + j, :, :].rearrange("p s c -> p (s c)").bitcast(F32), ident[:, :])
                last.then_inc(m_X, 1)

            def moe_logits(b, q):
                pe.wait_ge(m_xs, 2 * b + q + 1)
                for j in range(T):
                    last = t.matmul(bank[6 + q][:, 2 * E * j:2 * E * (j + 1)],
                                    xs[:, b % 2, CH * q + P * j:CH * q + P * (j + 1)],
                                    router[:, :, :].rearrange("p s e -> p (s e)"), start=True, stop=True)
                last.then_inc(m_L, 1)

            def moe_c(b, q):
                pe.wait_ge(m_chl, 2 * b + 2)
                for j in range(T):
                    last = t.transpose(bank[6 + q][:, P * j:P * (j + 1)],
                                       chl[:, T * q + j, :, :].rearrange("p s e -> p (s e)").bitcast(F32), ident[:, :])
                last.then_inc(m_C, 1)

            def moe_first(b, n):
                N, q, k = 8 * b + n, n // KP, n % KP
                wait(pe, m_sc, N - 1)
                pe.wait_ge(m_cs, 2 * b + q + 1)
                t.matmul(bank[2 + n % 2][:, :], sel[:, k, :], cs[:, CH * q:CH * (q + 1)], start=True, stop=True).then_inc(m_cb, 1)
                wait(pe, m_act, N - 1)
                for part in range(2):
                    last = t.matmul(bank[n % 2][:, :], w1s[:, part, P * k:P * (k + 1)], xs[:, b % 2, CH * q:CH * (q + 1)],
                                    start=(part == 0), stop=(part == 1))
                last.then_inc(m_z, 1)

            def moe_second(b, n):
                N, q, k = 8 * b + n, n // KP, n % KP
                if k == 0:
                    wait(pe, m_yT, 2 * b + q - 1)
                    wait(pe, m_res, 2 * b + q - 1)
                    for half in range(2):
                        t.matmul(bank[4 + q][C * half:C * (half + 1), 0:2 * P], b2rows[:, :],
                                 cs[:, CH * q + 2 * P * half:CH * q + 2 * P * (half + 1)].bitcast(F32), start=True, stop=False)
                pe.wait_ge(m_sc, N + 1)
                for half in range(2):
                    last = t.matmul(bank[4 + q][C * half:C * (half + 1), 0:2 * P], w2[:, k, :],
                                    scaled[:, n % 2, 2 * P * half:2 * P * (half + 1)], start=False, stop=(k == KP - 1))
                last.then_inc(m_l2, 1)

            def back(yt, s_yT, s_yo, b, q):
                pe.wait_ge(s_yT, 2 * b + q + 1)
                o = bank[4 + q][:, 2 * P:4 * P].rearrange("p (h j c) -> p j h c", h=2, j=2)
                for j in range(2):
                    last = t.transpose(o[:, j], yt[:, q, P * j:P * (j + 1)], ident[:, :])
                last.then_inc(s_yo, 1)

            pe.wait_ge(g_c2, 1)
            pe.wait_ge(g_s, 1)
            pe.wait_ge(a_zus, 1)
            moe_x(0, 0)
            moe_x(0, 1)
            pe.wait_ge(w_split, 7)
            moe_logits(0, 0)
            moe_logits(0, 1)
            pe.wait_ge(g_done, 2)
            pe.wait_ge(conv_wTs, 2)
            pe.wait_ge(conv_vs, 2)
            pe.wait_ge(bn_step, 20)
            for b in range(NB):
                more = b + 1 < NB
                pe.wait_ge(m_chl, 2 * b + 2)
                moe_c(b, 0)
                moe_c(b, 1)
                for n in range(8):
                    moe_first(b, n)
                    if n >= 2:
                        moe_second(b, n - 2)
                    elif b:
                        moe_second(b - 1, n + 6)
                    if n == 0 and more:
                        pe.wait_ge(m_cs, 2 * b + 1)
                        moe_x(b + 1, 0)
                    if n == 1 and more:
                        pe.wait_ge(m_cs, 2 * b + 2)
                        moe_x(b + 1, 1)
                    if n == 3:
                        if more:
                            moe_logits(b + 1, 0)
                        if b:
                            back(yTs, m_yT, m_yo, b - 1, 1)
                    if n == 4 and more:
                        moe_logits(b + 1, 1)
                back(yTs, m_yT, m_yo, b, 0)
            moe_second(NB - 1, 6)
            moe_second(NB - 1, 7)
            back(yTs, m_yT, m_yo, NB - 1, 1)

            pe.wait_ge(m_act, 8 * NB)
            for b in range(NB):
                pe.wait_ge(c_lo, b + 1)
                wait(pe, d_xs, 2 * b)
                for q in range(2):
                    for j in range(T):
                        last = t.transpose(bank[6 + q][:, P * j:P * (j + 1)],
                                           hl[:, T * q + j, :, :].rearrange("p s c -> p (s c)").bitcast(F32), ident[:, :])
                    last.then_inc(c_X, 1)
                for q in range(2):
                    i = 2 * b + q
                    pe.wait_ge(c_xp, i + 1)
                    wait(pe, c_cvs, i - 1)
                    for d, (dx, dy) in enumerate(DIRECTIONS):
                        src = xp[:, 2 * q:2 * q + 2, 1 - dy:1 - dy + H, 1 - dx:1 - dx + W]
                        last = t.matmul(bank[q][:, :], vconv[:, d, :, :].rearrange("p s c -> p (s c)"), src,
                                        start=(d == 0), stop=(d == 7))
                    last.then_inc(c_cv, 1)
                for q in range(2):
                    i = 2 * b + q
                    pe.wait_ge(c_cvs, i + 1)
                    wait(pe, c_r2, i - 1)
                    pe.wait_ge(m_res, 2 * NB)
                    for j in range(T):
                        last = t.transpose(bank[4 + q][:, P * j:P * (j + 1)], cvs[:, q, j:CH:T], ident[:, :])
                    last.then_inc(c_bk, 1)
                pe.wait_ge(d_lo, b + 1)
                pe.wait_ge(c_xp, 2 * b + 2)
                for q in range(2):
                    for j in range(T):
                        last = t.transpose(bank[6 + q][:, P * j:P * (j + 1)],
                                           hl[:, T * q + j, :, :].rearrange("p s c -> p (s c)").bitcast(F32), ident[:, :])
                    last.then_inc(d_X, 1)

            pe.wait_ge(d_acc, NB)
            pe.wait_ge(c_cvs, 2 * NB)
            for q in range(2):
                last = t.matmul(bank[0][:, 0:T * C], half_mean[:, :], fsum[:, T * q:T * (q + 1), :].rearrange("p t c -> p (t c)"),
                                start=(q == 0), stop=(q == 1))
            last.then_inc(r_pe, 1)
            pe.wait_ge(r_dve, R_FEAT)
            for j in range(T):
                last = t.transpose(bank[1][0:C, P * j:P * (j + 1)], feat[:, j, :], ident[:, :])
            last.then_inc(r_pe, 1)
            pe.wait_ge(r_dve, R_FEATT)
            for j in range(T):
                last = t.matmul(bank[2][:, E * j:E * (j + 1)], featT[:, P * j:P * (j + 1)], wr[:, :], start=True, stop=True)
            last.then_inc(r_pe, 1)
            pe.wait_ge(r_dve, R_W)
            for j in range(T):
                last = t.transpose(bank[3][0:E, P * j:P * (j + 1)], fl[:, 3, j, :], ident[:, :])
            last.then_inc(r_pe, 1)
            pe.wait_ge(bn_step, 19)
            pe.wait_ge(c_r2, 2 * NB)
            for k in range(KP):
                last = t.matmul(bank[4][0:E, 0:C], b2sel[:, k, :], fo[:, k, :], start=(k == 0), stop=(k == KP - 1))
            last.then_inc(r_pe, 1)
            pe.wait_ge(r_dve, R_U8)
            for j in range(T):
                last = t.matmul(bank[5][:, C * j:C * (j + 1)], wtT[:, P * j:P * (j + 1)], u8[:, :], start=True, stop=True)
            last.then_inc(r_pe, 1)
            for k in range(KP):
                for j in range(T):
                    src = wrep[:, j, 2 * k:2 * k + 2, :].rearrange("p e c -> p (e c)")
                    last = t.transpose(bank[k][:, P * j:P * (j + 1)], src, ident[:, :])
                last.then_inc(r_pe, 1)

            def ffn1(N):
                b, n = divmod(N, 8)
                q, k = n // KP, n % KP
                wait(pe, f_h1, N - 1)
                if N < 2:
                    pe.wait_ge(d_xs, 2 * NB)
                for part in range(2):
                    last = t.matmul(bank[6 + n % 2][:, :], f1s[:, part, P * k:P * (k + 1)], xs_ffn[:, b, CH * q:CH * (q + 1)],
                                    start=(part == 0), stop=(part == 1))
                last.then_inc(f_z1, 1)

            def ffn2(N):
                b, n = divmod(N, 8)
                k = n % KP
                pe.wait_ge(f_h1, N + 1)
                wait(pe, f_h2, N - 1)
                if N < 2:
                    pe.wait_ge(r_dve, R_WS + 3)
                    pe.wait_ge(bn_step, 20)
                t.matmul(bank[2 + n % 2][:, :], f2[:, k, :], act[:, n % 2, :], start=True, stop=True).then_inc(f_z2, 1)

            def ffn3(N):
                b, n = divmod(N, 8)
                q, k = n // KP, n % KP
                if k == 0:
                    wait(pe, f_yT, 2 * b + q - 1)
                    wait(pe, f_res, 2 * b + q - 1)
                    if b == 0:
                        pe.wait_ge(r_dve, R_CTAB)
                pe.wait_ge(f_h2, N + 1)
                for half in range(2):
                    last = t.matmul(bank[4 + q][C * half:C * (half + 1), 0:2 * P], fo[:, k, :],
                                    scaled[:, n % 2, 2 * P * half:2 * P * (half + 1)], start=(k == 0), stop=(k == KP - 1))
                last.then_inc(f_l3, 1)

            for N in range(8 * NB + 2):
                if N < 8 * NB:
                    ffn1(N)
                if 1 <= N <= 8 * NB:
                    ffn2(N - 1)
                if N >= 2:
                    ffn3(N - 2)
                n = N % 8
                if n == 3 and N > 8:
                    back(yTs, f_yT, f_yo, N // 8 - 1, 1)
                if n == 7:
                    back(yTs, f_yT, f_yo, N // 8, 0)
            back(yTs, f_yT, f_yo, NB - 1, 1)


_INS = ['x', 'L0_conv_w1', 'L0_conv_b1', 'L0_conv_w2', 'L0_conv_b2', 'L0_ffn_router_w', 'L0_ffn_w1', 'L0_ffn_b1',
        'L0_ffn_w2', 'L0_ffn_b2', 'L1_conv_Wd', 'L1_conv_Wc', 'L1_conv_bc', 'L1_ffn_Wr', 'L1_ffn_br', 'L1_ffn_W1',
        'L1_ffn_b1', 'L1_ffn_g1', 'L1_ffn_be1', 'L1_ffn_m1', 'L1_ffn_v1', 'L1_ffn_W2', 'L1_ffn_b2', 'L1_ffn_g2',
        'L1_ffn_be2', 'L1_ffn_m2', 'L1_ffn_v2', 'L1_ffn_Wo', 'L1_ffn_bo']
_OUTS = [((32, 16, 16, 64), 'float32')]


def kernel(**inputs):
    import numpy as _np
    import concourse.bacc as _bacc
    from concourse import mybir as _mybir
    from concourse.bass_utils import run_bass_kernel_spmd as _run

    nc = _bacc.Bacc("TRN2", target_bir_lowering=False, num_devices=1)
    arrays, args = {}, {}
    for name in _INS:
        arr = _np.ascontiguousarray(inputs[name])
        arrays[f"in_{name}_dram"] = arr
        args[name] = nc.dram_tensor(f"in_{name}_dram", arr.shape, _mybir.dt.from_np(arr.dtype), kind="ExternalInput").ap()
    outs = []
    for i, (shape, dtype) in enumerate(_OUTS):
        dt = _mybir.dt.from_np(_np.dtype(dtype))
        outs.append(nc.dram_tensor(f"out_{i}_dram", shape, dt, kind="ExternalOutput").ap())
    metaformer_kernel(nc, args, outs[0])
    r = _run(nc, [arrays], core_ids=[0])
    got = tuple(r.results[0][f"out_{i}_dram"] for i in range(len(_OUTS)))
    return got[0]
```

```python
from contextlib import ExitStack

import concourse.bass as bass
from concourse import mybir

ALU = mybir.AluOpType
ACT = mybir.ActivationFunctionType
AX = mybir.AxisListType
F32 = mybir.dt.float32
F32R = mybir.dt.float32r

P = 128
B, H, W, C = 32, 16, 16, 64
E = 8
T = 4
NP = B // 2
KP = E // 2
CH = P * T
NB = NP // 2
T2 = 2 * T
NG = 4
GP = NP // NG
M = H * W
PADH, PADW = H + 2, W + 2
LAG = 4
NM = NB + LAG
EPS_C, EPS_T, EPS_BN = 1e-6, 1e-5, 1e-3
ROUNDS = 3
DIRECTIONS = [(0, -1), (1, -1), (1, 0), (1, 1), (0, 1), (-1, 1), (-1, 0), (-1, -1)]

VECS = ["L0_ffn_b1", "L1_ffn_b1", "L1_ffn_g1", "L1_ffn_be1", "L1_ffn_m1", "L1_ffn_v1",
        "L1_ffn_b2", "L1_ffn_g2", "L1_ffn_be2", "L1_ffn_m2", "L1_ffn_v2"]
ROW = {name: KP * n for n, name in enumerate(VECS)}
ROW_GB1 = KP * len(VECS)
ROW_GB2 = ROW_GB1 + 1
ROW_BC = ROW_GB1 + 2
ROW_ROUTER = ROW_GB1 + 4
NROWS = ROW_ROUTER + E


def wait(eng, sem, value):
    if isinstance(value, int) and value <= 0:
        return
    eng.wait_ge(sem, value)


def rep(ap, axis, n):
    shape = list(ap.shape)
    shape[axis] = n
    return ap.broadcast_to(shape)


def metaformer_kernel(nc, a, out):
    ctx = ExitStack()
    with ctx:
        def sb(name, shape, dt=F32):
            return ctx.enter_context(nc.sbuf_tensor(name, shape, dt))

        sems = {}

        def sem(name):
            sems[name] = ctx.enter_context(nc.semaphore(name))
            return sems[name]

        bank = [ctx.enter_context(nc.psum_tensor(f"bank{i}", [P, 512], F32)) for i in range(8)]

        x = sb("x", [P, NP, T * C])
        xn = sb("xn", [P, NP, T * C])
        gate = sb("gate", [P, NP, C])
        xs_ffn = sb("xs_ffn", [P, NB, T2 * P], F32R)

        ident = sb("ident", [P, P])
        two_ident15 = sb("two_ident15", [P, C])
        same_img = sb("same_img", [P, P])
        two_ident = sb("two_ident", [P, C])
        half_mean = sb("half_mean", [P, P])
        sel_f = sb("sel_f", [P, KP, P])
        sel = sb("sel", [P, KP, P], F32R)
        rank = sb("rank", [P, E])
        neg_half = sb("neg_half", [P, 16])
        pos_half = sb("pos_half", [P, 16])
        eps_vec = sb("eps_vec", [P, 2 * T2])

        vec_rows = sb("vec_rows", [NROWS, P])
        cols = sb("cols", [P, NROWS])
        gw1 = sb("gw1", [C, C])
        gw2 = sb("gw2", [C, C])
        half_gb2 = sb("half_gb2", [C, 1])
        w1f = sb("w1f", [P, E * C])
        w1s = sb("w1s", [P, 2, E * C], F32R)
        w2 = sb("w2", [P, KP, C])
        b2rows = sb("b2rows", [P, C])
        router = sb("router", [P, 2, E], F32R)
        wd = sb("wd", [P, 4, C])
        wc = sb("wc", [C, 8, C])
        wdT = sb("wdT", [C, 8, 2, C])
        wcT = sb("wcT", [C, 8, C])
        vconv = sb("vconv", [P, 8, 2, C], F32R)
        f1f = sb("f1f", [P, E * C])
        f1s = sb("f1s", [P, 2, E * C], F32R)
        f2 = sb("f2", [P, KP, P])
        fo = sb("fo", [P, KP, C])
        bo = sb("bo", [2 * E, C])
        wr = sb("wr", [C, E])
        br = sb("br", [P, E])
        bn1 = sb("bn1", [P, 2, KP])
        bn2 = sb("bn2", [P, 3, KP])
        bn_t = sb("bn_t", [P, 4, KP])

        stats = sb("stats", [P, 16, 6])
        mv2 = sb("mv", [P, 2, 16, 2])
        mv = mv2[:, 0]
        veps = sb("veps", [P, 16])
        rstd = sb("rstd", [P, 16])
        rsum = sb("rsum", [P, GP])
        rmean = sb("rmean", [P, 2, GP])
        xcc = [sb("xcc", [P, GP, M]), gate[:, :, :].rearrange("p (i u) c -> p i (u c)", i=GP)]
        sqj = sb("sqj", [P, M])
        sumsq = sb("sumsq", [P, NP])
        xT = sb("xT", [P, 2, GP * P])
        rtrace = sb("rtrace", [P, NP])
        trm = sb("trm", [P, NP])
        root = sb("root", [P, NP])
        Ac = sb("Ac", [P, NP, C])
        YZ = sb("YZ", [P, NP, 2, C])
        Zd = sb("Zd", [P, NP, P])
        Td = sb("Td", [P, NP, P])
        u_sum = sb("u_sum", [P, NP])
        u_own = sb("u_own", [P, NP, 2])
        z_own = sb("z_own", [P, NP, 2])
        yv = sb("yv", [C, 4, NP, 2])
        g1 = sb("g1", [C, NP * 2])
        g2 = sb("g2", [C, NP, 2])
        gsig = sb("gsig", [P, NP])
        gspread = sb("gspread", [P, NP, C])

        xc = sb("xc", [P, T2, C])
        xnb = sb("xnb", [P, 2, T2, C])
        hl = sb("hl", [P, T2, 2, C], F32R)
        xs = sb("xs", [P, 2, T2 * P], F32R)
        cs = sb("cs", [P, T2 * P], F32R)
        act = sb("act", [P, 2, CH])
        scaled = sb("scaled", [P, 2, CH])
        yTs = sb("yTs", [P, 2, 2 * P])
        lg = sb("lg", [P, T2, E])
        tmp = sb("tmp", [P, T2, E])
        one1 = sb("one1", [P, T2, E])
        one2 = sb("one2", [P, T2, E])
        m12 = sb("m12", [P, 8, T2])
        cw = sb("cw", [P, T2, E])
        chl = sb("chl", [P, T2, P // E, E], F32R)
        xp = sb("xp", [P, 4, PADH, PADW], F32R)
        cvs = sb("cvs", [P, 2, CH])
        xcn = Zd[:, 0:NP // 2, :].rearrange("p i (u c) -> p (i u) c", c=C)
        xnc = YZ[:, :, :, :].rearrange("p (v i) t c -> p v (i t) c", v=2)
        hlc = xn[:, :, :].bitcast(F32R).rearrange("p (v i) (t s c) -> p v (i t) s c", v=2, t=2, s=2)
        fsum = sb("fsum", [P, T2, C])
        feat = Td[:, 8:10, :].rearrange("p i (u c) -> p (i u) c", u=2)
        featT = Td[0:C, 0:4, :].rearrange("p i n -> p (i n)")
        fl = sb("fl", [P, 4, T, E])
        fm = sb("fm", [P, 4, T])
        whl = sb("whl", [P, T, 2, E], F32R)
        wT = sb("wT", [2 * E, T * P], F32R)
        wspread = YZ[:, :, :, :].rearrange("p (k i) t c -> p k (i t c)", k=KP)
        b2sel = sb("b2sel", [P, KP, 2, E])
        u16 = sb("u16", [2 * E, C])
        ctab = sb("ctab", [P, T * C])

        S = sem
        x_in = [S(f"x_in{g}") for g in range(NG)]
        w_gate, w_moe, w_conv, w_ffn, w_vec = S("w_gate"), S("w_moe"), S("w_conv"), S("w_ffn"), S("w_vec")
        consts, consts_v, zeroed = S("consts"), S("consts_v"), S("zeroed")
        vecs_ready, cols_ready = S("vecs_ready"), S("cols_ready")
        w_hi, w_lo, f2_scaled, b2_sel, diag_zero = (S(n) for n in ("w_hi", "w_lo", "f2_scaled", "b2_sel", "diag_zero"))
        bn_step, bn_pow, s2_spread = S("bn_step"), S("bn_pow"), S("s2_spread")
        conv_wT, conv_wTs, conv_v, conv_vs = S("conv_wT"), S("conv_wTs"), S("conv_v"), S("conv_vs")
        a_stats, a_mv, a_veps, a_rstd, a_xc, a_xn = (S(n) for n in ("a_stats", "a_mv", "a_veps", "a_rstd", "a_xc", "a_xn"))
        a_rsum, a_rmean, a_xcc, a_sq, a_xT, a_xTs, a_gram = (S(n) for n in ("a_rsum", "a_rmean", "a_xcc", "a_sq", "a_xT", "a_xTs", "a_gram"))
        a_trace, a_rtr, a_trm, a_root, a_A, a_Z0, a_Zd, a_P0, a_Y0 = (S(n) for n in ("a_trace", "a_rtr", "a_trm", "a_root", "a_A", "a_Z0", "a_Zd", "a_P0", "a_Y0"))
        n_P, n_T, n_YZ, n_C, n_Z = (S(n) for n in ("n_P", "n_T", "n_YZ", "n_C", "n_Z"))
        a_us, a_u, a_zu, a_zus, a_w, a_yi, a_y = (S(n) for n in ("a_us", "a_u", "a_zu", "a_zus", "a_w", "a_yi", "a_y"))
        g_c1, g_r1, g_c2, g_s, g_sp, g_G, g_done = (S(n) for n in ("g_c1", "g_r1", "g_c2", "g_s", "g_sp", "g_G", "g_done"))
        m_gx, m_x1, m_st, m_mv, m_ve, m_rs, m_xc, m_xn, m_hi, m_lo, m_xr = (S("m_" + n) for n in ("gx", "x1", "st", "mv", "ve", "rs", "xc", "xn", "hi", "lo", "xr"))
        m_X, m_xs, m_L, m_route, m_C, m_cs, m_cb, m_z, m_act, m_sc, m_l2, m_y, m_yT, m_yo, m_res = (
            S("m_" + n) for n in ("X", "xs", "L", "route", "C", "cs", "cb", "z", "act", "sc", "l2", "y", "yT", "yo", "res"))
        c_st, c_mv, c_ve, c_rs, c_xc, c_xn, c_hi, c_lo, c_X, c_xp, c_cv, c_cvs, c_bk, c_r2 = (
            S("c_" + n) for n in ("st", "mv", "ve", "rs", "xc", "xn", "hi", "lo", "X", "xp", "cv", "cvs", "bk", "r2"))
        d_X, d_xs, d_acc = S("d_X"), S("d_xs"), S("d_acc")
        r_log = S("r_log")
        r_pe, r_dve, r_act, r_add = S("r_pe"), S("r_dve"), S("r_act"), S("r_add")
        r_spread, r_ws, r_wa, r_warm = S("r_spread"), S("r_ws"), S("r_wa"), S("r_warm")
        f_z1, f_h1, f_z2, f_h2, f_l3, f_y, f_yT, f_yo, f_res = (S("f_" + n) for n in ("z1", "h1", "z2", "h2", "l3", "y", "yT", "yo", "res"))
        stored = S("stored")
        a_sqj, m_tanh, m_chl, m_gx0 = S("a_sqj"), S("m_tanh"), S("m_chl"), S("m_gx0")

        x_dram = a["x"].rearrange("b h w c -> (b h w c)").rearrange("(i p n) -> p i n", p=P, n=T * C)
        o_dram = out.rearrange("b h w c -> (b h w c)").rearrange("(i p n) -> p i n", p=P, n=T * C)

        def blk(t, b):
            return t[:, bass.ds(2 * b, 2), :].rearrange("p i (t c) -> p (i t) c", c=C)

        def slots(g):
            return slice(0 if g < NB else T2, T2 if g < LAG else 2 * T2)

        def halves(j):
            return slice(C * j, C * (j + 1))

        def on_diag(t, gr, j):
            return t[halves(j), GP * gr:GP * (gr + 1), halves(j)]

        block = ctx.enter_context(nc.Block())

        @block.sync
        def _(sp):
            for g in range(NG):
                sp.dma_start(x[:, GP * g:GP * (g + 1), :], x_dram[:, GP * g:GP * (g + 1), :]).then_inc(x_in[g], 16)
            sp.dma_start(gw1[:, :], a["L0_conv_w1"][1, 1]).then_inc(w_gate, 16)
            sp.dma_start(gw2[:, :], a["L0_conv_w2"][1, 1]).then_inc(w_gate, 16)
            sp.wait_ge(zeroed, 3)
            for name in VECS:
                sp.dma_start(vec_rows[ROW[name]:ROW[name] + KP, :],
                             a[name].rearrange("(k two) h -> k (two h)", two=2)).then_inc(w_vec, 16)
            for half in range(2):
                s = slice(C * half, C * (half + 1))
                sp.dma_start(vec_rows[ROW_GB1:ROW_GB1 + 1, s], a["L0_conv_b1"].rearrange("(a c) -> a c", a=1)).then_inc(w_vec, 16)
                sp.dma_start(vec_rows[ROW_GB2:ROW_GB2 + 1, s], a["L0_conv_b2"].rearrange("(a c) -> a c", a=1)).then_inc(w_vec, 16)
                sp.dma_start(vec_rows[ROW_ROUTER:NROWS, s], a["L0_ffn_router_w"]).then_inc(w_vec, 16)
            sp.dma_start(vec_rows[ROW_BC:ROW_BC + 1, 0:C], a["L1_conv_bc"].rearrange("(a c) -> a c", a=1)).then_inc(w_vec, 16)
            for half in range(2):
                s = slice(C * half, C * (half + 1))
                sp.dma_start(w1f[s, :].rearrange("p (e h) -> p e h", e=E), a["L0_ffn_w1"].rearrange("e c h -> c e h")).then_inc(w_moe, 16)
                sp.dma_start(b2rows[E * half:E * (half + 1), :], a["L0_ffn_b2"]).then_inc(w_moe, 16)
                sp.dma_start(w2[s, :, :], a["L0_ffn_w2"].rearrange("(k two) h c -> two h k c", two=2)[half]).then_inc(w_moe, 16)
                sp.dma_start(wd[s, :, :], a["L1_conv_Wd"].rearrange("(k two) c e -> two c k e", two=2)[half]).then_inc(w_conv, 16)
            sp.dma_start(wc[:, :, :], a["L1_conv_Wc"].rearrange("o (d e) -> o d e", d=8)).then_inc(w_conv, 16)
            for half in range(2):
                s = slice(C * half, C * (half + 1))
                sp.dma_start(f1f[s, :].rearrange("p (e h) -> p e h", e=E), a["L1_ffn_W1"].rearrange("e c h -> c e h")).then_inc(w_ffn, 16)
                sp.dma_start(f2[s, :, s], a["L1_ffn_W2"].rearrange("(k two) h o -> two h k o", two=2)[half]).then_inc(w_ffn, 16)
                sp.dma_start(fo[s, :, :], a["L1_ffn_Wo"].rearrange("(k two) h c -> two h k c", two=2)[half]).then_inc(w_ffn, 16)
            for part in range(2):
                sp.dma_start(bo[E * part:E * (part + 1), :], a["L1_ffn_bo"]).then_inc(w_ffn, 16)
            sp.dma_start(wr[:, :], a["L1_ffn_Wr"]).then_inc(w_ffn, 16)
            sp.dma_start(br[:, :], rep(a["L1_ffn_br"].rearrange("(a e) -> a e", a=1), 0, P)).then_inc(w_ffn, 16)
            for b in range(NB):
                for q in range(2):
                    sp.wait_ge(f_res, 2 * b + q + 1)
                    sp.dma_start(o_dram[:, 2 * b + q:2 * b + q + 1, :], x[:, 2 * b + q:2 * b + q + 1, :]).then_inc(stored, 16)
            sp.wait_ge(stored, 16 * NP)
        R_FEAT, R_FEATT, R_LOG, R_MAX, R_SUB, R_SUM, R_REC, R_W, R_WH, R_WL, R_U16, R_CTAB = range(1, 13)

        W_GATE, W_VEC, W_MOE, W_CONV, W_FFN = 32, 16 * (len(VECS) + 7), 96, 48, 16 * 10

        @block.gpsimd
        def _(pool):
            g = nc.gpsimd
            g.memset(neg_half[:, :], -0.5).then_inc(consts, 1)
            g.memset(pos_half[:, :], 0.5).then_inc(consts, 1)
            g.memset(eps_vec[:, 0:T2], EPS_C).then_inc(consts, 1)
            g.memset(eps_vec[:, T2:2 * T2], EPS_T).then_inc(consts, 1)
            g.memset(vec_rows[:, :], 0.0).then_inc(zeroed, 1)
            g.memset(b2rows[:, :], 0.0).then_inc(zeroed, 1)
            g.memset(f2[:, :, :], 0.0).then_inc(zeroed, 1)
            g.memset(ident[:, :], 0.0).then_inc(consts, 1)
            g.memset(two_ident15[:, :], 0.0).then_inc(consts, 1)
            g.memset(two_ident[:, :], 0.0).then_inc(consts, 1)
            g.memset(half_mean[:, :], 0.0).then_inc(consts, 1)
            g.memset(sel_f[:, :, :], 0.0).then_inc(consts, 1)
            g.memset(same_img[:, :], 0.0).then_inc(consts, 1)
            for e in range(E):
                g.memset(rank[:, e:e + 1], float(E - e)).then_inc(consts, 1)
            pool.wait_ge(consts, 18)
            g.memset(same_img[0:C, 0:C], 1.0).then_inc(consts, 1)
            pool.wait_ge(consts, 19)
            g.memset(same_img[C:P, C:P], 1.0).then_inc(consts, 1)
            pool.wait_ge(consts, 20)

            def fill(tile, value, base, pattern):
                return g.affine_select(out=tile, in_=tile, compare_op=ALU.not_equal, fill=value, base=base,
                                       pattern=pattern, channel_multiplier=1)
            fill(ident[:, :], 1.0, 0, [[-1, P]]).then_inc(consts, 1)
            n = 21
            for tile, value, step in ((two_ident, 1.0, (0, -C)), (two_ident15, 1.5, (0, -C)), (half_mean, 1.0 / B, (0, -C, C))):
                for base in step:
                    pool.wait_ge(consts, n)
                    fill(tile[:, :], value, base, [[-1, tile.shape[1]]]).then_inc(consts, 1)
                    n += 1
            for base in (0, -E):
                pool.wait_ge(consts, n)
                fill(sel_f[:, :, :].rearrange("p k (u h) -> p k u h", u=2), 1.0, base, [[-2, KP], [-1, 2], [0, C]]).then_inc(consts, 1)
                n += 1

            pool.wait_ge(zeroed, 3)
            def tok_rstd(gr):
                pool.wait_ge(a_mv, gr + 1)
                wait(pool, a_rstd, gr)
                g.tensor_scalar(veps[:, :], mv2[:, gr % 2, :, 1], EPS_C, None, ALU.add).then_inc(a_veps, 1)
                pool.wait_ge(a_veps, gr + 1)
                wait(pool, a_xn, gr)
                g.tensor_tensor(rstd[:, :], veps[:, :], neg_half[:, :], ALU.pow).then_inc(a_rstd, 1)

            tok_rstd(0)
            for gr in range(NG):
                if gr + 1 < NG:
                    tok_rstd(gr + 1)
                pool.wait_ge(a_rmean, gr + 1)
                wait(pool, a_xT, 2 * (gr - 1))
                wait(pool, a_sqj, GP * (gr - 1))
                g.tensor_tensor(xcc[gr % 2][:, :, :], xn[:, GP * gr:GP * (gr + 1), :],
                                rep(rmean[:, gr % 2, :].rearrange("p (n o) -> p n o", o=1), 2, M), ALU.subtract).then_inc(a_xcc, 1)
            pool.wait_ge(a_trm, 1)
            g.tensor_tensor(root[:, :], trm[:, :], pos_half[:, :], ALU.pow).then_inc(a_root, 1)

            g.memset(xp[:, :, :, :].bitcast(F32), 0.0).then_inc(consts_v, 1)
            g.memset(chl[:, :, :, :].bitcast(F32), 0.0).then_inc(consts_v, 1)
            g.memset(fsum[:, :, :], 0.0).then_inc(consts_v, 1)
            pool.wait_ge(consts_v, 3)
            pool.wait_ge(cols_ready, 1)
            col = lambda name: cols[:, ROW[name]:ROW[name] + KP]
            for i, n in enumerate("12"):
                g.tensor_scalar(bn_t[:, 2 * i, :], col("L1_ffn_v" + n), EPS_BN, None, ALU.add).then_inc(bn_step, 1)
            for i in range(2):
                pool.wait_ge(bn_step, i + 1)
                g.tensor_tensor(bn_t[:, 2 * i + 1, :], bn_t[:, 2 * i, :], neg_half[:, 0:KP], ALU.pow).then_inc(bn_pow, 1)
            for i, (n, bn) in enumerate((("1", bn1), ("2", bn2))):
                pool.wait_ge(bn_pow, i + 1)
                k = 2 + 4 * i
                g.tensor_tensor(bn[:, 0, :], bn_t[:, 2 * i + 1, :], col("L1_ffn_g" + n), ALU.mult).then_inc(bn_step, 1)
                g.tensor_tensor(bn_t[:, 2 * i, :], col("L1_ffn_b" + n), col("L1_ffn_m" + n), ALU.subtract).then_inc(bn_step, 1)
                pool.wait_ge(bn_step, k + 2)
                g.tensor_tensor(bn_t[:, 2 * i + 1, :], bn_t[:, 2 * i, :], bn[:, 0, :], ALU.mult).then_inc(bn_step, 1)
                pool.wait_ge(bn_step, k + 3)
                g.tensor_tensor(bn[:, 1, :], bn_t[:, 2 * i + 1, :], col("L1_ffn_be" + n), ALU.add).then_inc(bn_step, 1)
            pool.wait_ge(bn_step, 10)
            g.tensor_scalar(bn2[:, 2, :], bn2[:, 1, :], -1.0, None, ALU.mult).then_inc(bn_step, 1)
            for i, (lo, src, high) in enumerate(((router[:, 1, :], cols[:, ROW_ROUTER:NROWS], router[:, 0, :]),
                                                 (w1s[:, 1, :], w1f[:, :], w1s[:, 0, :]),
                                                 (f1s[:, 1, :], f1f[:, :], f1s[:, 0, :]))):
                pool.wait_ge(w_hi, i + 1)
                g.tensor_tensor(lo, src, high.bitcast(F32), ALU.subtract).then_inc(w_lo, 1)

            def moe_x1(b):
                if b >= NB:
                    return
                pool.wait_ge(g_done, 1 if b < NB // 2 else 2)
                gx = blk(xn, b).rearrange("p (i t) c -> p i t c", t=T)
                gb = rep(gate[:, 2 * b:2 * b + 2, :].rearrange("p i (o c) -> p i o c", o=1), 2, T)
                g.tensor_tensor(gx, gx, gb, ALU.mult).then_inc(m_gx, 1)
                pool.wait_ge(m_gx, b)
                g.tensor_tensor(blk(x, b), blk(x, b), blk(xn, b), ALU.add).then_inc(m_x1, 1)

            def moe_rstd(b):
                if b >= NB:
                    return
                pool.wait_ge(m_mv, b + 1)
                wait(pool, m_rs, b)
                g.tensor_scalar(veps[:, 0:T2], mv[:, 0:T2, 1], EPS_T, None, ALU.add).then_inc(m_ve, 1)
                pool.wait_ge(m_ve, b + 1)
                wait(pool, m_xn, b)
                g.tensor_tensor(rstd[:, 0:T2], veps[:, 0:T2], neg_half[:, 0:T2], ALU.pow).then_inc(m_rs, 1)

            def moe_sub(b):
                if b >= NB:
                    return
                pool.wait_ge(m_xn, b)
                g.tensor_tensor(xc[:, :, :], blk(x, b), rep(mv[:, 0:T2, 0].rearrange("p (n o) -> p n o", o=1), 2, C),
                                ALU.subtract).then_inc(m_xc, 1)

            def moe_low(b):
                if b >= NB:
                    return
                pool.wait_ge(m_hi, b + 1)
                g.tensor_tensor(hl[:, :, 1, :], xnb[:, b % 2], hl[:, :, 0, :].bitcast(F32), ALU.subtract).then_inc(m_lo, 1)
                g.tensor_tensor(blk(x, b), blk(x, b), xnb[:, b % 2], ALU.add).then_inc(m_xr, 1)

            moe_x1(1)
            moe_rstd(0)
            moe_low(0)
            moe_rstd(1)
            moe_x1(2)
            moe_low(1)
            moe_rstd(2)
            moe_x1(3)
            for b in range(NB):
                moe_low(b + 2)
                moe_x1(b + 4)
                moe_rstd(b + 3)
                moe_sub(b + 3)

            def mix_rstd(g_):
                sl = slots(g_)
                pool.wait_ge(c_mv, g_ + 1)
                wait(pool, c_rs, g_)
                if g_ == 0:
                    pool.wait_ge(m_rs, NB)
                    pool.wait_ge(m_xn, NB)
                g.tensor_tensor(veps[:, sl], mv[:, sl, 1], eps_vec[:, sl], ALU.add).then_inc(c_ve, 1)
                pool.wait_ge(c_ve, g_ + 1)
                wait(pool, c_xn, g_)
                g.tensor_tensor(rstd[:, sl], veps[:, sl], neg_half[:, sl], ALU.pow).then_inc(c_rs, 1)

            def mix_low(g_):
                sl = slots(g_)
                pool.wait_ge(c_hi, g_ + 1)
                g.tensor_tensor(hlc[:, g_ % 2, sl, 1, :], xnc[:, g_ % 2, sl], hlc[:, g_ % 2, sl, 0, :].bitcast(F32),
                                ALU.subtract).then_inc(c_lo, 1)

            mix_rstd(0)
            mix_rstd(1)
            mix_low(0)
            for g_ in range(2, NM + 1):
                if g_ < NM:
                    mix_rstd(g_)
                mix_low(g_ - 1)
                if g_ - 1 >= LAG:
                    wait(pool, d_acc, g_ - 1 - LAG)
                    g.tensor_tensor(fsum[:, :, :], fsum[:, :, :], xnc[:, (g_ - 1) % 2, T2:2 * T2], ALU.add).then_inc(d_acc, 1)

            pool.wait_ge(r_dve, R_CTAB)
            for b in range(NB):
                ct = rep(ctab[:, :].rearrange("p (o n) -> p o n", o=1), 1, 2)
                g.tensor_tensor(x[:, 2 * b:2 * b + 2, :], x[:, 2 * b:2 * b + 2, :], ct, ALU.add).then_inc(r_add, 1)

        @block.vector
        def _(dve):
            v = nc.vector

            def token_stats(b, src, n, s_st, s_mv, free=None):
                for t in range(n):
                    last = v.bn_stats(stats[:, t, :], src(t))
                last.then_inc(s_st, 1)
                dve.wait_ge(s_st, b + 1)
                for t in range(n):
                    last = v.bn_aggr(mv[:, t, :], stats[:, t, :])
                last.then_inc(s_mv, 1)

            def over(col, n, c=C):
                return rep(col.rearrange("p (n o) -> p n o", o=1), 2, c)

            v.memset(Zd[:, :, :], 0.0).then_inc(diag_zero, 1)
            v.memset(Td[:, :, :], 0.0).then_inc(diag_zero, 1)
            v.memset(z_own[:, :, :], 0.0).then_inc(diag_zero, 1)
            v.memset(b2sel[:, :, :, :], 0.0).then_inc(diag_zero, 1)

            def tok_stats(gr):
                dve.wait_ge(x_in[gr], 16)
                xg = x[:, GP * gr:GP * (gr + 1), :].rearrange("p i (t c) -> p (i t) c", c=C)
                wait(dve, a_mv, gr)
                for t in range(16):
                    last = v.bn_stats(stats[:, t, :], xg[:, t, :])
                last.then_inc(a_stats, 1)
                dve.wait_ge(a_stats, gr + 1)
                wait(dve, a_veps, gr - 1)
                wait(dve, a_xc, gr - 1)
                for t in range(16):
                    last = v.bn_aggr(mv2[:, gr % 2, t, :], stats[:, t, :])
                last.then_inc(a_mv, 1)

            def tok_sub(gr):
                xg = x[:, GP * gr:GP * (gr + 1), :].rearrange("p i (t c) -> p (i t) c", c=C)
                ng = xn[:, GP * gr:GP * (gr + 1), :].rearrange("p i (t c) -> p (i t) c", c=C)
                dve.wait_ge(a_mv, gr + 1)
                v.tensor_tensor(ng, xg, over(mv2[:, gr % 2, :, 0], 16), ALU.subtract).then_inc(a_xc, 1)

            def tok_mult(gr):
                ng = xn[:, GP * gr:GP * (gr + 1), :].rearrange("p i (t c) -> p (i t) c", c=C)
                dve.wait_ge(a_xc, gr + 1)
                dve.wait_ge(a_rstd, gr + 1)
                v.tensor_tensor(ng, ng, over(rstd[:, :], 16), ALU.mult).then_inc(a_xn, 1)
                dve.wait_ge(a_xn, gr + 1)
                wait(dve, a_rmean, gr)
                v.tensor_reduce(rsum[:, :], xn[:, GP * gr:GP * (gr + 1), :], AX.X, ALU.add).then_inc(a_rsum, 1)
                dve.wait_ge(a_rsum, gr + 1)
                wait(dve, a_xcc, gr - 1)
                v.tensor_scalar(rmean[:, gr % 2, :], rsum[:, :], 1.0 / M, None, ALU.mult).then_inc(a_rmean, 1)

            def cov(gr):
                dve.wait_ge(a_trace, gr + 1)
                gs = slice(GP * gr, GP * (gr + 1))
                v.reciprocal(rtrace[:, gs], bank[6][:, gs]).then_inc(a_rtr, 1)
                v.tensor_scalar(trm[:, gs], bank[6][:, gs], 1.0 / M, None, ALU.mult).then_inc(a_trm if gr == NG - 1 else a_rtr, 1)
                dve.wait_ge(a_rtr, 2 * gr + 1)
                dve.wait_ge(a_gram, gr + 1)
                for j in range(2):
                    gram = bank[gr % 2][halves(j), :].rearrange("p (i n) -> p i n", n=P)[:, :, halves(j)]
                    last = v.tensor_tensor(Ac[halves(j), gs, :], gram, over(rtrace[halves(j), gs], GP), ALU.mult)
                last.then_inc(a_A, 1)
                dve.wait_ge(a_A, gr + 1)
                v.scalar_tensor_tensor(out=YZ[:, gs, 1, :], in0=Ac[:, gs, :], scalar=-0.5, in1=rep(two_ident15[:, :].rearrange("p (o n) -> p o n", o=1), 1, GP),
                                       op0=ALU.mult, op1=ALU.add).then_inc(a_Z0, 1)

            tok_stats(0)
            tok_sub(0)
            tok_stats(1)
            tok_mult(0)
            tok_sub(1)
            tok_stats(2)
            tok_mult(1)
            tok_sub(2)
            cov(0)
            tok_stats(3)
            tok_mult(2)
            tok_sub(3)
            cov(1)
            dve.wait_ge(vecs_ready, 1)
            v.tensor_copy(cols[:, :], bank[7][:, 0:NROWS]).then_inc(cols_ready, 1)
            tok_mult(3)
            dve.wait_ge(cols_ready, 1)
            v.tensor_scalar(half_gb2[:, :], cols[0:C, ROW_GB2:ROW_GB2 + 1], 0.5, None, ALU.mult).then_inc(cols_ready, 1)
            cov(2)
            cov(3)
            def diagonals(n):
                gr = n % NG
                dve.wait_ge(n_C, n + 1)
                for j in range(2):
                    last = v.tensor_copy(on_diag(Zd, gr, j), YZ[halves(j), GP * gr:GP * (gr + 1), 1, :])
                last.then_inc(n_Z, 1)

            def row_sums(gr):
                gs = slice(GP * gr, GP * (gr + 1))
                dve.wait_ge(n_C, NG * (ROUNDS - 1) + gr + 1)
                v.tensor_reduce(u_sum[:, gs], YZ[:, gs, 0, :], AX.X, ALU.add).then_inc(a_us, 1)
                dve.wait_ge(a_us, gr + 1)
                own = rep(same_img[:, 0:P:C].rearrange("p (o n) -> p o n", o=1), 1, GP)
                v.tensor_tensor(u_own[:, gs, :], over(u_sum[:, gs], GP, 2), own, ALU.mult).then_inc(a_u, 1)

            dve.wait_ge(diag_zero, 4)
            for n in range(NG * ROUNDS):
                gr = n % NG
                dve.wait_ge(n_P, n + 1)
                for j in range(2):
                    p = bank[gr % 2][halves(j), 0:GP * C].rearrange("p (i c) -> p i c", c=C)
                    i15 = rep(two_ident15[halves(j), :].rearrange("p (o n) -> p o n", o=1), 1, GP)
                    last = v.scalar_tensor_tensor(out=on_diag(Td, gr, j), in0=p, scalar=-0.5, in1=i15, op0=ALU.mult, op1=ALU.add)
                last.then_inc(n_T, 1)
                if 1 <= n <= NG * (ROUNDS - 1):
                    diagonals(n - 1)
                if n > NG * (ROUNDS - 1):
                    row_sums(gr - 1)
                if n == 7:
                    dve.wait_ge(bn_step, 11)
                    for half in range(2):
                        flat = b2sel[halves(half), :, :, :].rearrange("p k s e -> p (k s e)")
                        step = 2 * E + 2
                        for part in range(2):
                            first = E * part + half
                            v.tensor_copy(flat[:, first:first + (KP - 1) * step + 1:step], bn2[halves(half), 1, :]).then_inc(b2_sel, 1)
                if n == 8:
                    dve.wait_ge(s2_spread, 1)
                    dve.wait_ge(w_ffn, W_FFN)
                    v.tensor_tensor(f2[:, :, :], f2[:, :, :], bank[6][:, :].rearrange("p (k n) -> p k n", n=P), ALU.mult).then_inc(f2_scaled, 1)
                if n == 10:
                    dve.wait_ge(conv_vs, 1)
                    v8 = bank[7][:, :].rearrange("p (d o) -> p d o", d=8)
                    v.tensor_tensor(vconv[:, :, 1, :], v8, vconv[:, :, 0, :].bitcast(F32), ALU.subtract).then_inc(conv_vs, 1)
            row_sums(NG - 1)
            for j in range(2):
                v.tensor_scalar(yv[:, 1, :, j], u_sum[halves(j), :], 1.5 / C, None, ALU.mult).then_inc(a_yi, 1)
            dve.wait_ge(a_root, 1)
            for j in range(2):
                v.tensor_copy(yv[:, 0, :, j], root[halves(j), :]).then_inc(a_yi, 1)
            dve.wait_ge(a_zu, 1)
            for j in range(2):
                v.tensor_copy(z_own[halves(j), :, j], bank[4][0:C, j:2 * NP:2]).then_inc(a_zus, 1)
            dve.wait_ge(a_w, 1)
            dve.wait_ge(a_yi, 4)
            yf = yv[:, :, :, :].rearrange("p k i j -> p k (i j)")
            v.scalar_tensor_tensor(out=yf[:, 2, :], in0=bank[5][0:C, 0:2 * NP], scalar=-0.5 / C, in1=yf[:, 1, :],
                                   op0=ALU.mult, op1=ALU.add).then_inc(a_y, 1)
            dve.wait_ge(a_y, 1)
            v.tensor_tensor(yf[:, 3, :], yf[:, 2, :], yf[:, 0, :], ALU.mult).then_inc(a_y, 1)
            dve.wait_ge(g_s, 1)
            for j in range(2):
                v.tensor_scalar(gsig[halves(j), :], g2[:, :, j], 0.5, 0.5, ALU.mult, ALU.add).then_inc(g_sp, 1)
            dve.wait_ge(g_sp, 2)
            for i in range(2):
                h8 = slice(8 * i, 8 * (i + 1))
                v.tensor_tensor(gspread[:, h8, :], over(gsig[:, h8], 8), rep(two_ident[:, :].rearrange("p (o c) -> p o c", o=1), 1, 8),
                                ALU.mult).then_inc(g_sp, 1)

            def moe_stats(b):
                if b:
                    dve.wait_ge(m_x1, b)
                    wait(dve, m_ve, b)
                    wait(dve, m_xc, b)
                src = blk(x, b)
                token_stats(b, lambda t: src[:, t, :], T2, m_st, m_mv)

            def moe_sub(b):
                dve.wait_ge(m_mv, b + 1)
                wait(dve, m_xn, b)
                v.tensor_tensor(xc[:, :, :], blk(x, b), over(mv[:, 0:T2, 0], T2), ALU.subtract).then_inc(m_xc, 1)

            def moe_mult(b):
                u = b % 2
                dve.wait_ge(m_rs, b + 1)
                dve.wait_ge(m_xc, b + 1)
                wait(dve, m_xr, b - 1)
                wait(dve, m_lo, b - 1)
                wait(dve, m_hi, b - 1)
                v.tensor_tensor(xnb[:, u], xc[:, :, :], over(rstd[:, 0:T2], T2), ALU.mult).then_inc(m_xn, 1)

            ROUTE = 19

            def route(b, part):
                base = ROUTE * b
                mx = lambda i: m12[:, i, :]
                rk = rep(rank[:, :].rearrange("p (o e) -> p o e", o=1), 1, T2)
                TT = v.tensor_tensor

                def largest(values, m, onehot, n):
                    v.tensor_reduce(mx(m), values, AX.X, ALU.max).then_inc(m_route, 1)
                    dve.wait_ge(m_route, base + n + 1)
                    TT(onehot, values, over(mx(m), T2, E), ALU.is_equal).then_inc(m_route, 1)

                def first_of(onehot, n):
                    dve.wait_ge(m_route, base + n)
                    TT(onehot, onehot, rk, ALU.mult).then_inc(m_route, 1)
                    dve.wait_ge(m_route, base + n + 1)
                    v.tensor_reduce(mx(7), onehot, AX.X, ALU.max).then_inc(m_route, 1)
                    dve.wait_ge(m_route, base + n + 2)
                    TT(onehot, onehot, over(mx(7), T2, E), ALU.is_equal).then_inc(m_route, 1)

                if part == 0:
                    dve.wait_ge(m_L, 2 * b + 2)
                    for q in range(2):
                        lq = bank[6 + q][:, 0:T * 2 * E].rearrange("p (t s e) -> p t e s", t=T, s=2)
                        v.tensor_reduce(lg[:, T * q:T * (q + 1), :], lq, AX.X, ALU.add).then_inc(m_route, 1)
                    dve.wait_ge(m_route, base + 2)
                    largest(lg[:, :, :], 0, one1[:, :, :], 2)
                if part == 1:
                    first_of(one1[:, :, :], 4)
                if part == 2:
                    dve.wait_ge(m_route, base + 7)
                    v.scalar_tensor_tensor(out=tmp[:, :, :], in0=one1[:, :, :], scalar=-3.0e38, in1=lg[:, :, :],
                                           op0=ALU.mult, op1=ALU.add).then_inc(m_route, 1)
                    dve.wait_ge(m_route, base + 8)
                    largest(tmp[:, :, :], 1, one2[:, :, :], 8)
                if part == 3:
                    TT(mx(2), mx(1), mx(0), ALU.subtract).then_inc(m_route, 1)
                    first_of(one2[:, :, :], 11)
                if part == 4:
                    dve.wait_ge(m_tanh, b + 1)
                    v.tensor_scalar(mx(4), mx(3), 0.5, 0.5, ALU.mult, ALU.add).then_inc(m_route, 1)
                    v.tensor_scalar(mx(5), mx(3), -0.5, 0.5, ALU.mult, ALU.add).then_inc(m_route, 1)
                    dve.wait_ge(m_route, base + 16)
                    TT(one1[:, :, :], one1[:, :, :], over(mx(5), T2, E), ALU.mult).then_inc(m_route, 1)
                    TT(one2[:, :, :], one2[:, :, :], over(mx(4), T2, E), ALU.mult).then_inc(m_route, 1)
                    dve.wait_ge(m_route, base + 18)
                    wait(dve, m_chl, 2 * b)
                    TT(cw[:, :, :], one1[:, :, :], one2[:, :, :], ALU.add).then_inc(m_route, 1)
                    dve.wait_ge(m_route, base + 19)
                    wait(dve, m_C, 2 * b)
                    v.tensor_copy(chl[:, :, 0, :], cw[:, :, :]).then_inc(m_chl, 1)
                    dve.wait_ge(m_chl, 2 * b + 1)
                    v.tensor_tensor(chl[:, :, 1, :], cw[:, :, :], chl[:, :, 0, :].bitcast(F32), ALU.subtract).then_inc(m_chl, 1)

            def moe_add(b, q):
                dve.wait_ge(m_yo, 2 * b + q + 1)
                dve.wait_ge(m_xr, b + 1)
                i = 2 * b + q
                v.tensor_tensor(x[:, i, :], x[:, i, :], bank[4 + q][:, 2 * P:4 * P], ALU.add).then_inc(m_res, 1)

            def moe_scale(b, n):
                N = 8 * b + n
                dve.wait_ge(m_cb, N + 1)
                dve.wait_ge(m_act, N + 1)
                wait(dve, m_l2, N - 1)
                v.tensor_tensor(scaled[:, n % 2, :], act[:, n % 2, :], bank[2 + n % 2][:, :], ALU.mult).then_inc(m_sc, 1)

            def mix_parts(g_):
                parts = []
                if g_ < NB:
                    parts.append((g_, 0))
                if g_ >= LAG:
                    parts.append((g_ - LAG, T2))
                return parts

            def mix_stats(g_):
                if g_ == 0:
                    dve.wait_ge(m_ve, NB)
                    dve.wait_ge(m_xc, NB)
                wait(dve, c_ve, g_)
                if g_ < NB:
                    dve.wait_ge(m_res, 2 * g_ + 2)
                if g_ >= LAG:
                    dve.wait_ge(c_r2, 2 * (g_ - LAG) + 2)
                for b, s0 in mix_parts(g_):
                    src = blk(x, b)
                    for t in range(T2):
                        last = v.bn_stats(stats[:, s0 + t, :], src[:, t, :])
                last.then_inc(c_st, 1)
                dve.wait_ge(c_st, g_ + 1)
                wait(dve, c_xc, g_)
                for b, s0 in mix_parts(g_):
                    for t in range(T2):
                        last = v.bn_aggr(mv[:, s0 + t, :], stats[:, s0 + t, :])
                last.then_inc(c_mv, 1)

            def mix_sub(g_):
                dve.wait_ge(c_mv, g_ + 1)
                wait(dve, c_xn, g_)
                for b, s0 in mix_parts(g_):
                    last = v.tensor_tensor(xcn[:, s0:s0 + T2], blk(x, b), over(mv[:, s0:s0 + T2, 0], T2), ALU.subtract)
                last.then_inc(c_xc, 1)

            def mix_mult(g_):
                sl = slots(g_)
                dve.wait_ge(c_xc, g_ + 1)
                dve.wait_ge(c_rs, g_ + 1)
                wait(dve, c_lo, g_ - 1)
                wait(dve, c_hi, g_ - 1)
                wait(dve, d_acc, g_ - 1 - LAG)
                v.tensor_tensor(xnc[:, g_ % 2, sl], xcn[:, sl], over(rstd[:, sl], sl.stop - sl.start), ALU.mult).then_inc(c_xn, 1)

            def mix_add(b, q):
                i = 2 * b + q
                dve.wait_ge(c_bk, i + 1)
                v.tensor_tensor(x[:, i, :], x[:, i, :], bank[4 + q][:, 0:T * C], ALU.add).then_inc(c_r2, 1)

            dve.wait_ge(g_done, 1)
            gx = blk(xn, 0).rearrange("p (i t) c -> p i t c", t=T)
            gb = rep(gate[:, 0:2, :].rearrange("p i (o c) -> p i o c", o=1), 2, T)
            v.tensor_tensor(gx, gx, gb, ALU.mult).then_inc(m_gx0, 1)
            dve.wait_ge(m_gx0, 1)
            v.tensor_tensor(blk(x, 0), blk(x, 0), blk(xn, 0), ALU.add).then_inc(m_gx0, 1)
            dve.wait_ge(m_gx0, 2)
            moe_stats(0)
            moe_sub(0)
            moe_stats(1)
            moe_mult(0)
            moe_sub(1)
            moe_mult(1)
            for part in range(5):
                route(0, part)
            moe_stats(2)
            moe_sub(2)
            for b in range(NB):
                more, more2, more3 = b + 1 < NB, b + 2 < NB, b + 3 < NB
                if not more:
                    break
                moe_scale(b, 0)
                if b:
                    moe_add(b - 1, 0)
                moe_scale(b, 1)
                if more:
                    route(b + 1, 0)
                moe_scale(b, 2)
                if more2:
                    moe_mult(b + 2)
                if more:
                    route(b + 1, 1)
                moe_scale(b, 3)
                if more:
                    route(b + 1, 2)
                moe_scale(b, 4)
                if b:
                    moe_add(b - 1, 1)
                if more:
                    route(b + 1, 3)
                moe_scale(b, 5)
                if more:
                    route(b + 1, 4)
                moe_scale(b, 6)
                if more3:
                    moe_stats(b + 3)
                moe_scale(b, 7)
                if b == NB - 2:
                    mix_stats(0)
                    mix_sub(0)
            b = NB - 1
            moe_scale(b, 0)
            moe_add(b - 1, 0)
            moe_scale(b, 1)
            mix_mult(0)
            moe_scale(b, 2)
            mix_stats(1)
            moe_scale(b, 3)
            moe_add(b - 1, 1)
            mix_sub(1)
            moe_scale(b, 4)
            mix_mult(1)
            moe_scale(b, 5)
            mix_stats(2)
            moe_scale(b, 6)
            mix_sub(2)
            moe_scale(b, 7)
            moe_add(b, 0)
            moe_add(b, 1)

            for b in range(NM - 2):
                if b + 3 < NM:
                    mix_stats(b + 3)
                mix_mult(b + 2)
                if b + 3 < NM:
                    mix_sub(b + 3)
                if 0 <= b < NB:
                    mix_add(b, 0)
                    mix_add(b, 1)

            def rstep(n, ins):
                ins.then_inc(r_dve, 1)
            dve.wait_ge(r_pe, 2)
            rstep(R_FEAT, v.tensor_copy(feat[:, :, :].rearrange("p t c -> p (t c)"), bank[0][:, 0:T * C]))
            dve.wait_ge(r_pe, 3)
            rstep(R_FEATT, v.tensor_copy(featT[:, :], bank[1][0:C, :]))
            dve.wait_ge(r_log, 1)
            brb = rep(br[:, :].rearrange("p (o e) -> p o e", o=1), 1, T)
            rstep(R_LOG, v.tensor_tensor(fl[:, 0], bank[0][:, 0:T * E].rearrange("p (t e) -> p t e", t=T), brb, ALU.add))
            dve.wait_ge(r_dve, R_LOG)
            rstep(R_MAX, v.tensor_reduce(fm[:, 0, :], fl[:, 0], AX.X, ALU.max))
            dve.wait_ge(r_dve, R_MAX)
            rstep(R_SUB, v.tensor_tensor(fl[:, 1], fl[:, 0], over(fm[:, 0, :], T, E), ALU.subtract))
            dve.wait_ge(r_act, 1)
            rstep(R_SUM, v.tensor_reduce(fm[:, 1, :], fl[:, 2], AX.X, ALU.add))
            dve.wait_ge(r_dve, R_SUM)
            rstep(R_REC, v.reciprocal(fm[:, 2, :], fm[:, 1, :]))
            dve.wait_ge(r_dve, R_REC)
            rstep(R_W, v.tensor_tensor(fl[:, 3], fl[:, 2], over(fm[:, 2, :], T, E), ALU.mult))
            dve.wait_ge(r_dve, R_W)
            rstep(R_WH, v.tensor_copy(whl[:, :, 0, :], fl[:, 3]))
            dve.wait_ge(r_dve, R_WH)
            rstep(R_WL, v.tensor_tensor(whl[:, :, 1, :], fl[:, 3], whl[:, :, 0, :].bitcast(F32), ALU.subtract))
            rstep(R_U16, v.tensor_tensor(u16[:, :], bank[4][0:2 * E, 0:C], bo[:, :], ALU.add))
            dve.wait_ge(r_spread, 1)
            v.tensor_copy(wspread[:, 0, :], bank[0][:, :]).then_inc(r_ws, 1)

            def ffn_add(b, q):
                i = 2 * b + q
                dve.wait_ge(f_yo, i + 1)
                dve.wait_ge(r_add, b + 1)
                v.tensor_tensor(x[:, i, :], x[:, i, :], bank[4 + q][:, 2 * P:4 * P], ALU.add).then_inc(f_res, 1)

            for b in range(NB):
                for n in range(8):
                    N, k = 8 * b + n, n % KP
                    dve.wait_ge(f_z2, N + 1)
                    wait(dve, f_l3, N - 1)
                    if N in (1, 3):
                        dve.wait_ge(r_wa, (N + 1) // 2)
                    if N == 2:
                        dve.wait_ge(r_spread, 3)
                        v.tensor_copy(wspread[:, 2, :], bank[0][:, :]).then_inc(r_ws, 1)
                        dve.wait_ge(r_pe, 5)
                        rstep(R_CTAB, v.tensor_copy(ctab[:, :], bank[5][:, 0:T * C]))
                    if N in (0, 2):
                        dve.wait_ge(r_ws, N // 2 + 1)
                    v.scalar_tensor_tensor(out=scaled[:, n % 2, :], in0=bank[2 + n % 2][:, :], scalar=bn2[:, 2, k:k + 1],
                                           in1=wspread[:, k, :], op0=ALU.max, op1=ALU.mult).then_inc(f_h2, 1)
                    if n == 3 and b:
                        ffn_add(b - 1, 1)
                ffn_add(b, 0)
            ffn_add(NB - 1, 1)

        @block.scalar
        def _(act_e):
            s = nc.scalar
            def z_diagonals(gr):
                act_e.wait_ge(a_Z0, gr + 1)
                act_e.wait_ge(diag_zero, 1)
                for j in range(2):
                    last = s.activation(on_diag(Zd, gr, j), YZ[halves(j), GP * gr:GP * (gr + 1), 1, :], ACT.Copy)
                last.then_inc(a_Zd, 1)

            def first_y(gr):
                act_e.wait_ge(a_P0, gr + 1)
                s.activation(YZ[:, GP * gr:GP * (gr + 1), 0, :], bank[2 + gr % 2][:, 0:GP * C].rearrange("p (i c) -> p i c", c=C),
                             ACT.Copy).then_inc(a_Y0, 1)

            for gr in range(NG):
                act_e.wait_ge(a_xcc, gr + 1)
                for i in range(GP):
                    if gr or i:
                        act_e.wait_ge(a_sqj, GP * gr + i)
                    last = s.activation(sqj[:, :], xcc[gr % 2][:, i, :], ACT.Square, accum_out=sumsq[:, GP * gr + i:GP * gr + i + 1])
                    last.then_inc(a_sqj, 1)
                for c in range(2):
                    act_e.wait_ge(a_xT, 2 * gr + c + 1)
                    wait(act_e, a_gram, gr)
                    s.activation(xT[:, c, :], bank[4 + c][:, :], ACT.Copy).then_inc(a_xTs, 1)
                if gr:
                    z_diagonals(gr - 1)
                    first_y(gr - 1)
            z_diagonals(NG - 1)
            first_y(NG - 1)
            for n in range(NG * ROUNDS):
                gr = n % NG
                act_e.wait_ge(n_YZ, n + 1)
                s.activation(YZ[:, GP * gr:GP * (gr + 1), :, :].rearrange("p i s c -> p (i s c)"), bank[2 + gr % 2][:, :],
                             ACT.Copy).then_inc(n_C, 1)
                if n == 0:
                    act_e.wait_ge(cols_ready, 1)
                    act_e.wait_ge(w_moe, W_MOE)
                    act_e.wait_ge(w_ffn, W_FFN)
                    s.activation(router[:, 0, :], cols[:, ROW_ROUTER:NROWS], ACT.Copy).then_inc(w_hi, 1)
                if n == 1:
                    s.activation(w1s[:, 0, :], w1f[:, :], ACT.Copy).then_inc(w_hi, 1)
                if n == 2:
                    s.activation(f1s[:, 0, :], f1f[:, :], ACT.Copy).then_inc(w_hi, 1)
                if n == 3:
                    act_e.wait_ge(consts, 30)
                    s.activation(sel[:, :, :], sel_f[:, :, :], ACT.Copy).then_inc(w_hi, 1)
                if n in (4, 5):
                    act_e.wait_ge(conv_wT, 1)
                    s.activation(wdT[:, :, n - 4, :], bank[4][0:C, :].rearrange("p (d c) -> p d c", d=8), ACT.Copy).then_inc(conv_wTs, 1)
                if n == 6:
                    s.activation(wcT[:, :, :].rearrange("p d c -> p (d c)"), bank[5][0:C, :], ACT.Copy).then_inc(conv_wTs, 1)
                if n == 9:
                    act_e.wait_ge(conv_v, 1)
                    s.activation(vconv[:, :, 0, :], bank[7][:, :].rearrange("p (d o) -> p d o", d=8), ACT.Copy).then_inc(conv_vs, 1)
            act_e.wait_ge(g_c1, 1)
            act_e.wait_ge(cols_ready, 2)
            s.activation(g1[:, :], bank[6][0:C, 0:2 * NP], ACT.Relu, bias=cols[0:C, ROW_GB1:ROW_GB1 + 1]).then_inc(g_r1, 1)
            act_e.wait_ge(g_c2, 1)
            s.activation(g2[:, :, :].rearrange("p i j -> p (i j)"), bank[7][0:C, 0:2 * NP], ACT.Tanh, scale=0.5, bias=half_gb2[:, 0:1]).then_inc(g_s, 1)
            for i in range(2):
                act_e.wait_ge(g_G, i + 1)
                s.activation(gate[:, 8 * i:8 * (i + 1), :].rearrange("p i c -> p (i c)"), bank[i][:, :], ACT.Copy).then_inc(g_done, 1)

            def evac_x(b, q):
                act_e.wait_ge(m_X, 2 * b + q + 1)
                s.activation(xs[:, b % 2, CH * q:CH * (q + 1)], bank[6 + q][:, :], ACT.Copy).then_inc(m_xs, 1)

            def hi(b, u, s_xn, s_hi, free):
                act_e.wait_ge(s_xn, b + 1)
                for s_used, k in free:
                    wait(act_e, s_used, k)
                s.activation(hl[:, :, 0, :], xnb[:, u], ACT.Copy).then_inc(s_hi, 1)

            def tanh(b):
                act_e.wait_ge(m_route, 19 * b + 12)
                s.activation(m12[:, 3, :], m12[:, 2, :], ACT.Tanh, scale=0.5).then_inc(m_tanh, 1)

            def evac_c(b, q):
                act_e.wait_ge(m_C, 2 * b + q + 1)
                wait(act_e, m_cb, 8 * (b - 1) + KP * (q + 1))
                wait(act_e, m_l2, 8 * (b - 1) + KP * q + 1)
                s.activation(cs[:, CH * q:CH * (q + 1)], bank[6 + q][:, :], ACT.Copy).then_inc(m_cs, 1)

            def evac_y(b, q):
                act_e.wait_ge(m_l2, KP * (2 * b + q + 1))
                wait(act_e, m_yo, 2 * b + q - 1)
                s.activation(yTs[:, q, :], bank[4 + q][:, 0:2 * P], ACT.Copy).then_inc(m_yT, 1)

            def gelu(b, n):
                N = 8 * b + n
                act_e.wait_ge(m_z, N + 1)
                wait(act_e, m_sc, N - 1)
                s.activation(act[:, n % 2, :], bank[n % 2][:, :], ACT.Gelu, bias=cols[:, n % KP:n % KP + 1]).then_inc(m_act, 1)

            def mix_high(g_):
                sl = slots(g_)
                act_e.wait_ge(c_xn, g_ + 1)
                if g_ == 0:
                    act_e.wait_ge(m_x1, NB - 1)
                wait(act_e, c_X, 2 * min(g_ - 1, NB))
                wait(act_e, d_X, 2 * (g_ - 1 - LAG))
                s.activation(hlc[:, g_ % 2, sl, 0, :], xnc[:, g_ % 2, sl], ACT.Copy).then_inc(c_hi, 1)

            def mix_pad(b, q):
                i = 2 * b + q
                act_e.wait_ge(c_X, i + 1)
                wait(act_e, c_cv, i - 1)
                src = bank[6 + q][:, :].rearrange("p (t i r w) -> p i r w t", t=T, i=2, r=H)
                for j in range(2):
                    dst = xp[:, 2 * q + j, 1:H + 1, 1:W + 1].rearrange("p r (w t) -> p r w t", t=T)
                    last = s.activation(dst, src[:, j], ACT.Copy)
                last.then_inc(c_xp, 1)

            def mix_bias(b, q):
                i = 2 * b + q
                act_e.wait_ge(c_cv, i + 1)
                wait(act_e, c_bk, i - 1)
                s.activation(cvs[:, q, :], bank[q][:, :], ACT.Identity, bias=cols[:, ROW_BC:ROW_BC + 1]).then_inc(c_cvs, 1)

            def ffn_in(b, q):
                act_e.wait_ge(d_X, 2 * b + q + 1)
                s.activation(xs_ffn[:, b, CH * q:CH * (q + 1)], bank[2 + q][:, :], ACT.Copy).then_inc(d_xs, 1)

            hi(0, 0, m_xn, m_hi, [])
            evac_x(0, 0)
            evac_x(0, 1)
            hi(1, 1, m_xn, m_hi, [(m_X, 2)])
            tanh(0)
            evac_c(0, 0)
            evac_c(0, 1)
            for b in range(NB):
                more, more2 = b + 1 < NB, b + 2 < NB
                gelu(b, 0)
                if more:
                    evac_x(b + 1, 0)
                    evac_x(b + 1, 1)
                gelu(b, 1)
                gelu(b, 2)
                if b:
                    evac_y(b - 1, 1)
                gelu(b, 3)
                if more2:
                    hi(b + 2, b % 2, m_xn, m_hi, [(m_X, 2 * b + 4)])
                if not more:
                    mix_high(0)
                gelu(b, 4)
                if more:
                    tanh(b + 1)
                gelu(b, 5)
                gelu(b, 6)
                evac_y(b, 0)
                gelu(b, 7)
                if more:
                    evac_c(b + 1, 0)
                    evac_c(b + 1, 1)
            act_e.wait_ge(consts_v, 1)
            mix_pad(0, 0)
            mix_high(1)
            evac_y(NB - 1, 1)
            mix_pad(0, 1)

            for b in range(NM - 1):
                if b + 1 < NB:
                    mix_pad(b + 1, 0)
                if 0 <= b < NB:
                    mix_bias(b, 0)
                if b + 2 < NM:
                    mix_high(b + 2)
                if b + 1 < NB:
                    mix_pad(b + 1, 1)
                if 0 <= b < NB:
                    mix_bias(b, 1)
                if b + 1 >= LAG:
                    ffn_in(b + 1 - LAG, 0)
                    ffn_in(b + 1 - LAG, 1)

            def evac_f(b, q):
                act_e.wait_ge(f_l3, KP * (2 * b + q + 1))
                wait(act_e, f_yo, 2 * b + q - 1)
                s.activation(yTs[:, q, :], bank[4 + q][:, 0:2 * P], ACT.Copy).then_inc(f_yT, 1)

            def first_relu(N):
                n, k = N % 8, N % KP
                act_e.wait_ge(f_z1, N + 1)
                wait(act_e, f_z2, N - 1)
                if N == 0:
                    act_e.wait_ge(bn_step, 11)
                s.activation(act[:, n % 2, :], bank[6 + n % 2][:, :], ACT.Relu, scale=bn1[:, 0, k:k + 1],
                             bias=bn1[:, 1, k:k + 1]).then_inc(f_h1, 1)

            s.activation(fm[:, 3, :], neg_half[:, 0:T], ACT.Exp).then_inc(r_warm, 1)
            first_relu(0)
            first_relu(1)
            act_e.wait_ge(r_dve, R_SUB)
            s.activation(fl[:, 2], fl[:, 1], ACT.Exp).then_inc(r_act, 1)
            act_e.wait_ge(r_pe, 4)
            s.activation(wT[:, :], bank[1][0:2 * E, :], ACT.Copy).then_inc(r_act, 1)
            for i in range(2):
                act_e.wait_ge(r_spread, 2 * i + 2)
                s.activation(wspread[:, 2 * i + 1, :], bank[1][:, :], ACT.Copy).then_inc(r_wa, 1)
            for N in range(2, 8 * NB):
                first_relu(N)
                if N % 8 == 2 and N > 8:
                    evac_f(N // 8 - 1, 1)
                if N % 8 == 6:
                    evac_f(N // 8, 0)
            evac_f(NB - 1, 1)

        @block.tensor
        def _(pe):
            t = nc.tensor
            def first_product(gr):
                pe.wait_ge(a_Zd, gr + 1)
                wait(pe, a_Y0, gr - 1)
                for i in range(GP):
                    k = GP * gr + i
                    last = t.matmul(bank[2 + gr % 2][:, C * i:C * (i + 1)], Zd[:, k, :], Ac[:, k, :], start=True, stop=True)
                last.then_inc(a_P0, 1)

            pe.wait_ge(consts, 30)
            for gr in range(NG):
                pe.wait_ge(a_xcc, gr + 1)
                wait(pe, a_xTs, 2 * gr)
                for c in range(2):
                    for i in range(GP):
                        last = t.transpose(bank[4 + c][:, P * i:P * (i + 1)], xcc[gr % 2][:, i, P * c:P * (c + 1)], ident[:, :])
                    last.then_inc(a_xT, 1)
                pe.wait_ge(a_sqj, GP * (gr + 1))
                wait(pe, a_rtr, 2 * gr)
                t.matmul(bank[6][:, GP * gr:GP * (gr + 1)], same_img[:, :], sumsq[:, GP * gr:GP * (gr + 1)],
                         start=True, stop=True).then_inc(a_trace, 1)
                pe.wait_ge(a_xTs, 2 * gr + 2)
                wait(pe, a_A, gr - 1)
                for i in range(GP):
                    cs_ = slice(P * i, P * (i + 1))
                    for c in range(2):
                        last = t.matmul(bank[gr % 2][:, cs_], xT[:, c, cs_], xT[:, c, cs_], start=(c == 0), stop=(c == 1))
                last.then_inc(a_gram, 1)
                if gr:
                    first_product(gr - 1)
                if gr == 1:
                    pe.wait_ge(w_vec, W_VEC)
                    t.transpose(bank[7][:, 0:NROWS], vec_rows[:, :], ident[0:NROWS, 0:NROWS]).then_inc(vecs_ready, 1)
            first_product(NG - 1)

            def prod_p(n):
                gr = n % NG
                if n < NG:
                    pe.wait_ge(a_Y0, gr + 1)
                    pe.wait_ge(a_A, NG)
                wait(pe, n_C, n - NG + 1)
                wait(pe, n_Z, n - NG + 1)
                wait(pe, n_T, n - 1)
                for i in range(GP):
                    k = GP * gr + i
                    last = t.matmul(bank[gr % 2][:, C * i:C * (i + 1)], Zd[:, k, :], YZ[:, k, 0, :], start=True, stop=True)
                last.then_inc(n_P, 1)

            def prod_yz(n):
                gr = n % NG
                pe.wait_ge(n_T, n + 1)
                wait(pe, n_C, n - 1)
                if n == 0:
                    pe.wait_ge(a_Y0, NG)
                for i in range(GP):
                    k = GP * gr + i
                    last = t.matmul(bank[2 + gr % 2][:, P * i:P * (i + 1)], Td[:, k, :],
                                    YZ[:, k, :, :].rearrange("p s c -> p (s c)"), start=True, stop=True)
                last.then_inc(n_YZ, 1)

            prod_p(0)
            prod_p(1)
            for n in range(NG * ROUNDS):
                prod_yz(n)
                if n + 2 < NG * ROUNDS:
                    prod_p(n + 2)
                if n == 2:
                    pe.wait_ge(w_conv, W_CONV)
                    pe.wait_ge(a_xTs, 2 * NG)
                    for k in range(4):
                        t.transpose(bank[4][0:C, P * k:P * (k + 1)], wd[:, k, :], ident[:, :])
                    for d in range(8):
                        last = t.transpose(bank[5][0:C, C * d:C * (d + 1)], wc[:, d, :], ident[0:C, 0:C])
                    last.then_inc(conv_wT, 1)
                if n == 6:
                    pe.wait_ge(bn_step, 10)
                    pe.wait_ge(a_trm, 1)
                    for k in range(KP):
                        last = t.transpose(bank[6][:, P * k:P * (k + 1)], rep(bn2[:, 0, k:k + 1], 1, P), ident[:, :])
                    last.then_inc(s2_spread, 1)
                if n == 7:
                    pe.wait_ge(conv_wTs, 3)
                    pe.wait_ge(cols_ready, 1)
                    for d in range(8):
                        last = t.matmul(bank[7][:, C * d:C * (d + 1)],
                                        wdT[:, d, :, :].rearrange("p o c -> p (o c)"),
                                        wcT[:, d, :], start=True, stop=True)
                    last.then_inc(conv_v, 1)
            for i in range(NP):
                if i % GP == 0:
                    pe.wait_ge(a_u, i // GP + 1)
                last = t.matmul(bank[4][0:C, 2 * i:2 * i + 2], YZ[:, i, 1, :], u_own[:, i, :], start=True, stop=True)
            last.then_inc(a_zu, 1)
            pe.wait_ge(a_zus, 2)
            for i in range(NP):
                last = t.matmul(bank[5][0:C, 2 * i:2 * i + 2], YZ[:, i, 0, :], z_own[:, i, :], start=True, stop=True)
            last.then_inc(a_w, 1)
            pe.wait_ge(a_y, 2)
            pe.wait_ge(w_gate, W_GATE)
            pe.wait_ge(f2_scaled, 1)
            t.matmul(bank[6][0:C, 0:2 * NP], gw1[:, :], yv[:, 3, :, :].rearrange("p i j -> p (i j)"), start=True, stop=True).then_inc(g_c1, 1)
            pe.wait_ge(g_r1, 1)
            pe.wait_ge(conv_vs, 2)
            t.matmul(bank[7][0:C, 0:2 * NP], gw2[:, :], g1[:, :], start=True, stop=True).then_inc(g_c2, 1)
            for i in range(2):
                pe.wait_ge(g_sp, 3 + i)
                t.matmul(bank[i][:, :], same_img[:, :], gspread[:, 8 * i:8 * (i + 1), :].rearrange("p i c -> p (i c)"),
                         start=True, stop=True).then_inc(g_G, 1)

            def moe_x(b, q):
                pe.wait_ge(m_lo, b + 1)
                for j in range(T):
                    last = t.transpose(bank[6 + q][:, P * j:P * (j + 1)],
                                       hl[:, T * q + j, :, :].rearrange("p s c -> p (s c)").bitcast(F32), ident[:, :])
                last.then_inc(m_X, 1)

            def moe_logits(b, q):
                pe.wait_ge(m_xs, 2 * b + q + 1)
                for j in range(T):
                    last = t.matmul(bank[6 + q][:, 2 * E * j:2 * E * (j + 1)],
                                    xs[:, b % 2, CH * q + P * j:CH * q + P * (j + 1)],
                                    router[:, :, :].rearrange("p s e -> p (s e)"), start=True, stop=True)
                last.then_inc(m_L, 1)

            def moe_c(b, q):
                pe.wait_ge(m_chl, 2 * b + 2)
                for j in range(T):
                    last = t.transpose(bank[6 + q][:, P * j:P * (j + 1)],
                                       chl[:, T * q + j, :, :].rearrange("p s e -> p (s e)").bitcast(F32), ident[:, :])
                last.then_inc(m_C, 1)

            def moe_first(b, n):
                N, q, k = 8 * b + n, n // KP, n % KP
                wait(pe, m_sc, N - 1)
                pe.wait_ge(m_cs, 2 * b + q + 1)
                t.matmul(bank[2 + n % 2][:, :], sel[:, k, :], cs[:, CH * q:CH * (q + 1)], start=True, stop=True).then_inc(m_cb, 1)
                wait(pe, m_act, N - 1)
                for part in range(2):
                    last = t.matmul(bank[n % 2][:, :], w1s[:, part, P * k:P * (k + 1)], xs[:, b % 2, CH * q:CH * (q + 1)],
                                    start=(part == 0), stop=(part == 1))
                last.then_inc(m_z, 1)

            def moe_second(b, n):
                N, q, k = 8 * b + n, n // KP, n % KP
                if k == 0:
                    wait(pe, m_yT, 2 * b + q - 1)
                    wait(pe, m_res, 2 * b + q - 1)
                    for half in range(2):
                        t.matmul(bank[4 + q][C * half:C * (half + 1), 0:2 * P], b2rows[:, :],
                                 cs[:, CH * q + 2 * P * half:CH * q + 2 * P * (half + 1)].bitcast(F32), start=True, stop=False)
                pe.wait_ge(m_sc, N + 1)
                for half in range(2):
                    last = t.matmul(bank[4 + q][C * half:C * (half + 1), 0:2 * P], w2[:, k, :],
                                    scaled[:, n % 2, 2 * P * half:2 * P * (half + 1)], start=False, stop=(k == KP - 1))
                last.then_inc(m_l2, 1)

            def back(yt, s_yT, s_yo, b, q):
                pe.wait_ge(s_yT, 2 * b + q + 1)
                o = bank[4 + q][:, 2 * P:4 * P].rearrange("p (h j c) -> p j h c", h=2, j=2)
                for j in range(2):
                    last = t.transpose(o[:, j], yt[:, q, P * j:P * (j + 1)], ident[:, :])
                last.then_inc(s_yo, 1)

            def mix_x(g_, part, q):
                pe.wait_ge(c_lo, g_ + 1)
                if part == 0:
                    wait(pe, c_xp, 2 * g_ + q - 1)
                else:
                    wait(pe, d_xs, 2 * (g_ - LAG) + q - 1)
                for j in range(T):
                    last = t.transpose(bank[(2 if part else 6) + q][:, P * j:P * (j + 1)],
                                       hlc[:, g_ % 2, T2 * part + T * q + j, :, :].rearrange("p s c -> p (s c)").bitcast(F32), ident[:, :])
                last.then_inc(d_X if part else c_X, 1)

            def mix_conv(b, q):
                i = 2 * b + q
                pe.wait_ge(c_xp, i + 1)
                wait(pe, c_cvs, i - 1)
                for d, (dx, dy) in enumerate(DIRECTIONS):
                    src = xp[:, 2 * q:2 * q + 2, 1 - dy:1 - dy + H, 1 - dx:1 - dx + W]
                    last = t.matmul(bank[q][:, :], vconv[:, d, :, :].rearrange("p s c -> p (s c)"), src,
                                    start=(d == 0), stop=(d == 7))
                last.then_inc(c_cv, 1)

            def mix_back(b, q):
                i = 2 * b + q
                pe.wait_ge(c_cvs, i + 1)
                wait(pe, c_r2, i - 1)
                if b == 0:
                    pe.wait_ge(m_res, 2 * NB)
                for j in range(T):
                    last = t.matmul(bank[4 + q][:, C * j:C * (j + 1)], cvs[:, q, j:CH:T], two_ident[:, :], start=True, stop=True)
                last.then_inc(c_bk, 1)

            moe_x(0, 0)
            moe_x(0, 1)
            pe.wait_ge(w_lo, 3)
            moe_logits(0, 0)
            moe_logits(0, 1)
            pe.wait_ge(g_done, 2)
            pe.wait_ge(w_hi, 4)
            moe_c(0, 0)
            moe_c(0, 1)
            for b in range(NB):
                more = b + 1 < NB
                for n in range(8):
                    moe_first(b, n)
                    if n >= 2:
                        moe_second(b, n - 2)
                    elif b:
                        moe_second(b - 1, n + 6)
                    if n == 0 and more:
                        pe.wait_ge(m_cs, 2 * b + 2)
                        moe_x(b + 1, 0)
                        moe_x(b + 1, 1)
                    if n == 1 and more:
                        moe_logits(b + 1, 0)
                        moe_logits(b + 1, 1)
                    if n == 3 and b:
                        back(yTs, m_yT, m_yo, b - 1, 1)
                    if n == 7 and not more:
                        pe.wait_ge(m_cs, 2 * NB)
                        mix_x(0, 0, 0)
                        mix_x(0, 0, 1)
                if more:
                    moe_c(b + 1, 0)
                    moe_c(b + 1, 1)
                back(yTs, m_yT, m_yo, b, 0)
            moe_second(NB - 1, 6)
            moe_second(NB - 1, 7)
            back(yTs, m_yT, m_yo, NB - 1, 1)

            pe.wait_ge(m_act, 8 * NB)
            pe.wait_ge(m_sc, 8 * NB)
            for b in range(NM - 1):
                if 0 <= b < NB:
                    mix_conv(b, 0)
                if b + 1 < NB:
                    mix_x(b + 1, 0, 0)
                    mix_x(b + 1, 0, 1)
                if 0 <= b < NB:
                    mix_conv(b, 1)
                    mix_back(b, 0)
                if b + 1 >= LAG:
                    mix_x(b + 1, 1, 0)
                    mix_x(b + 1, 1, 1)
                if 0 <= b < NB:
                    mix_back(b, 1)

            def ffn1(N):
                b, n = divmod(N, 8)
                q, k = n // KP, n % KP
                wait(pe, f_h1, N - 1)
                if q == 0 and k == 0:
                    pe.wait_ge(d_xs, 2 * b + 2)
                for part in range(2):
                    last = t.matmul(bank[6 + n % 2][:, :], f1s[:, part, P * k:P * (k + 1)], xs_ffn[:, b, CH * q:CH * (q + 1)],
                                    start=(part == 0), stop=(part == 1))
                last.then_inc(f_z1, 1)

            def ffn2(N):
                b, n = divmod(N, 8)
                k = n % KP
                pe.wait_ge(f_h1, N + 1)
                wait(pe, f_h2, N - 1)
                if N < 2:
                    pe.wait_ge(f2_scaled, 1)
                t.matmul(bank[2 + n % 2][:, :], f2[:, k, :], act[:, n % 2, :], start=True, stop=True).then_inc(f_z2, 1)

            def ffn3(N):
                b, n = divmod(N, 8)
                q, k = n // KP, n % KP
                if k == 0:
                    wait(pe, f_yT, 2 * b + q - 1)
                    wait(pe, f_res, 2 * b + q - 1)
                    if N == KP:
                        pe.wait_ge(r_dve, R_CTAB)
                pe.wait_ge(f_h2, N + 1)
                for half in range(2):
                    last = t.matmul(bank[4 + q][C * half:C * (half + 1), 0:2 * P], fo[:, k, :],
                                    scaled[:, n % 2, 2 * P * half:2 * P * (half + 1)], start=(k == 0), stop=(k == KP - 1))
                last.then_inc(f_l3, 1)

            pe.wait_ge(b2_sel, 4)
            pe.wait_ge(c_r2, 2 * NB)
            for k in range(KP):
                last = t.matmul(bank[4][0:2 * E, 0:C], b2sel[:, k, :, :].rearrange("p s e -> p (s e)"), fo[:, k, :],
                                start=(k == 0), stop=(k == KP - 1))
            last.then_inc(r_pe, 1)
            pe.wait_ge(c_cvs, 2 * NB)
            pe.wait_ge(c_xp, 2 * NB)
            ffn1(0)
            pe.wait_ge(d_acc, NB)
            for q in range(2):
                last = t.matmul(bank[0][:, 0:T * C], half_mean[:, :], fsum[:, T * q:T * (q + 1), :].rearrange("p t c -> p (t c)"),
                                start=(q == 0), stop=(q == 1))
            last.then_inc(r_pe, 1)
            ffn1(1)
            pe.wait_ge(r_dve, R_FEAT)
            for j in range(T):
                last = t.transpose(bank[1][0:C, P * j:P * (j + 1)], feat[:, j, :], ident[:, :])
            last.then_inc(r_pe, 1)
            pe.wait_ge(r_dve, R_FEATT)
            for j in range(T):
                last = t.matmul(bank[0][:, E * j:E * (j + 1)], featT[:, P * j:P * (j + 1)], wr[:, :], start=True, stop=True)
            last.then_inc(r_log, 1)
            pe.wait_ge(d_xs, 2 * NB)
            ffn2(0)
            ffn2(1)
            pe.wait_ge(r_dve, R_WL)
            for j in range(T):
                last = t.transpose(bank[1][0:2 * E, P * j:P * (j + 1)], whl[:, j, :, :].rearrange("p s e -> p (s e)").bitcast(F32), ident[:, :])
            last.then_inc(r_pe, 1)
            pe.wait_ge(r_act, 2)
            for k in range(KP):
                if k == 2:
                    pe.wait_ge(r_dve, R_U16)
                    for j in range(T):
                        last = t.matmul(bank[5][:, C * j:C * (j + 1)], wT[:, P * j:P * (j + 1)].bitcast(F32), u16[:, :], start=True, stop=True)
                    last.then_inc(r_pe, 1)
                    pe.wait_ge(r_ws, 1)
                if k == 3:
                    pe.wait_ge(r_wa, 1)
                t.matmul(bank[k % 2][:, :], sel[0:2 * E, k, :], wT[:, :], start=True, stop=True).then_inc(r_spread, 1)

            for N in range(8 * NB + 2):
                if 2 <= N < 8 * NB:
                    ffn1(N)
                if 3 <= N <= 8 * NB:
                    ffn2(N - 1)
                if N >= 2:
                    ffn3(N - 2)
                n = N % 8
                if n == 3 and N > 8:
                    back(yTs, f_yT, f_yo, N // 8 - 1, 1)
                if n == 7:
                    back(yTs, f_yT, f_yo, N // 8, 0)
            back(yTs, f_yT, f_yo, NB - 1, 1)


_INS = ['x', 'L0_conv_w1', 'L0_conv_b1', 'L0_conv_w2', 'L0_conv_b2', 'L0_ffn_router_w', 'L0_ffn_w1', 'L0_ffn_b1',
        'L0_ffn_w2', 'L0_ffn_b2', 'L1_conv_Wd', 'L1_conv_Wc', 'L1_conv_bc', 'L1_ffn_Wr', 'L1_ffn_br', 'L1_ffn_W1',
        'L1_ffn_b1', 'L1_ffn_g1', 'L1_ffn_be1', 'L1_ffn_m1', 'L1_ffn_v1', 'L1_ffn_W2', 'L1_ffn_b2', 'L1_ffn_g2',
        'L1_ffn_be2', 'L1_ffn_m2', 'L1_ffn_v2', 'L1_ffn_Wo', 'L1_ffn_bo']
_OUTS = [((32, 16, 16, 64), 'float32')]


def kernel(**inputs):
    import numpy as _np
    import concourse.bacc as _bacc
    from concourse import mybir as _mybir
    from concourse.bass_utils import run_bass_kernel_spmd as _run

    nc = _bacc.Bacc("TRN2", target_bir_lowering=False, num_devices=1)
    arrays, args = {}, {}
    for name in _INS:
        arr = _np.ascontiguousarray(inputs[name])
        arrays[f"in_{name}_dram"] = arr
        args[name] = nc.dram_tensor(f"in_{name}_dram", arr.shape, _mybir.dt.from_np(arr.dtype), kind="ExternalInput").ap()
    outs = []
    for i, (shape, dtype) in enumerate(_OUTS):
        dt = _mybir.dt.from_np(_np.dtype(dtype))
        outs.append(nc.dram_tensor(f"out_{i}_dram", shape, dt, kind="ExternalOutput").ap())
    metaformer_kernel(nc, args, outs[0])
    r = _run(nc, [arrays], core_ids=[0])
    got = tuple(r.results[0][f"out_{i}_dram"] for i in range(len(_OUTS)))
    return got[0]
```

```python
from contextlib import ExitStack

import concourse.bass as bass
from concourse import mybir

ALU = mybir.AluOpType
ACT = mybir.ActivationFunctionType
AX = mybir.AxisListType
F32 = mybir.dt.float32
F32R = mybir.dt.float32r

P = 128
B, H, W, C = 32, 16, 16, 64
E = 8
T = 4
NP = B // 2
KP = E // 2
CH = P * T
NB = NP // 2
T2 = 2 * T
NG = 4
GP = NP // NG
M = H * W
PADH, PADW = H + 2, W + 2
LAG = 4
NM = NB + LAG
EPS_C, EPS_T, EPS_BN = 1e-6, 1e-5, 1e-3
ROUNDS = 3
DIRECTIONS = [(0, -1), (1, -1), (1, 0), (1, 1), (0, 1), (-1, 1), (-1, 0), (-1, -1)]

VECS = ["L0_ffn_b1", "L1_ffn_b1", "L1_ffn_g1", "L1_ffn_be1", "L1_ffn_m1", "L1_ffn_v1",
        "L1_ffn_b2", "L1_ffn_g2", "L1_ffn_be2", "L1_ffn_m2", "L1_ffn_v2"]
ROW = {name: KP * n for n, name in enumerate(VECS)}
ROW_GB1 = KP * len(VECS)
ROW_GB2 = ROW_GB1 + 1
ROW_BC = ROW_GB1 + 2
ROW_ROUTER = ROW_GB1 + 4
NROWS = ROW_ROUTER + E


def wait(eng, sem, value):
    if isinstance(value, int) and value <= 0:
        return
    eng.wait_ge(sem, value)


def rep(ap, axis, n):
    shape = list(ap.shape)
    shape[axis] = n
    return ap.broadcast_to(shape)


def metaformer_kernel(nc, a, out):
    ctx = ExitStack()
    with ctx:
        def sb(name, shape, dt=F32):
            return ctx.enter_context(nc.sbuf_tensor(name, shape, dt))

        sems = {}

        def sem(name):
            sems[name] = ctx.enter_context(nc.semaphore(name))
            return sems[name]

        bank = [ctx.enter_context(nc.psum_tensor(f"bank{i}", [P, 512], F32)) for i in range(8)]

        x = sb("x", [P, NP, T * C])
        xn = sb("xn", [P, NP, T * C])
        gate = sb("gate", [P, NP, C])
        xs_ffn = sb("xs_ffn", [P, NB, T2 * P], F32R)

        ident = sb("ident", [P, P])
        two_ident15 = sb("two_ident15", [P, C])
        same_img = sb("same_img", [P, P])
        two_ident = sb("two_ident", [P, C])
        half_mean = sb("half_mean", [P, P])
        sel_f = sb("sel_f", [P, KP, P])
        sel = sb("sel", [P, KP, P], F32R)
        rank = sb("rank", [P, E])
        neg_half = sb("neg_half", [P, 16])
        pos_half = sb("pos_half", [P, 16])
        eps_vec = sb("eps_vec", [P, 2 * T2])

        vec_rows = sb("vec_rows", [NROWS, P])
        cols = sb("cols", [P, NROWS])
        gw1 = sb("gw1", [C, C])
        gw2 = sb("gw2", [C, C])
        half_gb2 = sb("half_gb2", [C, 1])
        w1f = sb("w1f", [P, E * C])
        w1s = sb("w1s", [P, 2, E * C], F32R)
        w2 = sb("w2", [P, KP, C])
        b2rows = sb("b2rows", [P, C])
        router = sb("router", [P, 2, E], F32R)
        wd = sb("wd", [P, 4, C])
        wc = sb("wc", [C, 8, C])
        wdT = sb("wdT", [C, 8, 2, C])
        wcT = sb("wcT", [C, 8, C])
        vconv = sb("vconv", [P, 8, 2, C], F32R)
        f1f = sb("f1f", [P, E * C])
        f1s = sb("f1s", [P, 2, E * C], F32R)
        f2 = sb("f2", [P, KP, P])
        fo = sb("fo", [P, KP, C])
        bo = sb("bo", [2 * E, C])
        wr = sb("wr", [C, E])
        br = sb("br", [P, E])
        bn1 = sb("bn1", [P, 2, KP])
        bn2 = sb("bn2", [P, 3, KP])
        bn_t = sb("bn_t", [P, 4, KP])

        stats = sb("stats", [P, 16, 6])
        mv2 = sb("mv", [P, 2, 16, 2])
        mv = mv2[:, 0]
        veps = sb("veps", [P, 16])
        rstd = sb("rstd", [P, 16])
        rsum = sb("rsum", [P, GP])
        rmean = sb("rmean", [P, 2, GP])
        xcc = [sb("xcc", [P, GP, M]), gate[:, :, :].rearrange("p (i u) c -> p i (u c)", i=GP)]
        sqj = sb("sqj", [P, M])
        sumsq = sb("sumsq", [P, NP])
        xT = sb("xT", [P, 2, GP * P])
        rtrace = sb("rtrace", [P, NP])
        trm = sb("trm", [P, NP])
        root = sb("root", [P, NP])
        Ac = sb("Ac", [P, NP, C])
        YZ = sb("YZ", [P, NP, 2, C])
        Zd = sb("Zd", [P, NP, P])
        Td = sb("Td", [P, NP, P])
        u_sum = sb("u_sum", [P, NP])
        u_own = sb("u_own", [P, NP, 2])
        z_own = sb("z_own", [P, NP, 2])
        yv = sb("yv", [C, 4, NP, 2])
        g1 = sb("g1", [C, NP * 2])
        g2 = sb("g2", [C, NP, 2])
        gsig = sb("gsig", [P, NP])
        gspread = sb("gspread", [P, NP, C])

        xc = sb("xc", [P, T2, C])
        xnb = sb("xnb", [P, 2, T2, C])
        hl = sb("hl", [P, T2, 2, C], F32R)
        xs = sb("xs", [P, 2, T2 * P], F32R)
        cs = sb("cs", [P, T2 * P], F32R)
        act = sb("act", [P, 2, CH])
        scaled = sb("scaled", [P, 2, CH])
        yTs = sb("yTs", [P, 2, 2 * P])
        lg = sb("lg", [P, T2, E])
        tmp = sb("tmp", [P, T2, E])
        one1 = sb("one1", [P, T2, E])
        one2 = sb("one2", [P, T2, E])
        m12 = sb("m12", [P, 8, T2])
        cw = sb("cw", [P, T2, E])
        chl = sb("chl", [P, T2, P // E, E], F32R)
        xp = sb("xp", [P, 4, PADH, PADW], F32R)
        cvs = sb("cvs", [P, 2, CH])
        rstdc = sb("rstdc", [P, 2, 2 * T2])
        xcn = Zd[:, 0:NP // 2, :].rearrange("p i (u c) -> p (i u) c", c=C)
        xnc = YZ[:, :, :, :].rearrange("p (v i) t c -> p v (i t) c", v=2)
        hlc = xn[:, :, :].bitcast(F32R).rearrange("p (v i) (t s c) -> p v (i t) s c", v=2, t=2, s=2)
        fsum = sb("fsum", [P, T2, C])
        feat = Td[:, 8:10, :].rearrange("p i (u c) -> p (i u) c", u=2)
        featT = Td[0:C, 0:4, :].rearrange("p i n -> p (i n)")
        fl = sb("fl", [P, 4, T, E])
        fm = sb("fm", [P, 4, T])
        whl = sb("whl", [P, T, 2, E], F32R)
        wT = sb("wT", [2 * E, T * P], F32R)
        wspread = YZ[:, :, :, :].rearrange("p (k i) t c -> p k (i t c)", k=KP)
        b2sel = sb("b2sel", [P, KP, 2, E])
        u16 = sb("u16", [2 * E, C])
        ctab = sb("ctab", [P, T * C])

        S = sem
        x_in = [S(f"x_in{g}") for g in range(NG)]
        x_first = [S(f"x_first{half}") for half in range(2)]
        w_gate, w_moe, w_conv, w_ffn, w_vec = S("w_gate"), S("w_moe"), S("w_conv"), S("w_ffn"), S("w_vec")
        consts, consts_v, zeroed = S("consts"), S("consts_v"), S("zeroed")
        vecs_ready, cols_ready = S("vecs_ready"), S("cols_ready")
        w_hi, w_lo, f2_scaled, b2_sel, diag_zero = (S(n) for n in ("w_hi", "w_lo", "f2_scaled", "b2_sel", "diag_zero"))
        own_zero = S("own_zero")
        bn_step, bn_pow, s2_spread = S("bn_step"), S("bn_pow"), S("s2_spread")
        conv_wT, conv_wTs, conv_v, conv_vs = S("conv_wT"), S("conv_wTs"), S("conv_v"), S("conv_vs")
        tok_stats_taken = S("tok_stats_taken")
        tok_mean_var = S("tok_mean_var")
        tok_var_eps = S("tok_var_eps")
        tok_rstd_ready = S("tok_rstd_ready")
        tok_centred = S("tok_centred")
        tok_normed = S("tok_normed")
        row_sum = S("row_sum")
        row_mean = S("row_mean")
        rows_centred = S("rows_centred")
        row_squares = S("row_squares")
        rows_T = S("rows_T")
        rows_T_copied = S("rows_T_copied")
        gram_done = S("gram_done")
        trace_done = S("trace_done")
        trace_read = S("trace_read")
        trace_all = S("trace_all")
        root_trace = S("root_trace")
        A_ready = S("A_ready")
        Z0_ready = S("Z0_ready")
        Z0_on_diag = S("Z0_on_diag")
        Y0_done = S("Y0_done")
        Y0_copied = S("Y0_copied")
        ns_ZY = S("ns_ZY")
        ns_T_ready = S("ns_T_ready")
        ns_TYTZ = S("ns_TYTZ")
        ns_YZ_copied = S("ns_YZ_copied")
        ns_Z_on_diag = S("ns_Z_on_diag")
        u_summed = S("u_summed")
        u_split = S("u_split")
        zu_done = S("zu_done")
        zu_split = S("zu_split")
        yzu_done = S("yzu_done")
        y_terms_ready = S("y_terms_ready")
        y_ready = S("y_ready")
        conv1_done = S("conv1_done")
        conv1_relu = S("conv1_relu")
        conv2_done = S("conv2_done")
        conv2_tanh = S("conv2_tanh")
        gate_rows_ready = S("gate_rows_ready")
        gate_in_psum = S("gate_in_psum")
        gate_ready = S("gate_ready")
        first_x1 = S("first_x1")
        gated = S("gated")
        x1_ready = S("x1_ready")
        moe_slot_stats = S("moe_slot_stats")
        moe_mean_var = S("moe_mean_var")
        moe_var_eps = S("moe_var_eps")
        moe_rstd_ready = S("moe_rstd_ready")
        moe_centred = S("moe_centred")
        moe_normed = S("moe_normed")
        moe_high = S("moe_high")
        moe_low_ready = S("moe_low_ready")
        moe_residual = S("moe_residual")
        tok_T = S("tok_T")
        tok_T_copied = S("tok_T_copied")
        logits_done = S("logits_done")
        route_step = S("route_step")
        route_tanh = S("route_tanh")
        weights_split = S("weights_split")
        weights_T = S("weights_T")
        weights_T_copied = S("weights_T_copied")
        weights_spread = S("weights_spread")
        hidden_done = S("hidden_done")
        hidden_gelu = S("hidden_gelu")
        hidden_scaled = S("hidden_scaled")
        second_done = S("second_done")
        moe_y_copied = S("moe_y_copied")
        moe_y_back = S("moe_y_back")
        moe_added = S("moe_added")
        mix_slot_stats = S("mix_slot_stats")
        mix_mean_var = S("mix_mean_var")
        mix_var_eps = S("mix_var_eps")
        mix_rstd_ready = S("mix_rstd_ready")
        mix_centred = S("mix_centred")
        mix_normed = S("mix_normed")
        mix_high_ready = S("mix_high_ready")
        mix_low_ready = S("mix_low_ready")
        mix_low_last = S("mix_low_last")
        mix_T = S("mix_T")
        mix_padded = S("mix_padded")
        conv_done = S("conv_done")
        conv_copied = S("conv_copied")
        mix_back_done = S("mix_back_done")
        mix_added = S("mix_added")
        ffn_T = S("ffn_T")
        ffn_T_copied = S("ffn_T_copied")
        batch_sum = S("batch_sum")
        rt_tensor = S("rt_tensor")
        rt_logits = S("rt_logits")
        rt_vector = S("rt_vector")
        rt_scalar = S("rt_scalar")
        rt_exp_table = S("rt_exp_table")
        rt_spread = S("rt_spread")
        rt_copied_vector = S("rt_copied_vector")
        rt_copied_scalar = S("rt_copied_scalar")
        const_added = S("const_added")
        layer1_done = S("layer1_done")
        layer1_relu = S("layer1_relu")
        layer2_done = S("layer2_done")
        layer2_scaled = S("layer2_scaled")
        layer3_done = S("layer3_done")
        ffn_y_copied = S("ffn_y_copied")
        ffn_y_back = S("ffn_y_back")
        ffn_added = S("ffn_added")
        stored = S("stored")

        x_dram = a["x"].rearrange("b h w c -> (b h w c)").rearrange("(i p n) -> p i n", p=P, n=T * C)
        o_dram = out.rearrange("b h w c -> (b h w c)").rearrange("(i p n) -> p i n", p=P, n=T * C)

        def blk(t, b):
            return t[:, bass.ds(2 * b, 2), :].rearrange("p i (t c) -> p (i t) c", c=C)

        def slots(g):
            return slice(0 if g < NB else T2, T2 if g < LAG else 2 * T2)

        STEPS = 2 * ROUNDS

        def ns_group(n):
            return 2 * (n // STEPS) + n % 2

        def ns_last(n):
            return n % STEPS >= STEPS - 2

        def z_moves(n):
            return sum(not ns_last(m) for m in range(n))

        GRAM_BANK, Y0_BANK = (0, 1, 6, 6), (2, 3, 6, 6)
        HP = NP // 2
        COL_ZU, COL_W, COL_C1, COL_C2 = 0, 2 * NP, 4 * NP, 6 * NP
        COL_VECS = 8 * NP

        def halves(j):
            return slice(C * j, C * (j + 1))

        def on_diag(t, gr, j):
            return t[halves(j), GP * gr:GP * (gr + 1), halves(j)]

        block = ctx.enter_context(nc.Block())

        @block.sync
        def _(sp):
            for half in range(2):
                first = slice(GP // 2 * half, GP // 2 * (half + 1))
                sp.dma_start(x[:, first, :], x_dram[:, first, :]).then_inc(x_first[half], 16)
            for g in range(1, NG):
                sp.dma_start(x[:, GP * g:GP * (g + 1), :], x_dram[:, GP * g:GP * (g + 1), :]).then_inc(x_in[g], 16)
            sp.dma_start(gw1[:, :], a["L0_conv_w1"][1, 1]).then_inc(w_gate, 16)
            sp.dma_start(gw2[:, :], a["L0_conv_w2"][1, 1]).then_inc(w_gate, 16)
            sp.wait_ge(zeroed, 3)
            for name in VECS:
                sp.dma_start(vec_rows[ROW[name]:ROW[name] + KP, :],
                             a[name].rearrange("(k two) h -> k (two h)", two=2)).then_inc(w_vec, 16)
            for half in range(2):
                s = slice(C * half, C * (half + 1))
                sp.dma_start(vec_rows[ROW_GB1:ROW_GB1 + 1, s], a["L0_conv_b1"].rearrange("(a c) -> a c", a=1)).then_inc(w_vec, 16)
                sp.dma_start(vec_rows[ROW_GB2:ROW_GB2 + 1, s], a["L0_conv_b2"].rearrange("(a c) -> a c", a=1)).then_inc(w_vec, 16)
                sp.dma_start(vec_rows[ROW_ROUTER:NROWS, s], a["L0_ffn_router_w"]).then_inc(w_vec, 16)
            sp.dma_start(vec_rows[ROW_BC:ROW_BC + 1, 0:C], a["L1_conv_bc"].rearrange("(a c) -> a c", a=1)).then_inc(w_vec, 16)
            for half in range(2):
                s = slice(C * half, C * (half + 1))
                sp.dma_start(w1f[s, :].rearrange("p (e h) -> p e h", e=E), a["L0_ffn_w1"].rearrange("e c h -> c e h")).then_inc(w_moe, 16)
                sp.dma_start(b2rows[E * half:E * (half + 1), :], a["L0_ffn_b2"]).then_inc(w_moe, 16)
                sp.dma_start(w2[s, :, :], a["L0_ffn_w2"].rearrange("(k two) h c -> two h k c", two=2)[half]).then_inc(w_moe, 16)
                sp.dma_start(wd[s, :, :], a["L1_conv_Wd"].rearrange("(k two) c e -> two c k e", two=2)[half]).then_inc(w_conv, 16)
            sp.dma_start(wc[:, :, :], a["L1_conv_Wc"].rearrange("o (d e) -> o d e", d=8)).then_inc(w_conv, 16)
            for half in range(2):
                s = slice(C * half, C * (half + 1))
                sp.dma_start(f1f[s, :].rearrange("p (e h) -> p e h", e=E), a["L1_ffn_W1"].rearrange("e c h -> c e h")).then_inc(w_ffn, 16)
                sp.dma_start(f2[s, :, s], a["L1_ffn_W2"].rearrange("(k two) h o -> two h k o", two=2)[half]).then_inc(w_ffn, 16)
                sp.dma_start(fo[s, :, :], a["L1_ffn_Wo"].rearrange("(k two) h c -> two h k c", two=2)[half]).then_inc(w_ffn, 16)
            for part in range(2):
                sp.dma_start(bo[E * part:E * (part + 1), :], a["L1_ffn_bo"]).then_inc(w_ffn, 16)
            sp.dma_start(wr[:, :], a["L1_ffn_Wr"]).then_inc(w_ffn, 16)
            sp.dma_start(br[:, :], rep(a["L1_ffn_br"].rearrange("(a e) -> a e", a=1), 0, P)).then_inc(w_ffn, 16)
            with sp.Fori(0, NP) as i:
                sp.wait_ge(ffn_added, i + 1)
                sp.dma_start(o_dram[:, bass.ds(i, 1), :], x[:, bass.ds(i, 1), :]).then_inc(stored, 16)
            sp.wait_ge(stored, 16 * NP)
        R_FEAT, R_FEATT, R_LOG, R_MAX, R_SUB, R_SUM, R_REC, R_W, R_WH, R_WL, R_U16, R_CTAB = range(1, 13)

        W_GATE, W_VEC, W_MOE, W_CONV, W_FFN = 32, 16 * (len(VECS) + 7), 96, 48, 16 * 10

        @block.gpsimd
        def _(pool):
            g = nc.gpsimd
            g.memset(neg_half[:, :], -0.5).then_inc(consts, 1)
            g.memset(pos_half[:, :], 0.5).then_inc(consts, 1)
            g.memset(eps_vec[:, 0:T2], EPS_C).then_inc(consts, 1)
            g.memset(eps_vec[:, T2:2 * T2], EPS_T).then_inc(consts, 1)
            g.memset(vec_rows[:, :], 0.0).then_inc(zeroed, 1)
            g.memset(b2rows[:, :], 0.0).then_inc(zeroed, 1)
            g.memset(f2[:, :, :], 0.0).then_inc(zeroed, 1)
            g.memset(ident[:, :], 0.0).then_inc(consts, 1)
            g.memset(two_ident15[:, :], 0.0).then_inc(consts, 1)
            g.memset(two_ident[:, :], 0.0).then_inc(consts, 1)
            g.memset(half_mean[:, :], 0.0).then_inc(consts, 1)
            g.memset(sel_f[:, :, :], 0.0).then_inc(consts, 1)
            g.memset(same_img[:, :], 0.0).then_inc(consts, 1)
            for e in range(E):
                g.memset(rank[:, e:e + 1], float(E - e)).then_inc(consts, 1)
            pool.wait_ge(consts, 18)
            g.memset(same_img[0:C, 0:C], 1.0).then_inc(consts, 1)
            pool.wait_ge(consts, 19)
            g.memset(same_img[C:P, C:P], 1.0).then_inc(consts, 1)
            pool.wait_ge(consts, 20)

            def fill(tile, value, base, pattern):
                return g.affine_select(out=tile, in_=tile, compare_op=ALU.not_equal, fill=value, base=base,
                                       pattern=pattern, channel_multiplier=1)
            fill(ident[:, :], 1.0, 0, [[-1, P]]).then_inc(consts, 1)
            n = 21
            for tile, value, step in ((two_ident, 1.0, (0, -C)), (two_ident15, 1.5, (0, -C)), (half_mean, 1.0 / B, (0, -C, C))):
                for base in step:
                    pool.wait_ge(consts, n)
                    fill(tile[:, :], value, base, [[-1, tile.shape[1]]]).then_inc(consts, 1)
                    n += 1
            for base in (0, -E):
                pool.wait_ge(consts, n)
                fill(sel_f[:, :, :].rearrange("p k (u h) -> p k u h", u=2), 1.0, base, [[-2, KP], [-1, 2], [0, C]]).then_inc(consts, 1)
                n += 1

            pool.wait_ge(zeroed, 3)
            def tok_rstd(gr):
                pool.wait_ge(tok_mean_var, gr + 1)
                wait(pool, tok_rstd_ready, gr)
                g.tensor_scalar(veps[:, :], mv2[:, gr % 2, :, 1], EPS_C, None, ALU.add).then_inc(tok_var_eps, 1)
                pool.wait_ge(tok_var_eps, gr + 1)
                wait(pool, tok_normed, gr)
                g.tensor_tensor(rstd[:, :], veps[:, :], neg_half[:, :], ALU.pow).then_inc(tok_rstd_ready, 1)

            def centre_rows(gr):
                pool.wait_ge(row_mean, gr + 1)
                wait(pool, rows_T, 2 * (gr - 1))
                wait(pool, row_squares, GP * (gr - 1))
                g.tensor_tensor(xcc[gr % 2][:, :, :], xn[:, GP * gr:GP * (gr + 1), :],
                                rep(rmean[:, gr % 2, :].rearrange("p (n o) -> p n o", o=1), 2, M), ALU.subtract).then_inc(rows_centred, 1)

            tok_rstd(0)
            g.memset(Zd[:, :, :], 0.0).then_inc(diag_zero, 1)
            tok_rstd(1)
            centre_rows(0)
            g.memset(Td[:, :, :], 0.0).then_inc(diag_zero, 1)
            tok_rstd(2)
            centre_rows(1)
            centre_rows(2)
            tok_rstd(3)
            centre_rows(3)
            pool.wait_ge(trace_all, 1)
            g.tensor_tensor(root[:, :], trm[:, :], pos_half[:, :], ALU.pow).then_inc(root_trace, 1)

            g.memset(xp[:, :, :, :].bitcast(F32), 0.0).then_inc(consts_v, 1)
            g.memset(chl[:, :, :, :].bitcast(F32), 0.0).then_inc(consts_v, 1)
            g.memset(fsum[:, :, :], 0.0).then_inc(consts_v, 1)
            pool.wait_ge(consts_v, 3)
            pool.wait_ge(cols_ready, 1)
            col = lambda name: cols[:, ROW[name]:ROW[name] + KP]
            for i, n in enumerate("12"):
                g.tensor_scalar(bn_t[:, 2 * i, :], col("L1_ffn_v" + n), EPS_BN, None, ALU.add).then_inc(bn_step, 1)
            for i in range(2):
                pool.wait_ge(bn_step, i + 1)
                g.tensor_tensor(bn_t[:, 2 * i + 1, :], bn_t[:, 2 * i, :], neg_half[:, 0:KP], ALU.pow).then_inc(bn_pow, 1)
            for i, (n, bn) in enumerate((("1", bn1), ("2", bn2))):
                pool.wait_ge(bn_pow, i + 1)
                k = 2 + 4 * i
                g.tensor_tensor(bn[:, 0, :], bn_t[:, 2 * i + 1, :], col("L1_ffn_g" + n), ALU.mult).then_inc(bn_step, 1)
                g.tensor_tensor(bn_t[:, 2 * i, :], col("L1_ffn_b" + n), col("L1_ffn_m" + n), ALU.subtract).then_inc(bn_step, 1)
                pool.wait_ge(bn_step, k + 2)
                g.tensor_tensor(bn_t[:, 2 * i + 1, :], bn_t[:, 2 * i, :], bn[:, 0, :], ALU.mult).then_inc(bn_step, 1)
                pool.wait_ge(bn_step, k + 3)
                g.tensor_tensor(bn[:, 1, :], bn_t[:, 2 * i + 1, :], col("L1_ffn_be" + n), ALU.add).then_inc(bn_step, 1)
            pool.wait_ge(bn_step, 10)
            g.tensor_scalar(bn2[:, 2, :], bn2[:, 1, :], -1.0, None, ALU.mult).then_inc(bn_step, 1)
            for i, (lo, src, high) in enumerate(((router[:, 1, :], cols[:, ROW_ROUTER:NROWS], router[:, 0, :]),
                                                 (w1s[:, 1, :], w1f[:, :], w1s[:, 0, :]),
                                                 (f1s[:, 1, :], f1f[:, :], f1s[:, 0, :]))):
                pool.wait_ge(w_hi, i + 1)
                g.tensor_tensor(lo, src, high.bitcast(F32), ALU.subtract).then_inc(w_lo, 1)

            def moe_x1(b):
                if b >= NB:
                    return
                pool.wait_ge(gate_ready, 1 if b < NB // 2 else 2)
                gx = blk(xn, b).rearrange("p (i t) c -> p i t c", t=T)
                gb = rep(gate[:, 2 * b:2 * b + 2, :].rearrange("p i (o c) -> p i o c", o=1), 2, T)
                g.tensor_tensor(gx, gx, gb, ALU.mult).then_inc(gated, 1)
                pool.wait_ge(gated, b)
                g.tensor_tensor(blk(x, b), blk(x, b), blk(xn, b), ALU.add).then_inc(x1_ready, 1)

            def moe_rstd(b):
                if b >= NB:
                    return
                pool.wait_ge(moe_mean_var, b + 1)
                wait(pool, moe_rstd_ready, b)
                g.tensor_scalar(veps[:, 0:T2], mv[:, 0:T2, 1], EPS_T, None, ALU.add).then_inc(moe_var_eps, 1)
                pool.wait_ge(moe_var_eps, b + 1)
                wait(pool, moe_normed, b)
                g.tensor_tensor(rstd[:, 0:T2], veps[:, 0:T2], neg_half[:, 0:T2], ALU.pow).then_inc(moe_rstd_ready, 1)

            def moe_sub(b):
                if b >= NB:
                    return
                pool.wait_ge(moe_normed, b)
                g.tensor_tensor(xc[:, :, :], blk(x, b), rep(mv[:, 0:T2, 0].rearrange("p (n o) -> p n o", o=1), 2, C),
                                ALU.subtract).then_inc(moe_centred, 1)

            def moe_mult(b):
                if b >= NB:
                    return
                pool.wait_ge(moe_centred, b + 1)
                pool.wait_ge(moe_rstd_ready, b + 1)
                pool.wait_ge(moe_high, b - 1)
                pool.wait_ge(moe_low_ready, b - 1)
                pool.wait_ge(moe_residual, b - 1)
                g.tensor_tensor(xnb[:, b % 2], xc[:, :, :], rep(rstd[:, 0:T2].rearrange("p (n o) -> p n o", o=1), 2, C),
                                ALU.mult).then_inc(moe_normed, 1)

            def moe_low(b):
                if b >= NB:
                    return
                pool.wait_ge(moe_high, b + 1)
                g.tensor_tensor(hl[:, :, 1, :], xnb[:, b % 2], hl[:, :, 0, :].bitcast(F32), ALU.subtract).then_inc(moe_low_ready, 1)
                g.tensor_tensor(blk(x, b), blk(x, b), xnb[:, b % 2], ALU.add).then_inc(moe_residual, 1)

            moe_x1(1)
            moe_rstd(0)
            moe_low(0)
            moe_rstd(1)
            moe_x1(2)
            moe_low(1)
            moe_rstd(2)
            moe_mult(2)
            moe_x1(3)
            for b in range(NB):
                moe_x1(b + 4)
                moe_low(b + 2)
                moe_rstd(b + 3)
                moe_sub(b + 3)
                moe_mult(b + 3)

            def mix_rstd(g_):
                sl = slots(g_)
                pool.wait_ge(mix_mean_var, g_ + 1)
                wait(pool, mix_rstd_ready, g_)
                if g_ == 0:
                    pool.wait_ge(moe_rstd_ready, NB)
                g.tensor_tensor(veps[:, sl], mv[:, sl, 1], eps_vec[:, sl], ALU.add).then_inc(mix_var_eps, 1)
                pool.wait_ge(mix_var_eps, g_ + 1)
                wait(pool, mix_normed, g_ - 1)
                g.tensor_tensor(rstdc[:, g_ % 2, sl], veps[:, sl], neg_half[:, sl], ALU.pow).then_inc(mix_rstd_ready, 1)

            def mix_low(g_):
                sl = slots(g_)
                pool.wait_ge(mix_high_ready, g_ + 1)
                g.tensor_tensor(hlc[:, g_ % 2, sl, 1, :], xnc[:, g_ % 2, sl], hlc[:, g_ % 2, sl, 0, :].bitcast(F32),
                                ALU.subtract).then_inc(mix_low_ready, 1)

            mix_rstd(0)
            mix_low(0)
            mix_rstd(1)
            for g_ in range(2, NM + 1):
                if g_ < NM:
                    mix_rstd(g_)
                if g_ - 1 < NM - 1:
                    mix_low(g_ - 1)
                if LAG <= g_ - 1 < NM - 2:
                    wait(pool, batch_sum, g_ - 1 - LAG)
                    pool.wait_ge(mix_normed, g_)
                    g.tensor_tensor(fsum[:, :, :], fsum[:, :, :], xnc[:, (g_ - 1) % 2, T2:2 * T2], ALU.add).then_inc(batch_sum, 1)

            pool.wait_ge(rt_vector, R_CTAB)
            ct = rep(ctab[:, :].rearrange("p (o n) -> p o n", o=1), 1, 2)
            with g.Fori(0, NB) as b:
                g.tensor_tensor(x[:, bass.ds(2 * b, 2), :], x[:, bass.ds(2 * b, 2), :], ct, ALU.add).then_inc(const_added, 1)

        @block.vector
        def _(dve):
            v = nc.vector

            def over(col, n, c=C):
                return rep(col.rearrange("p (n o) -> p n o", o=1), 2, c)

            v.memset(z_own[:, :, :], 0.0).then_inc(own_zero, 1)
            v.memset(b2sel[:, :, :, :], 0.0).then_inc(own_zero, 1)

            def tok_stats(gr):
                dve.wait_ge(x_in[gr] if gr else x_first[0], 16)
                xg = x[:, GP * gr:GP * (gr + 1), :].rearrange("p i (t c) -> p (i t) c", c=C)
                wait(dve, tok_mean_var, gr)
                for t in range(16):
                    if gr == 0 and t == 8:
                        dve.wait_ge(x_first[1], 16)
                    last = v.bn_stats(stats[:, t, :], xg[:, t, :])
                last.then_inc(tok_stats_taken, 1)
                dve.wait_ge(tok_stats_taken, gr + 1)
                wait(dve, tok_var_eps, gr - 1)
                wait(dve, tok_centred, gr - 1)
                for t in range(16):
                    last = v.bn_aggr(mv2[:, gr % 2, t, :], stats[:, t, :])
                last.then_inc(tok_mean_var, 1)

            def tok_sub(gr):
                xg = x[:, GP * gr:GP * (gr + 1), :].rearrange("p i (t c) -> p (i t) c", c=C)
                ng = xn[:, GP * gr:GP * (gr + 1), :].rearrange("p i (t c) -> p (i t) c", c=C)
                dve.wait_ge(tok_mean_var, gr + 1)
                v.tensor_tensor(ng, xg, over(mv2[:, gr % 2, :, 0], 16), ALU.subtract).then_inc(tok_centred, 1)

            def tok_mult(gr):
                ng = xn[:, GP * gr:GP * (gr + 1), :].rearrange("p i (t c) -> p (i t) c", c=C)
                dve.wait_ge(tok_centred, gr + 1)
                dve.wait_ge(tok_rstd_ready, gr + 1)
                v.tensor_tensor(ng, ng, over(rstd[:, :], 16), ALU.mult).then_inc(tok_normed, 1)
                dve.wait_ge(tok_normed, gr + 1)
                wait(dve, row_mean, gr)
                v.tensor_reduce(rsum[:, :], xn[:, GP * gr:GP * (gr + 1), :], AX.X, ALU.add).then_inc(row_sum, 1)
                dve.wait_ge(row_sum, gr + 1)
                wait(dve, rows_centred, gr - 1)
                v.tensor_scalar(rmean[:, gr % 2, :], rsum[:, :], 1.0 / M, None, ALU.mult).then_inc(row_mean, 1)

            def cov(gr):
                dve.wait_ge(trace_done, gr + 1)
                gs = slice(GP * gr, GP * (gr + 1))
                v.reciprocal(rtrace[:, gs], bank[7][:, gs]).then_inc(trace_read, 1)
                v.tensor_scalar(trm[:, gs], bank[7][:, gs], 1.0 / M, None, ALU.mult).then_inc(trace_all if gr == NG - 1 else trace_read, 1)
                dve.wait_ge(trace_read, 2 * gr + 1)
                dve.wait_ge(gram_done, gr + 1)
                for j in range(2):
                    gram = bank[GRAM_BANK[gr]][halves(j), :].rearrange("p (i n) -> p i n", n=P)[:, :, halves(j)]
                    last = v.tensor_tensor(Ac[halves(j), gs, :], gram, over(rtrace[halves(j), gs], GP), ALU.mult)
                last.then_inc(A_ready, 1)
                dve.wait_ge(A_ready, gr + 1)
                v.scalar_tensor_tensor(out=YZ[:, gs, 1, :], in0=Ac[:, gs, :], scalar=-0.5, in1=rep(two_ident15[:, :].rearrange("p (o n) -> p o n", o=1), 1, GP),
                                       op0=ALU.mult, op1=ALU.add).then_inc(Z0_ready, 1)

            def diagonals(n):
                gr = ns_group(n)
                dve.wait_ge(ns_YZ_copied, n + 1)
                for j in range(2):
                    last = v.tensor_copy(on_diag(Zd, gr, j), YZ[halves(j), GP * gr:GP * (gr + 1), 1, :])
                last.then_inc(ns_Z_on_diag, 1)

            def row_sums(gr):
                gs = slice(GP * gr, GP * (gr + 1))
                dve.wait_ge(ns_YZ_copied, STEPS * (gr // 2) + STEPS - 1 + gr % 2)
                v.tensor_reduce(u_sum[:, gs], YZ[:, gs, 0, :], AX.X, ALU.add).then_inc(u_summed, 1)
                dve.wait_ge(u_summed, gr + 1)
                own = rep(same_img[:, 0:P:C].rearrange("p (o n) -> p o n", o=1), 1, GP)
                v.tensor_tensor(u_own[:, gs, :], over(u_sum[:, gs], GP, 2), own, ALU.mult).then_inc(u_split, 1)
            def moe_stat(b, t):
                if b >= NB:
                    return
                if t == 0:
                    wait(dve, x1_ready, b)
                    wait(dve, moe_mean_var, b)
                v.bn_stats(stats[:, t, :], blk(x, b)[:, t, :]).then_inc(moe_slot_stats, 1)

            def moe_aggr(b):
                dve.wait_ge(moe_slot_stats, T2 * (b + 1))
                wait(dve, moe_var_eps, b)
                wait(dve, moe_centred, b)
                for t in range(T2):
                    last = v.bn_aggr(mv[:, t, :], stats[:, t, :])
                last.then_inc(moe_mean_var, 1)

            def moe_stats(b):
                for t in range(T2):
                    moe_stat(b, t)
                moe_aggr(b)

            def moe_sub(b):
                dve.wait_ge(moe_mean_var, b + 1)
                wait(dve, moe_normed, b)
                v.tensor_tensor(xc[:, :, :], blk(x, b), over(mv[:, 0:T2, 0], T2), ALU.subtract).then_inc(moe_centred, 1)

            def moe_mult(b):
                u = b % 2
                dve.wait_ge(moe_rstd_ready, b + 1)
                dve.wait_ge(moe_centred, b + 1)
                wait(dve, moe_residual, b - 1)
                wait(dve, moe_low_ready, b - 1)
                wait(dve, moe_high, b - 1)
                v.tensor_tensor(xnb[:, u], xc[:, :, :], over(rstd[:, 0:T2], T2), ALU.mult).then_inc(moe_normed, 1)

            ROUTE = 19

            def route(b, part):
                base = ROUTE * b
                mx = lambda i: m12[:, i, :]
                rk = rep(rank[:, :].rearrange("p (o e) -> p o e", o=1), 1, T2)
                TT = v.tensor_tensor

                def largest(values, m, onehot, n, slot=None):
                    v.tensor_reduce(mx(m), values, AX.X, ALU.max).then_inc(route_step, 1)
                    if slot is not None and b:
                        moe_stat(b + 2, slot)
                    dve.wait_ge(route_step, base + n + 1)
                    TT(onehot, values, over(mx(m), T2, E), ALU.is_equal).then_inc(route_step, 1)

                def first_of(onehot, n, slot):
                    dve.wait_ge(route_step, base + n)
                    TT(onehot, onehot, rk, ALU.mult).then_inc(route_step, 1)
                    if b:
                        moe_stat(b + 2, slot)
                    dve.wait_ge(route_step, base + n + 1)
                    v.tensor_reduce(mx(7), onehot, AX.X, ALU.max).then_inc(route_step, 1)
                    if b:
                        moe_stat(b + 2, slot + 1)
                    dve.wait_ge(route_step, base + n + 2)
                    TT(onehot, onehot, over(mx(7), T2, E), ALU.is_equal).then_inc(route_step, 1)

                if part == 0:
                    dve.wait_ge(logits_done, 2 * b + 2)
                    for q in range(2):
                        lq = bank[6 + q][:, 0:T * 2 * E].rearrange("p (t s e) -> p t e s", t=T, s=2)
                        v.tensor_reduce(lg[:, T * q:T * (q + 1), :], lq, AX.X, ALU.add).then_inc(route_step, 1)
                    dve.wait_ge(route_step, base + 2)
                    largest(lg[:, :, :], 0, one1[:, :, :], 2)
                if part == 1:
                    first_of(one1[:, :, :], 4, 0)
                if part == 2:
                    dve.wait_ge(route_step, base + 7)
                    v.scalar_tensor_tensor(out=tmp[:, :, :], in0=one1[:, :, :], scalar=-3.0e38, in1=lg[:, :, :],
                                           op0=ALU.mult, op1=ALU.add).then_inc(route_step, 1)
                    if b:
                        moe_stat(b + 2, 2)
                    dve.wait_ge(route_step, base + 8)
                    largest(tmp[:, :, :], 1, one2[:, :, :], 8, 3)
                if part == 3:
                    TT(mx(2), mx(1), mx(0), ALU.subtract).then_inc(route_step, 1)
                    first_of(one2[:, :, :], 11, 4)
                if part == 4:
                    dve.wait_ge(route_tanh, b + 1)
                    v.tensor_scalar(mx(4), mx(3), 0.5, 0.5, ALU.mult, ALU.add).then_inc(route_step, 1)
                    v.tensor_scalar(mx(5), mx(3), -0.5, 0.5, ALU.mult, ALU.add).then_inc(route_step, 1)
                    dve.wait_ge(route_step, base + 16)
                    TT(one1[:, :, :], one1[:, :, :], over(mx(5), T2, E), ALU.mult).then_inc(route_step, 1)
                    TT(one2[:, :, :], one2[:, :, :], over(mx(4), T2, E), ALU.mult).then_inc(route_step, 1)
                    if b:
                        moe_stat(b + 2, 6)
                    dve.wait_ge(route_step, base + 18)
                    wait(dve, weights_split, 2 * b)
                    TT(cw[:, :, :], one1[:, :, :], one2[:, :, :], ALU.add).then_inc(route_step, 1)
                    dve.wait_ge(route_step, base + 19)
                    wait(dve, weights_T, 2 * b)
                    v.tensor_copy(chl[:, :, 0, :], cw[:, :, :]).then_inc(weights_split, 1)
                    if b:
                        moe_stat(b + 2, 7)
                    dve.wait_ge(weights_split, 2 * b + 1)
                    v.tensor_tensor(chl[:, :, 1, :], cw[:, :, :], chl[:, :, 0, :].bitcast(F32), ALU.subtract).then_inc(weights_split, 1)

            def moe_add(b, q):
                dve.wait_ge(moe_y_back, 2 * b + q + 1)
                dve.wait_ge(moe_residual, b + 1)
                i = 2 * b + q
                v.tensor_tensor(x[:, i, :], x[:, i, :], bank[4 + q][:, 2 * P:4 * P], ALU.add).then_inc(moe_added, 1)

            def moe_scale(b, n):
                N = 8 * b + n
                dve.wait_ge(weights_spread, N + 1)
                dve.wait_ge(hidden_gelu, N + 1)
                wait(dve, second_done, N - 1)
                v.tensor_tensor(scaled[:, n % 2, :], act[:, n % 2, :], bank[2 + n % 2][:, :], ALU.mult).then_inc(hidden_scaled, 1)

            def mix_parts(g_):
                parts = []
                if g_ < NB:
                    parts.append((g_, 0))
                if g_ >= LAG:
                    parts.append((g_ - LAG, T2))
                return parts

            def mix_stat(g_, part):
                b, s0 = (g_ - LAG, T2) if part else (g_, 0)
                if not 0 <= b < NB:
                    return
                wait(dve, mix_mean_var, g_)
                if g_ == 0:
                    dve.wait_ge(moe_mean_var, NB)
                if part:
                    dve.wait_ge(mix_added, 2 * b + 2)
                else:
                    dve.wait_ge(moe_added, 2 * b + 2)
                for t in range(T2):
                    last = v.bn_stats(stats[:, s0 + t, :], blk(x, b)[:, t, :])
                last.then_inc(mix_slot_stats, 1)

            def mix_aggr(g_):
                dve.wait_ge(mix_slot_stats, min(g_ + 1, NB) + max(g_ + 1 - LAG, 0))
                if g_ == 0:
                    dve.wait_ge(moe_var_eps, NB)
                    dve.wait_ge(moe_centred, NB)
                wait(dve, mix_var_eps, g_)
                wait(dve, mix_centred, g_)
                for b, s0 in mix_parts(g_):
                    for t in range(T2):
                        last = v.bn_aggr(mv[:, s0 + t, :], stats[:, s0 + t, :])
                last.then_inc(mix_mean_var, 1)

            def mix_stats(g_):
                mix_stat(g_, 0)
                mix_aggr(g_)

            def mix_sub(g_):
                dve.wait_ge(mix_mean_var, g_ + 1)
                wait(dve, mix_normed, g_)
                for b, s0 in mix_parts(g_):
                    last = v.tensor_tensor(xcn[:, s0:s0 + T2], blk(x, b), over(mv[:, s0:s0 + T2, 0], T2), ALU.subtract)
                last.then_inc(mix_centred, 1)

            def mix_mult(g_):
                sl = slots(g_)
                dve.wait_ge(mix_centred, g_ + 1)
                dve.wait_ge(mix_rstd_ready, g_ + 1)
                wait(dve, mix_low_ready, g_ - 1)
                wait(dve, mix_high_ready, g_ - 1)
                wait(dve, batch_sum, g_ - 1 - LAG)
                v.tensor_tensor(xnc[:, g_ % 2, sl], xcn[:, sl], over(rstdc[:, g_ % 2, sl], sl.stop - sl.start), ALU.mult).then_inc(mix_normed, 1)

            def mix_add(b, q):
                i = 2 * b + q
                dve.wait_ge(mix_back_done, i + 1)
                v.tensor_tensor(x[:, i, :], x[:, i, :], bank[4 + q][:, 0:T * C], ALU.add).then_inc(mix_added, 1)


            def ns_t(n):
                gr = ns_group(n)
                dve.wait_ge(ns_ZY, n + 1)
                for j in range(2):
                    p = bank[gr % 2][halves(j), 0:GP * C].rearrange("p (i c) -> p i c", c=C)
                    i15 = rep(two_ident15[halves(j), :].rearrange("p (o n) -> p o n", o=1), 1, GP)
                    last = v.scalar_tensor_tensor(out=on_diag(Td, gr, j), in0=p, scalar=-0.5, in1=i15, op0=ALU.mult, op1=ALU.add)
                last.then_inc(ns_T_ready, 1)

            def y_terms(h):
                hs = slice(HP * h, HP * (h + 1))
                dve.wait_ge(u_summed, 2 * h + 2)
                for j in range(2):
                    v.tensor_scalar(yv[:, 1, hs, j], u_sum[halves(j), hs], 1.5 / C, None, ALU.mult).then_inc(y_terms_ready, 1)
                dve.wait_ge(root_trace, 1)
                for j in range(2):
                    v.tensor_copy(yv[:, 0, hs, j], root[halves(j), hs]).then_inc(y_terms_ready, 1)

            def z_columns(h):
                hs = slice(HP * h, HP * (h + 1))
                dve.wait_ge(zu_done, h + 1)
                for j in range(2):
                    c0 = COL_ZU + 2 * HP * h + j
                    v.tensor_copy(z_own[halves(j), hs, j], bank[4][0:C, c0:c0 + 2 * HP - 1:2]).then_inc(zu_split, 1)

            def y_final(h):
                cs_ = slice(2 * HP * h, 2 * HP * (h + 1))
                yf = yv[:, :, :, :].rearrange("p k i j -> p k (i j)")
                dve.wait_ge(yzu_done, h + 1)
                dve.wait_ge(y_terms_ready, 4 * h + 4)
                v.scalar_tensor_tensor(out=yf[:, 2, cs_], in0=bank[4][0:C, COL_W + 2 * HP * h:COL_W + 2 * HP * (h + 1)],
                                       scalar=-0.5 / C, in1=yf[:, 1, cs_], op0=ALU.mult, op1=ALU.add).then_inc(y_ready, 1)
                dve.wait_ge(y_ready, 2 * h + 1)
                v.tensor_tensor(yf[:, 3, cs_], yf[:, 2, cs_], yf[:, 0, cs_], ALU.mult).then_inc(y_ready, 1)

            def gate_rows(h):
                hs = slice(HP * h, HP * (h + 1))
                dve.wait_ge(conv2_tanh, h + 1)
                for j in range(2):
                    v.tensor_scalar(gsig[halves(j), hs], g2[:, hs, j], 0.5, 0.5, ALU.mult, ALU.add).then_inc(gate_rows_ready, 1)
                dve.wait_ge(gate_rows_ready, 3 * h + 2)
                v.tensor_tensor(gspread[:, hs, :], over(gsig[:, hs], HP), rep(two_ident[:, :].rearrange("p (o c) -> p o c", o=1), 1, HP),
                                ALU.mult).then_inc(gate_rows_ready, 1)

            tok_stats(0)
            tok_sub(0)
            tok_stats(1)
            tok_mult(0)
            tok_sub(1)
            tok_stats(2)
            tok_mult(1)
            tok_sub(2)
            cov(0)
            tok_mult(2)
            tok_stats(3)
            tok_sub(3)
            cov(1)
            tok_mult(3)
            cov(2)
            dve.wait_ge(diag_zero, 2)
            dve.wait_ge(own_zero, 2)
            ns_t(0)
            ns_t(1)
            diagonals(0)
            diagonals(1)
            ns_t(2)
            ns_t(3)
            cov(3)
            diagonals(2)
            diagonals(3)
            ns_t(4)
            ns_t(5)
            dve.wait_ge(vecs_ready, 1)
            v.tensor_copy(cols[:, :], bank[4][:, COL_VECS:COL_VECS + NROWS]).then_inc(cols_ready, 1)
            dve.wait_ge(cols_ready, 1)
            v.tensor_scalar(half_gb2[:, :], cols[0:C, ROW_GB2:ROW_GB2 + 1], 0.5, None, ALU.mult).then_inc(cols_ready, 1)
            row_sums(0)
            row_sums(1)
            ns_t(6)
            y_terms(0)
            z_columns(0)
            ns_t(7)
            diagonals(6)
            y_final(0)
            diagonals(7)
            ns_t(8)
            ns_t(9)
            diagonals(8)
            gate_rows(0)
            diagonals(9)
            ns_t(10)
            ns_t(11)
            dve.wait_ge(bn_step, 11)
            for half in range(2):
                flat = b2sel[halves(half), :, :, :].rearrange("p k s e -> p (k s e)")
                step = 2 * E + 2
                for part in range(2):
                    first = E * part + half
                    v.tensor_copy(flat[:, first:first + (KP - 1) * step + 1:step], bn2[halves(half), 1, :]).then_inc(b2_sel, 1)
            dve.wait_ge(gate_ready, 1)
            gx = blk(xn, 0).rearrange("p (i t) c -> p i t c", t=T)
            gb = rep(gate[:, 0:2, :].rearrange("p i (o c) -> p i o c", o=1), 2, T)
            v.tensor_tensor(gx, gx, gb, ALU.mult).then_inc(first_x1, 1)
            dve.wait_ge(first_x1, 1)
            v.tensor_tensor(blk(x, 0), blk(x, 0), blk(xn, 0), ALU.add).then_inc(first_x1, 1)
            dve.wait_ge(first_x1, 2)
            moe_stats(0)
            moe_sub(0)
            row_sums(2)
            row_sums(3)
            dve.wait_ge(s2_spread, 1)
            dve.wait_ge(w_ffn, W_FFN)
            v.tensor_tensor(f2[:, :, :], f2[:, :, :], bank[6][:, :].rearrange("p (k n) -> p k n", n=P), ALU.mult).then_inc(f2_scaled, 1)
            dve.wait_ge(conv_vs, 1)
            v8 = bank[7][:, :].rearrange("p (d o) -> p d o", d=8)
            v.tensor_tensor(vconv[:, :, 1, :], v8, vconv[:, :, 0, :].bitcast(F32), ALU.subtract).then_inc(conv_vs, 1)
            y_terms(1)
            z_columns(1)
            moe_mult(0)
            y_final(1)
            moe_stats(1)
            moe_sub(1)
            moe_mult(1)
            gate_rows(1)
            for part in range(5):
                route(0, part)
            moe_stats(2)
            moe_sub(2)
            for b in range(NB):
                more, more2, more3 = b + 1 < NB, b + 2 < NB, b + 3 < NB
                if not more:
                    break
                moe_scale(b, 0)
                if b:
                    moe_add(b - 1, 0)
                moe_scale(b, 1)
                if more:
                    route(b + 1, 0)
                moe_scale(b, 2)
                if more:
                    route(b + 1, 1)
                moe_scale(b, 3)
                if more:
                    route(b + 1, 2)
                moe_scale(b, 4)
                if b:
                    moe_add(b - 1, 1)
                if more:
                    route(b + 1, 3)
                moe_scale(b, 5)
                if more:
                    route(b + 1, 4)
                moe_scale(b, 6)
                if more3:
                    moe_aggr(b + 3)
                moe_scale(b, 7)
                if b == NB - 2:
                    mix_stats(0)
                    mix_sub(0)
            b = NB - 1
            moe_scale(b, 0)
            moe_add(b - 1, 0)
            moe_scale(b, 1)
            mix_mult(0)
            moe_scale(b, 2)
            mix_stats(1)
            moe_scale(b, 3)
            moe_add(b - 1, 1)
            mix_sub(1)
            moe_scale(b, 4)
            mix_mult(1)
            moe_scale(b, 5)
            mix_stats(2)
            moe_scale(b, 6)
            mix_sub(2)
            moe_scale(b, 7)
            moe_add(b, 0)
            moe_add(b, 1)

            for b in range(NM - 2):
                mix_stat(b + 3, 0)
                if 1 <= b <= NB:
                    mix_add(b - 1, 0)
                    mix_add(b - 1, 1)
                mix_stat(b + 3, 1)
                if b + 3 < NM:
                    mix_aggr(b + 3)
                mix_mult(b + 2)
                if b + 3 < NM:
                    mix_sub(b + 3)
            dve.wait_ge(mix_high_ready, NM)
            sl, u = slots(NM - 1), (NM - 1) % 2
            v.tensor_tensor(hlc[:, u, sl, 1, :], xnc[:, u, sl], hlc[:, u, sl, 0, :].bitcast(F32), ALU.subtract).then_inc(mix_low_last, 1)

            def rstep(n, ins):
                ins.then_inc(rt_vector, 1)
            dve.wait_ge(rt_tensor, 2)
            rstep(R_FEAT, v.tensor_copy(feat[:, :, :].rearrange("p t c -> p (t c)"), bank[0][:, 0:T * C]))
            dve.wait_ge(rt_tensor, 3)
            rstep(R_FEATT, v.tensor_copy(featT[:, :], bank[1][0:C, :]))
            dve.wait_ge(rt_logits, 1)
            brb = rep(br[:, :].rearrange("p (o e) -> p o e", o=1), 1, T)
            rstep(R_LOG, v.tensor_tensor(fl[:, 0], bank[0][:, 0:T * E].rearrange("p (t e) -> p t e", t=T), brb, ALU.add))
            dve.wait_ge(rt_vector, R_LOG)
            rstep(R_MAX, v.tensor_reduce(fm[:, 0, :], fl[:, 0], AX.X, ALU.max))
            dve.wait_ge(rt_vector, R_MAX)
            rstep(R_SUB, v.tensor_tensor(fl[:, 1], fl[:, 0], over(fm[:, 0, :], T, E), ALU.subtract))
            dve.wait_ge(rt_scalar, 1)
            rstep(R_SUM, v.tensor_reduce(fm[:, 1, :], fl[:, 2], AX.X, ALU.add))
            dve.wait_ge(rt_vector, R_SUM)
            rstep(R_REC, v.reciprocal(fm[:, 2, :], fm[:, 1, :]))
            dve.wait_ge(rt_vector, R_REC)
            rstep(R_W, v.tensor_tensor(fl[:, 3], fl[:, 2], over(fm[:, 2, :], T, E), ALU.mult))
            dve.wait_ge(rt_vector, R_W)
            rstep(R_WH, v.tensor_copy(whl[:, :, 0, :], fl[:, 3]))
            dve.wait_ge(rt_vector, R_WH)
            rstep(R_WL, v.tensor_tensor(whl[:, :, 1, :], fl[:, 3], whl[:, :, 0, :].bitcast(F32), ALU.subtract))
            rstep(R_U16, v.tensor_tensor(u16[:, :], bank[4][0:2 * E, 0:C], bo[:, :], ALU.add))
            dve.wait_ge(rt_spread, 1)
            v.tensor_copy(wspread[:, 0, :], bank[0][:, :]).then_inc(rt_copied_vector, 1)

            def ffn_scale(b, n):
                k = n % KP
                dve.wait_ge(layer2_done, 8 * b + n + 1)
                wait(dve, layer3_done, 8 * b + n - 1)
                v.scalar_tensor_tensor(out=scaled[:, n % 2, :], in0=bank[2 + n % 2][:, :], scalar=bn2[:, 2, k:k + 1],
                                       in1=wspread[:, k, :], op0=ALU.max, op1=ALU.mult).then_inc(layer2_scaled, 1)

            def ffn_add(b, q):
                dve.wait_ge(ffn_y_back, 2 * b + q + 1)
                dve.wait_ge(const_added, b + 1)
                xi = x[:, bass.ds(2 * b + q, 1), :].rearrange("p o n -> p (o n)")
                v.tensor_tensor(xi, xi, bank[4 + q][:, 2 * P:4 * P], ALU.add).then_inc(ffn_added, 1)

            dve.wait_ge(rt_copied_vector, 1)
            ffn_scale(0, 0)
            dve.wait_ge(rt_copied_scalar, 1)
            ffn_scale(0, 1)
            dve.wait_ge(rt_spread, 3)
            v.tensor_copy(wspread[:, 2, :], bank[0][:, :]).then_inc(rt_copied_vector, 1)
            dve.wait_ge(rt_tensor, 5)
            rstep(R_CTAB, v.tensor_copy(ctab[:, :], bank[5][:, 0:T * C]))
            dve.wait_ge(rt_copied_vector, 2)
            ffn_scale(0, 2)
            dve.wait_ge(rt_copied_scalar, 2)
            for n in range(3, 8):
                ffn_scale(0, n)
            ffn_add(0, 0)
            with v.Fori(1, NB) as b:
                for n in range(8):
                    ffn_scale(b, n)
                    if n == 3:
                        ffn_add(b + -1, 1)
                ffn_add(b, 0)
            ffn_add(NB - 1, 1)

        @block.scalar
        def _(act_e):
            s = nc.scalar
            def z_diagonals(gr):
                act_e.wait_ge(Z0_ready, gr + 1)
                act_e.wait_ge(diag_zero, 1)
                for j in range(2):
                    last = s.activation(on_diag(Zd, gr, j), YZ[halves(j), GP * gr:GP * (gr + 1), 1, :], ACT.Copy)
                last.then_inc(Z0_on_diag, 1)

            def first_y(gr):
                act_e.wait_ge(Y0_done, gr + 1)
                s.activation(YZ[:, GP * gr:GP * (gr + 1), 0, :], bank[Y0_BANK[gr]][:, 0:GP * C].rearrange("p (i c) -> p i c", c=C),
                             ACT.Copy).then_inc(Y0_copied, 1)

            def squares_and_rows(gr):
                act_e.wait_ge(rows_centred, gr + 1)
                for i in range(GP):
                    if gr or i:
                        act_e.wait_ge(row_squares, GP * gr + i)
                    s.activation(sqj[:, :], xcc[gr % 2][:, i, :], ACT.Square,
                                 accum_out=sumsq[:, GP * gr + i:GP * gr + i + 1]).then_inc(row_squares, 1)
                for c in range(2):
                    act_e.wait_ge(rows_T, 2 * gr + c + 1)
                    wait(act_e, gram_done, gr)
                    s.activation(xT[:, c, :], bank[4 + c][:, :], ACT.Copy).then_inc(rows_T_copied, 1)

            def ns_copy(n):
                gr = ns_group(n)
                act_e.wait_ge(ns_TYTZ, n + 1)
                s.activation(YZ[:, GP * gr:GP * (gr + 1), :, :].rearrange("p i s c -> p (i s c)"), bank[2 + gr % 2][:, :],
                             ACT.Copy).then_inc(ns_YZ_copied, 1)

            def gate_relu(h):
                cs_ = slice(2 * HP * h, 2 * HP * (h + 1))
                act_e.wait_ge(conv1_done, h + 1)
                s.activation(g1[:, cs_], bank[4][0:C, COL_C1 + 2 * HP * h:COL_C1 + 2 * HP * (h + 1)], ACT.Relu,
                             bias=cols[0:C, ROW_GB1:ROW_GB1 + 1]).then_inc(conv1_relu, 1)

            def gate_tanh(h):
                cs_ = slice(2 * HP * h, 2 * HP * (h + 1))
                act_e.wait_ge(conv2_done, h + 1)
                act_e.wait_ge(cols_ready, 2)
                s.activation(g2[:, :, :].rearrange("p i j -> p (i j)")[:, cs_], bank[4][0:C, COL_C2 + 2 * HP * h:COL_C2 + 2 * HP * (h + 1)],
                             ACT.Tanh, scale=0.5, bias=half_gb2[:, 0:1]).then_inc(conv2_tanh, 1)

            def gate_out(h):
                act_e.wait_ge(gate_in_psum, h + 1)
                s.activation(gate[:, HP * h:HP * (h + 1), :].rearrange("p i c -> p (i c)"), bank[5][:, :], ACT.Copy).then_inc(gate_ready, 1)

            squares_and_rows(0)
            squares_and_rows(1)
            z_diagonals(0)
            first_y(0)
            squares_and_rows(2)
            z_diagonals(1)
            first_y(1)
            z_diagonals(2)
            first_y(2)
            ns_copy(0)
            ns_copy(1)
            squares_and_rows(3)
            ns_copy(2)
            ns_copy(3)
            z_diagonals(3)
            first_y(3)
            ns_copy(4)
            ns_copy(5)
            act_e.wait_ge(cols_ready, 1)
            s.activation(router[:, 0, :], cols[:, ROW_ROUTER:NROWS], ACT.Copy).then_inc(w_hi, 1)
            act_e.wait_ge(w_moe, W_MOE)
            s.activation(w1s[:, 0, :], w1f[:, :], ACT.Copy).then_inc(w_hi, 1)
            act_e.wait_ge(w_ffn, W_FFN)
            s.activation(f1s[:, 0, :], f1f[:, :], ACT.Copy).then_inc(w_hi, 1)
            act_e.wait_ge(consts, 30)
            s.activation(sel[:, :, :], sel_f[:, :, :], ACT.Copy).then_inc(w_hi, 1)
            ns_copy(6)
            act_e.wait_ge(conv_wT, 1)
            s.activation(wdT[:, :, 0, :], bank[6][0:C, :].rearrange("p (d c) -> p d c", d=8), ACT.Copy).then_inc(conv_wTs, 1)
            ns_copy(7)
            gate_relu(0)
            s.activation(wdT[:, :, 1, :], bank[6][0:C, :].rearrange("p (d c) -> p d c", d=8), ACT.Copy).then_inc(conv_wTs, 1)
            gate_tanh(0)
            ns_copy(8)
            s.activation(wcT[:, :, :].rearrange("p d c -> p (d c)"), bank[7][0:C, :], ACT.Copy).then_inc(conv_wTs, 1)
            ns_copy(9)
            gate_out(0)
            ns_copy(10)
            ns_copy(11)
            def evac_x(b, q):
                act_e.wait_ge(tok_T, 2 * b + q + 1)
                s.activation(xs[:, b % 2, CH * q:CH * (q + 1)], bank[6 + q][:, :], ACT.Copy).then_inc(tok_T_copied, 1)

            def hi(b, u, s_xn, s_hi, free):
                act_e.wait_ge(s_xn, b + 1)
                for s_used, k in free:
                    wait(act_e, s_used, k)
                s.activation(hl[:, :, 0, :], xnb[:, u], ACT.Copy).then_inc(s_hi, 1)

            def tanh(b):
                act_e.wait_ge(route_step, 19 * b + 12)
                s.activation(m12[:, 3, :], m12[:, 2, :], ACT.Tanh, scale=0.5).then_inc(route_tanh, 1)

            def evac_c(b, q):
                act_e.wait_ge(weights_T, 2 * b + q + 1)
                wait(act_e, weights_spread, 8 * (b - 1) + KP * (q + 1))
                wait(act_e, second_done, 8 * (b - 1) + KP * q + 1)
                s.activation(cs[:, CH * q:CH * (q + 1)], bank[6 + q][:, :], ACT.Copy).then_inc(weights_T_copied, 1)

            def evac_y(b, q):
                act_e.wait_ge(second_done, KP * (2 * b + q + 1))
                wait(act_e, moe_y_back, 2 * b + q - 1)
                s.activation(yTs[:, q, :], bank[4 + q][:, 0:2 * P], ACT.Copy).then_inc(moe_y_copied, 1)

            def gelu(b, n):
                N = 8 * b + n
                act_e.wait_ge(hidden_done, N + 1)
                wait(act_e, hidden_scaled, N - 1)
                s.activation(act[:, n % 2, :], bank[n % 2][:, :], ACT.Gelu, bias=cols[:, n % KP:n % KP + 1]).then_inc(hidden_gelu, 1)

            def mix_high(g_):
                sl = slots(g_)
                act_e.wait_ge(mix_normed, g_ + 1)
                if g_ == 0:
                    act_e.wait_ge(x1_ready, NB - 1)
                wait(act_e, mix_T, 2 * min(g_ - 1, NB))
                wait(act_e, ffn_T, 2 * (g_ - 1 - LAG))
                s.activation(hlc[:, g_ % 2, sl, 0, :], xnc[:, g_ % 2, sl], ACT.Copy).then_inc(mix_high_ready, 1)

            def mix_pad(b, q):
                i = 2 * b + q
                act_e.wait_ge(mix_T, i + 1)
                wait(act_e, conv_done, i - 1)
                src = bank[6 + q][:, :].rearrange("p (t i r w) -> p i r w t", t=T, i=2, r=H)
                for j in range(2):
                    dst = xp[:, 2 * q + j, 1:H + 1, 1:W + 1].rearrange("p r (w t) -> p r w t", t=T)
                    last = s.activation(dst, src[:, j], ACT.Copy)
                last.then_inc(mix_padded, 1)

            def mix_bias(b, q):
                i = 2 * b + q
                act_e.wait_ge(conv_done, i + 1)
                wait(act_e, mix_back_done, i - 1)
                s.activation(cvs[:, q, :], bank[q][:, :], ACT.Identity, bias=cols[:, ROW_BC:ROW_BC + 1]).then_inc(conv_copied, 1)

            def ffn_in(b, q):
                act_e.wait_ge(ffn_T, 2 * b + q + 1)
                s.activation(xs_ffn[:, b, CH * q:CH * (q + 1)], bank[2 + q][:, :], ACT.Copy).then_inc(ffn_T_copied, 1)

            act_e.wait_ge(conv_v, 1)
            s.activation(vconv[:, :, 0, :], bank[7][:, :].rearrange("p (d o) -> p d o", d=8), ACT.Copy).then_inc(conv_vs, 1)
            hi(0, 0, moe_normed, moe_high, [])
            gate_relu(1)
            gate_tanh(1)
            evac_x(0, 0)
            evac_x(0, 1)
            hi(1, 1, moe_normed, moe_high, [(tok_T, 2)])
            gate_out(1)
            tanh(0)
            evac_c(0, 0)
            evac_c(0, 1)
            for b in range(NB):
                more, more2 = b + 1 < NB, b + 2 < NB
                gelu(b, 0)
                if more:
                    evac_x(b + 1, 0)
                    evac_x(b + 1, 1)
                gelu(b, 1)
                gelu(b, 2)
                if b:
                    evac_y(b - 1, 1)
                gelu(b, 3)
                if more2:
                    hi(b + 2, b % 2, moe_normed, moe_high, [(tok_T, 2 * b + 4)])
                if not more:
                    mix_high(0)
                gelu(b, 4)
                gelu(b, 5)
                if more:
                    tanh(b + 1)
                gelu(b, 6)
                evac_y(b, 0)
                gelu(b, 7)
                if more:
                    evac_c(b + 1, 0)
                    evac_c(b + 1, 1)
            act_e.wait_ge(consts_v, 1)
            mix_pad(0, 0)
            mix_high(1)
            evac_y(NB - 1, 1)
            mix_pad(0, 1)

            for b in range(NM - 1):
                if b + 1 < NB:
                    mix_pad(b + 1, 0)
                if 0 <= b < NB:
                    mix_bias(b, 0)
                if 0 <= b < NB:
                    mix_bias(b, 1)
                if b + 2 < NM:
                    mix_high(b + 2)
                if b + 1 < NB:
                    mix_pad(b + 1, 1)
                if b + 2 == NM - 1:
                    s.activation(fm[:, 3, :], neg_half[:, 0:T], ACT.Exp).then_inc(rt_exp_table, 1)
                if b + 1 >= LAG:
                    ffn_in(b + 1 - LAG, 0)
                    ffn_in(b + 1 - LAG, 1)

            def evac_f(b, q):
                act_e.wait_ge(layer3_done, KP * (2 * b + q + 1))
                wait(act_e, ffn_y_back, 2 * b + q - 1)
                s.activation(yTs[:, q, :], bank[4 + q][:, 0:2 * P], ACT.Copy).then_inc(ffn_y_copied, 1)

            def first_relu(b, n):
                k = n % KP
                act_e.wait_ge(layer1_done, 8 * b + n + 1)
                wait(act_e, layer2_done, 8 * b + n - 1)
                s.activation(act[:, n % 2, :], bank[6 + n % 2][:, :], ACT.Relu, scale=bn1[:, 0, k:k + 1],
                             bias=bn1[:, 1, k:k + 1]).then_inc(layer1_relu, 1)

            act_e.wait_ge(bn_step, 11)
            first_relu(0, 0)
            act_e.wait_ge(rt_vector, R_SUB)
            s.activation(fl[:, 2], fl[:, 1], ACT.Exp).then_inc(rt_scalar, 1)
            first_relu(0, 1)
            act_e.wait_ge(rt_tensor, 4)
            s.activation(wT[:, :], bank[1][0:2 * E, :], ACT.Copy).then_inc(rt_scalar, 1)
            for i in range(2):
                act_e.wait_ge(rt_spread, 2 * i + 2)
                s.activation(wspread[:, 2 * i + 1, :], bank[1][:, :], ACT.Copy).then_inc(rt_copied_scalar, 1)
            for n in range(2, 8):
                first_relu(0, n)
                if n == 6:
                    evac_f(0, 0)
            with s.Fori(1, NB) as b:
                for n in range(8):
                    first_relu(b, n)
                    if n == 2:
                        evac_f(b + -1, 1)
                    if n == 6:
                        evac_f(b, 0)
            evac_f(NB - 1, 1)

        @block.tensor
        def _(pe):
            t = nc.tensor
            def rows_out(gr):
                pe.wait_ge(rows_centred, gr + 1)
                wait(pe, rows_T_copied, 2 * gr)
                for c in range(2):
                    for i in range(GP):
                        last = t.transpose(bank[4 + c][:, P * i:P * (i + 1)], xcc[gr % 2][:, i, P * c:P * (c + 1)], ident[:, :])
                    last.then_inc(rows_T, 1)
                pe.wait_ge(row_squares, GP * (gr + 1))
                wait(pe, trace_read, 2 * gr)
                t.matmul(bank[7][:, GP * gr:GP * (gr + 1)], same_img[:, :], sumsq[:, GP * gr:GP * (gr + 1)],
                         start=True, stop=True).then_inc(trace_done, 1)

            def gram(gr):
                pe.wait_ge(rows_T_copied, 2 * gr + 2)
                if gr == 3:
                    pe.wait_ge(Y0_copied, gr)
                for i in range(GP):
                    cs_ = slice(P * i, P * (i + 1))
                    for c in range(2):
                        last = t.matmul(bank[GRAM_BANK[gr]][:, cs_], xT[:, c, cs_], xT[:, c, cs_], start=(c == 0), stop=(c == 1))
                last.then_inc(gram_done, 1)

            def first_product(gr):
                pe.wait_ge(Z0_on_diag, gr + 1)
                for i in range(GP):
                    k = GP * gr + i
                    last = t.matmul(bank[Y0_BANK[gr]][:, C * i:C * (i + 1)], Zd[:, k, :], Ac[:, k, :], start=True, stop=True)
                last.then_inc(Y0_done, 1)

            def prod_p(n):
                gr = ns_group(n)
                pe.wait_ge(Y0_copied, gr + 1)
                if n % STEPS >= 2:
                    pe.wait_ge(ns_YZ_copied, n - 1)
                    pe.wait_ge(ns_Z_on_diag, z_moves(n - 1))
                wait(pe, ns_T_ready, n - 1)
                for i in range(GP):
                    k = GP * gr + i
                    last = t.matmul(bank[gr % 2][:, C * i:C * (i + 1)], Zd[:, k, :], YZ[:, k, 0, :], start=True, stop=True)
                last.then_inc(ns_ZY, 1)

            def prod_yz(n):
                gr = ns_group(n)
                pe.wait_ge(ns_T_ready, n + 1)
                wait(pe, ns_YZ_copied, n - 1)
                for i in range(GP):
                    k = GP * gr + i
                    last = t.matmul(bank[2 + gr % 2][:, P * i:P * (i + 1)], Td[:, k, :],
                                    YZ[:, k, :, :].rearrange("p s c -> p (s c)"), start=True, stop=True)
                last.then_inc(ns_TYTZ, 1)

            def z_times_u(h):
                for i in range(HP * h, HP * (h + 1)):
                    pe.wait_ge(u_split, i // GP + 1)
                    last = t.matmul(bank[4][0:C, COL_ZU + 2 * i:COL_ZU + 2 * i + 2], YZ[:, i, 1, :], u_own[:, i, :], start=True, stop=True)
                last.then_inc(zu_done, 1)

            def y_times_zu(h):
                pe.wait_ge(zu_split, 2 * h + 2)
                for i in range(HP * h, HP * (h + 1)):
                    last = t.matmul(bank[4][0:C, COL_W + 2 * i:COL_W + 2 * i + 2], YZ[:, i, 0, :], z_own[:, i, :], start=True, stop=True)
                last.then_inc(yzu_done, 1)

            def gate_conv1(h):
                pe.wait_ge(y_ready, 2 * h + 2)
                pe.wait_ge(w_gate, W_GATE)
                t.matmul(bank[4][0:C, COL_C1 + 2 * HP * h:COL_C1 + 2 * HP * (h + 1)], gw1[:, :],
                         yv[:, 3, HP * h:HP * (h + 1), :].rearrange("p i j -> p (i j)"), start=True, stop=True).then_inc(conv1_done, 1)

            def gate_conv2(h):
                cs_ = slice(2 * HP * h, 2 * HP * (h + 1))
                pe.wait_ge(conv1_relu, h + 1)
                t.matmul(bank[4][0:C, COL_C2 + 2 * HP * h:COL_C2 + 2 * HP * (h + 1)], gw2[:, :], g1[:, cs_],
                         start=True, stop=True).then_inc(conv2_done, 1)

            def gate_spread(h):
                pe.wait_ge(gate_rows_ready, 3 * h + 3)
                wait(pe, gate_ready, h)
                t.matmul(bank[5][:, :], same_img[:, :], gspread[:, HP * h:HP * (h + 1), :].rearrange("p i c -> p (i c)"),
                         start=True, stop=True).then_inc(gate_in_psum, 1)

            pe.wait_ge(consts, 30)
            rows_out(0)
            gram(0)
            rows_out(1)
            gram(1)
            first_product(0)
            rows_out(2)
            prod_p(0)
            gram(2)
            first_product(1)
            prod_p(1)
            first_product(2)
            prod_yz(0)
            prod_yz(1)
            rows_out(3)
            prod_p(2)
            prod_p(3)
            gram(3)
            prod_yz(2)
            prod_yz(3)
            pe.wait_ge(w_vec, W_VEC)
            pe.wait_ge(rows_T_copied, 2 * NG)
            t.transpose(bank[4][:, COL_VECS:COL_VECS + NROWS], vec_rows[:, :], ident[0:NROWS, 0:NROWS]).then_inc(vecs_ready, 1)
            prod_p(4)
            prod_p(5)
            first_product(3)
            prod_yz(4)
            prod_yz(5)
            prod_p(6)
            prod_p(7)
            prod_yz(6)
            pe.wait_ge(cols_ready, 1)
            z_times_u(0)
            pe.wait_ge(w_conv, W_CONV)
            pe.wait_ge(trace_all, 1)
            for k in range(4):
                t.transpose(bank[6][0:C, P * k:P * (k + 1)], wd[:, k, :], ident[:, :])
            for d in range(8):
                last = t.transpose(bank[7][0:C, C * d:C * (d + 1)], wc[:, d, :], ident[0:C, 0:C])
            last.then_inc(conv_wT, 1)
            prod_yz(7)
            y_times_zu(0)
            prod_p(8)
            gate_conv1(0)
            prod_p(9)
            gate_conv2(0)
            prod_yz(8)
            prod_yz(9)
            gate_spread(0)
            prod_p(10)
            prod_p(11)
            prod_yz(10)
            prod_yz(11)
            pe.wait_ge(bn_step, 10)
            pe.wait_ge(conv_wTs, 3)
            for k in range(KP):
                last = t.transpose(bank[6][:, P * k:P * (k + 1)], rep(bn2[:, 0, k:k + 1], 1, P), ident[:, :])
            last.then_inc(s2_spread, 1)
            for d in range(8):
                last = t.matmul(bank[7][:, C * d:C * (d + 1)],
                                wdT[:, d, :, :].rearrange("p o c -> p (o c)"),
                                wcT[:, d, :], start=True, stop=True)
            last.then_inc(conv_v, 1)
            z_times_u(1)
            y_times_zu(1)

            def moe_x(b, q):
                pe.wait_ge(moe_low_ready, b + 1)
                for j in range(T):
                    last = t.transpose(bank[6 + q][:, P * j:P * (j + 1)],
                                       hl[:, T * q + j, :, :].rearrange("p s c -> p (s c)").bitcast(F32), ident[:, :])
                last.then_inc(tok_T, 1)

            def moe_logits(b, q):
                pe.wait_ge(tok_T_copied, 2 * b + q + 1)
                for j in range(T):
                    last = t.matmul(bank[6 + q][:, 2 * E * j:2 * E * (j + 1)],
                                    xs[:, b % 2, CH * q + P * j:CH * q + P * (j + 1)],
                                    router[:, :, :].rearrange("p s e -> p (s e)"), start=True, stop=True)
                last.then_inc(logits_done, 1)

            def moe_c(b, q):
                pe.wait_ge(weights_split, 2 * b + 2)
                for j in range(T):
                    last = t.transpose(bank[6 + q][:, P * j:P * (j + 1)],
                                       chl[:, T * q + j, :, :].rearrange("p s e -> p (s e)").bitcast(F32), ident[:, :])
                last.then_inc(weights_T, 1)

            def moe_first(b, n):
                N, q, k = 8 * b + n, n // KP, n % KP
                wait(pe, hidden_gelu, N - 1)
                for part in range(2):
                    last = t.matmul(bank[n % 2][:, :], w1s[:, part, P * k:P * (k + 1)], xs[:, b % 2, CH * q:CH * (q + 1)],
                                    start=(part == 0), stop=(part == 1))
                last.then_inc(hidden_done, 1)
                wait(pe, hidden_scaled, N - 1)
                pe.wait_ge(weights_T_copied, 2 * b + q + 1)
                t.matmul(bank[2 + n % 2][:, :], sel[:, k, :], cs[:, CH * q:CH * (q + 1)], start=True, stop=True).then_inc(weights_spread, 1)

            def moe_second(b, n):
                N, q, k = 8 * b + n, n // KP, n % KP
                if k == 0:
                    wait(pe, moe_y_copied, 2 * b + q - 1)
                    wait(pe, moe_added, 2 * b + q - 1)
                    for half in range(2):
                        t.matmul(bank[4 + q][C * half:C * (half + 1), 0:2 * P], b2rows[:, :],
                                 cs[:, CH * q + 2 * P * half:CH * q + 2 * P * (half + 1)].bitcast(F32), start=True, stop=False)
                pe.wait_ge(hidden_scaled, N + 1)
                for half in range(2):
                    last = t.matmul(bank[4 + q][C * half:C * (half + 1), 0:2 * P], w2[:, k, :],
                                    scaled[:, n % 2, 2 * P * half:2 * P * (half + 1)], start=False, stop=(k == KP - 1))
                last.then_inc(second_done, 1)

            def back(yt, s_yT, s_yo, b, q):
                pe.wait_ge(s_yT, 2 * b + q + 1)
                o = bank[4 + q][:, 2 * P:4 * P].rearrange("p (h j c) -> p j h c", h=2, j=2)
                for j in range(2):
                    last = t.transpose(o[:, j], yt[:, q, P * j:P * (j + 1)], ident[:, :])
                last.then_inc(s_yo, 1)

            def mix_x(g_, part, q):
                if g_ == NM - 1:
                    pe.wait_ge(mix_low_last, 1)
                else:
                    pe.wait_ge(mix_low_ready, g_ + 1)
                if part == 0:
                    wait(pe, mix_padded, 2 * g_ + q - 1)
                else:
                    wait(pe, ffn_T_copied, 2 * (g_ - LAG) + q - 1)
                for j in range(T):
                    last = t.transpose(bank[(2 if part else 6) + q][:, P * j:P * (j + 1)],
                                       hlc[:, g_ % 2, T2 * part + T * q + j, :, :].rearrange("p s c -> p (s c)").bitcast(F32), ident[:, :])
                last.then_inc(ffn_T if part else mix_T, 1)

            def mix_conv(b, q):
                i = 2 * b + q
                pe.wait_ge(mix_padded, i + 1)
                wait(pe, conv_copied, i - 1)
                for d, (dx, dy) in enumerate(DIRECTIONS):
                    src = xp[:, 2 * q:2 * q + 2, 1 - dy:1 - dy + H, 1 - dx:1 - dx + W]
                    last = t.matmul(bank[q][:, :], vconv[:, d, :, :].rearrange("p s c -> p (s c)"), src,
                                    start=(d == 0), stop=(d == 7))
                last.then_inc(conv_done, 1)

            def mix_back(b, q):
                i = 2 * b + q
                pe.wait_ge(conv_copied, i + 1)
                wait(pe, mix_added, i - 1)
                if b == 0:
                    pe.wait_ge(moe_added, 2 * NB)
                for j in range(T):
                    last = t.matmul(bank[4 + q][:, C * j:C * (j + 1)], cvs[:, q, j:CH:T], two_ident[:, :], start=True, stop=True)
                last.then_inc(mix_back_done, 1)

            gate_conv1(1)
            pe.wait_ge(f2_scaled, 1)
            moe_x(0, 0)
            pe.wait_ge(conv_vs, 2)
            moe_x(0, 1)
            gate_conv2(1)
            pe.wait_ge(w_lo, 3)
            moe_logits(0, 0)
            moe_logits(0, 1)
            gate_spread(1)
            pe.wait_ge(gate_ready, 2)
            pe.wait_ge(conv2_tanh, 2)
            pe.wait_ge(w_hi, 4)
            pe.wait_ge(ns_YZ_copied, 2 * STEPS)
            moe_c(0, 0)
            moe_c(0, 1)
            for b in range(NB):
                more = b + 1 < NB
                for n in range(8):
                    moe_first(b, n)
                    if n >= 2:
                        moe_second(b, n - 2)
                    elif b:
                        moe_second(b - 1, n + 6)
                    if n == 0 and more:
                        pe.wait_ge(weights_T_copied, 2 * b + 2)
                        moe_x(b + 1, 0)
                        moe_x(b + 1, 1)
                    if n == 1 and more:
                        moe_logits(b + 1, 0)
                        moe_logits(b + 1, 1)
                    if n == 3 and b:
                        back(yTs, moe_y_copied, moe_y_back, b - 1, 1)
                    if n == 7 and not more:
                        pe.wait_ge(weights_T_copied, 2 * NB)
                        mix_x(0, 0, 0)
                        mix_x(0, 0, 1)
                if more:
                    moe_c(b + 1, 0)
                    moe_c(b + 1, 1)
                back(yTs, moe_y_copied, moe_y_back, b, 0)
            moe_second(NB - 1, 6)
            moe_second(NB - 1, 7)
            back(yTs, moe_y_copied, moe_y_back, NB - 1, 1)

            pe.wait_ge(hidden_gelu, 8 * NB)
            pe.wait_ge(hidden_scaled, 8 * NB)
            for b in range(NM - 3):
                if 0 <= b < NB:
                    mix_conv(b, 0)
                if b + 1 < NB:
                    mix_x(b + 1, 0, 0)
                    mix_x(b + 1, 0, 1)
                if 0 <= b < NB:
                    mix_conv(b, 1)
                    mix_back(b, 0)
                    mix_back(b, 1)
                if b + 1 >= LAG:
                    mix_x(b + 1, 1, 0)
                    mix_x(b + 1, 1, 1)
                if b == NB:
                    pe.wait_ge(b2_sel, 4)
                    pe.wait_ge(mix_added, 2 * NB)
                    for k in range(KP):
                        last = t.matmul(bank[4][0:2 * E, 0:C], b2sel[:, k, :, :].rearrange("p s e -> p (s e)"), fo[:, k, :],
                                        start=(k == 0), stop=(k == KP - 1))
                    last.then_inc(rt_tensor, 1)

            def ffn1(b, n):
                q, k = n // KP, n % KP
                wait(pe, layer1_relu, 8 * b + n - 1)
                if n == 0:
                    pe.wait_ge(ffn_T_copied, 2 * b + 2)
                src = xs_ffn[:, bass.ds(b, 1), CH * q:CH * (q + 1)].rearrange("p o n -> p (o n)")
                for part in range(2):
                    last = t.matmul(bank[6 + n % 2][:, :], f1s[:, part, P * k:P * (k + 1)], src,
                                    start=(part == 0), stop=(part == 1))
                last.then_inc(layer1_done, 1)

            def ffn2(b, n):
                k = n % KP
                pe.wait_ge(layer1_relu, 8 * b + n + 1)
                wait(pe, layer2_scaled, 8 * b + n - 1)
                t.matmul(bank[2 + n % 2][:, :], f2[:, k, :], act[:, n % 2, :], start=True, stop=True).then_inc(layer2_done, 1)

            def ffn3(b, n):
                q, k = (n // KP) % 2, n % KP
                if k == 0:
                    wait(pe, ffn_y_copied, 2 * b + q - 1)
                    wait(pe, ffn_added, 2 * b + q - 1)
                pe.wait_ge(layer2_scaled, 8 * b + n + 1)
                for half in range(2):
                    last = t.matmul(bank[4 + q][C * half:C * (half + 1), 0:2 * P], fo[:, k, :],
                                    scaled[:, n % 2, 2 * P * half:2 * P * (half + 1)], start=(k == 0), stop=(k == KP - 1))
                last.then_inc(layer3_done, 1)

            pe.wait_ge(conv_copied, 2 * NB)
            pe.wait_ge(mix_padded, 2 * NB)
            pe.wait_ge(batch_sum, NB - 2)
            for q in range(2):
                t.matmul(bank[0][:, 0:T * C], half_mean[:, :], fsum[:, T * q:T * (q + 1), :].rearrange("p t c -> p (t c)"),
                         start=(q == 0), stop=False)
            for g_ in (NM - 2, NM - 1):
                pe.wait_ge(mix_normed, g_ + 1)
                for q in range(2):
                    s0 = T2 + T * q
                    last = t.matmul(bank[0][:, 0:T * C], half_mean[:, :],
                                    xnc[:, g_ % 2, s0:s0 + T, :].rearrange("p t c -> p (t c)"),
                                    start=False, stop=(g_ == NM - 1 and q == 1))
            last.then_inc(rt_tensor, 1)
            mix_x(NM - 2, 1, 0)
            mix_x(NM - 2, 1, 1)
            pe.wait_ge(rt_vector, R_FEAT)
            for j in range(T):
                last = t.transpose(bank[1][0:C, P * j:P * (j + 1)], feat[:, j, :], ident[:, :])
            last.then_inc(rt_tensor, 1)
            mix_x(NM - 1, 1, 0)
            mix_x(NM - 1, 1, 1)
            ffn1(0, 0)
            pe.wait_ge(rt_vector, R_FEATT)
            for j in range(T):
                last = t.matmul(bank[0][:, E * j:E * (j + 1)], featT[:, P * j:P * (j + 1)], wr[:, :], start=True, stop=True)
            last.then_inc(rt_logits, 1)
            ffn1(0, 1)
            pe.wait_ge(ffn_T_copied, 2 * NB)
            pe.wait_ge(f2_scaled, 1)
            ffn2(0, 0)
            pe.wait_ge(rt_vector, R_WL)
            for j in range(T):
                last = t.transpose(bank[1][0:2 * E, P * j:P * (j + 1)], whl[:, j, :, :].rearrange("p s e -> p (s e)").bitcast(F32), ident[:, :])
            last.then_inc(rt_tensor, 1)
            ffn2(0, 1)
            pe.wait_ge(rt_scalar, 2)
            for k in range(KP):
                if k == 2:
                    pe.wait_ge(rt_vector, R_U16)
                    for j in range(T):
                        last = t.matmul(bank[5][:, C * j:C * (j + 1)], wT[:, P * j:P * (j + 1)].bitcast(F32), u16[:, :], start=True, stop=True)
                    last.then_inc(rt_tensor, 1)
                    pe.wait_ge(rt_copied_vector, 1)
                if k == 3:
                    pe.wait_ge(rt_copied_scalar, 1)
                t.matmul(bank[k % 2][:, :], sel[0:2 * E, k, :], wT[:, :], start=True, stop=True).then_inc(rt_spread, 1)

            for n in range(2, 8):
                ffn1(0, n)
                if n >= 3:
                    ffn2(0, n - 1)
                if n - 2 == KP:
                    pe.wait_ge(rt_vector, R_CTAB)
                ffn3(0, n - 2)
            back(yTs, ffn_y_copied, ffn_y_back, 0, 0)
            with t.Fori(1, NB) as b:
                for n in range(8):
                    ffn1(b, n)
                    ffn2(b, n - 1)
                    ffn3(b, n - 2)
                    if n == 3:
                        back(yTs, ffn_y_copied, ffn_y_back, b + -1, 1)
                back(yTs, ffn_y_copied, ffn_y_back, b, 0)
            ffn2(NB, -1)
            ffn3(NB, -2)
            ffn3(NB, -1)
            back(yTs, ffn_y_copied, ffn_y_back, NB - 1, 1)


_INS = ['x', 'L0_conv_w1', 'L0_conv_b1', 'L0_conv_w2', 'L0_conv_b2', 'L0_ffn_router_w', 'L0_ffn_w1', 'L0_ffn_b1',
        'L0_ffn_w2', 'L0_ffn_b2', 'L1_conv_Wd', 'L1_conv_Wc', 'L1_conv_bc', 'L1_ffn_Wr', 'L1_ffn_br', 'L1_ffn_W1',
        'L1_ffn_b1', 'L1_ffn_g1', 'L1_ffn_be1', 'L1_ffn_m1', 'L1_ffn_v1', 'L1_ffn_W2', 'L1_ffn_b2', 'L1_ffn_g2',
        'L1_ffn_be2', 'L1_ffn_m2', 'L1_ffn_v2', 'L1_ffn_Wo', 'L1_ffn_bo']
_OUTS = [((32, 16, 16, 64), 'float32')]


def kernel(**inputs):
    import numpy as _np
    import concourse.bacc as _bacc
    from concourse import mybir as _mybir
    from concourse.bass_utils import run_bass_kernel_spmd as _run

    nc = _bacc.Bacc("TRN2", target_bir_lowering=False, num_devices=1)
    arrays, args = {}, {}
    for name in _INS:
        arr = _np.ascontiguousarray(inputs[name])
        arrays[f"in_{name}_dram"] = arr
        args[name] = nc.dram_tensor(f"in_{name}_dram", arr.shape, _mybir.dt.from_np(arr.dtype), kind="ExternalInput").ap()
    outs = []
    for i, (shape, dtype) in enumerate(_OUTS):
        dt = _mybir.dt.from_np(_np.dtype(dtype))
        outs.append(nc.dram_tensor(f"out_{i}_dram", shape, dt, kind="ExternalOutput").ap())
    metaformer_kernel(nc, args, outs[0])
    r = _run(nc, [arrays], core_ids=[0])
    got = tuple(r.results[0][f"out_{i}_dram"] for i in range(len(_OUTS)))
    return got[0]
```
